# Optimizing a Trainium2 kernel written in Bass

```python
import numpy as np
import jax
import jax.numpy as jnp

def _softmax(x, axis=-1):
    return jax.nn.softmax(x, axis=axis)

def _gelu(x):
    return jax.nn.gelu(x, approximate=True)

def _silu(x):
    return jax.nn.silu(x)

def _sigmoid(x):
    return jax.nn.sigmoid(x)

def _layernorm(x, axis=-1, eps=1e-05):
    m = jnp.mean(x, axis=axis, keepdims=True)
    v = jnp.var(x, axis=axis, keepdims=True)
    return (x - m) / jnp.sqrt(v + eps)

def _scatter_add(tgt, idx, src, axis=0):
    return tgt.at[idx].add(src)

def _segment_sum(src, seg, n):
    return jax.ops.segment_sum(src, seg, n)
kernel_name = 'mk_prb_d1_jaxref_r4_a749c7'

def setup_inputs(seed: int=0):
    np.random.seed(seed)
    _w = jnp.asarray

    def _L0_attn_setup():
        import jax, jax.numpy as jnp
        import numpy as np
        DIM = 256
        NUM_HEADS = 16
        DIM_HEAD = 64
        FEATURE_DIM = 64
        INNER = NUM_HEADS * DIM_HEAD
        EPS = 1e-06

        def _feature_map(t, proj):
            return jax.nn.relu(jnp.einsum('bhnd,df->bhnf', t, proj)) + EPS
        key = jax.random.key(seed)
        ks = jax.random.split(key, 7)
        x = jax.random.normal(ks[0], (4, 2048, DIM), dtype=jnp.float32)
        s = 1.0 / np.sqrt(DIM)
        Wq = jax.random.normal(ks[1], (DIM, INNER), dtype=jnp.float32) * s
        Wk = jax.random.normal(ks[2], (DIM, INNER), dtype=jnp.float32) * s
        Wv = jax.random.normal(ks[3], (DIM, INNER), dtype=jnp.float32) * s
        proj = jax.random.normal(ks[4], (DIM_HEAD, FEATURE_DIM), dtype=jnp.float32) / np.sqrt(FEATURE_DIM)
        Wo = jax.random.normal(ks[5], (INNER, DIM), dtype=jnp.float32) * (1.0 / np.sqrt(INNER))
        bo = jnp.zeros((DIM,), dtype=jnp.float32)
        return {'x': x, 'Wq': Wq, 'Wk': Wk, 'Wv': Wv, 'proj': proj, 'Wo': Wo, 'bo': bo}
    _L0_attn_in = _L0_attn_setup()

    def _L0_ffn_setup():
        import jax, jax.numpy as jnp
        import numpy as np
        DIM = 256
        N_HEADS = 16
        N_KV_HEADS = 4
        HEAD_DIM = DIM // N_HEADS
        N_REP = N_HEADS // N_KV_HEADS
        N_EXPERTS = 4
        TOP_K = 2
        HIDDEN = 3 * DIM
        EPS = 1.1920928955078125e-07

        def _rmsnorm(x, g):
            var = jnp.mean(jnp.square(x), axis=-1, keepdims=True)
            return x * jax.lax.rsqrt(var + EPS) * g

        def _rotate_half(x):
            x1, x2 = jnp.split(x, 2, axis=-1)
            return jnp.concatenate([-x2, x1], axis=-1)

        def _rope_tables(S):
            inv_freq = 1.0 / 10000.0 ** (jnp.arange(0, HEAD_DIM, 2, dtype=jnp.float32) / HEAD_DIM)
            freqs = jnp.arange(S, dtype=jnp.float32)[:, None] * inv_freq[None, :]
            emb = jnp.concatenate([freqs, freqs], axis=-1)
            return (jnp.cos(emb), jnp.sin(emb))

        def _attention(x, wq, wk, wv, wo):
            B, S, D = x.shape
            q = (x @ wq).reshape(B, S, N_HEADS, HEAD_DIM).transpose(0, 2, 1, 3)
            k = (x @ wk).reshape(B, S, N_KV_HEADS, HEAD_DIM).transpose(0, 2, 1, 3)
            v = (x @ wv).reshape(B, S, N_KV_HEADS, HEAD_DIM).transpose(0, 2, 1, 3)
            cos, sin = _rope_tables(S)
            q = q * cos + _rotate_half(q) * sin
            k = k * cos + _rotate_half(k) * sin
            k = jnp.repeat(k, N_REP, axis=1)
            v = jnp.repeat(v, N_REP, axis=1)
            scores = jnp.einsum('bhqd,bhkd->bhqk', q, k) / jnp.sqrt(jnp.float32(HEAD_DIM))
            causal = jnp.tril(jnp.ones((S, S), dtype=bool))
            scores = jnp.where(causal, scores, -jnp.inf)
            attn = jax.nn.softmax(scores, axis=-1)
            out = jnp.einsum('bhqk,bhkd->bhqd', attn, v)
            return out.transpose(0, 2, 1, 3).reshape(B, S, D) @ wo

        def _moe(x, gate, w1, w2, w3):
            B, S, D = x.shape
            xf = x.reshape(-1, D)
            probs = jax.nn.softmax(xf @ gate, axis=-1)
            w, idx = jax.lax.top_k(probs, TOP_K)
            w = w / jnp.sum(w, axis=-1, keepdims=True)
            oh = jax.nn.one_hot(idx, N_EXPERTS, dtype=xf.dtype)
            comb = jnp.einsum('nk,nke->ne', w, oh)
            out = jnp.zeros_like(xf)
            for e in range(N_EXPERTS):
                h = jax.nn.silu(xf @ w1[e]) * (xf @ w3[e])
                out = out + comb[:, e:e + 1] * (h @ w2[e])
            return out.reshape(B, S, D)
        key = jax.random.key(seed)
        ks = jax.random.split(key, 12)
        s = 0.02
        B, S = (2, 512)
        return {'x': jax.random.normal(ks[0], (B, S, DIM), jnp.float32), 'g1': jnp.ones((DIM,), jnp.float32), 'g2': jnp.ones((DIM,), jnp.float32), 'wq': jax.random.normal(ks[1], (DIM, N_HEADS * HEAD_DIM), jnp.float32) * s, 'wk': jax.random.normal(ks[2], (DIM, N_KV_HEADS * HEAD_DIM), jnp.float32) * s, 'wv': jax.random.normal(ks[3], (DIM, N_KV_HEADS * HEAD_DIM), jnp.float32) * s, 'wo': jax.random.normal(ks[4], (N_HEADS * HEAD_DIM, DIM), jnp.float32) * s, 'gate': jax.random.normal(ks[5], (DIM, N_EXPERTS), jnp.float32) * s, 'w1': jax.random.normal(ks[6], (N_EXPERTS, DIM, HIDDEN), jnp.float32) * s, 'w2': jax.random.normal(ks[7], (N_EXPERTS, HIDDEN, DIM), jnp.float32) * s, 'w3': jax.random.normal(ks[8], (N_EXPERTS, DIM, HIDDEN), jnp.float32) * s}
    _L0_ffn_in = _L0_ffn_setup()
    _d = {'L0_attn_x': _L0_attn_in['x'], 'L0_attn_Wq': _L0_attn_in['Wq'], 'L0_attn_Wk': _L0_attn_in['Wk'], 'L0_attn_Wv': _L0_attn_in['Wv'], 'L0_attn_proj': _L0_attn_in['proj'], 'L0_attn_Wo': _L0_attn_in['Wo'], 'L0_attn_bo': _L0_attn_in['bo'], 'L0_ffn_g1': _L0_ffn_in['g1'], 'L0_ffn_g2': _L0_ffn_in['g2'], 'L0_ffn_wq': _L0_ffn_in['wq'], 'L0_ffn_wk': _L0_ffn_in['wk'], 'L0_ffn_wv': _L0_ffn_in['wv'], 'L0_ffn_wo': _L0_ffn_in['wo'], 'L0_ffn_gate': _L0_ffn_in['gate'], 'L0_ffn_w1': _L0_ffn_in['w1'], 'L0_ffn_w2': _L0_ffn_in['w2'], 'L0_ffn_w3': _L0_ffn_in['w3']}
    _x0 = _d['L0_attn_x']
    _d['L0_attn_x'] = jax.random.normal(jax.random.fold_in(jax.random.key(seed), 1), (8, 512, 256), dtype=_x0.dtype)
    del _x0
    return _d

def reference(L0_attn_x, L0_attn_Wq, L0_attn_Wk, L0_attn_Wv, L0_attn_proj, L0_attn_Wo, L0_attn_bo, L0_ffn_g1, L0_ffn_g2, L0_ffn_wq, L0_ffn_wk, L0_ffn_wv, L0_ffn_wo, L0_ffn_gate, L0_ffn_w1, L0_ffn_w2, L0_ffn_w3):

    def _L0_attn_ref(x, Wq, Wk, Wv, proj, Wo, bo):
        import jax, jax.numpy as jnp
        import numpy as np
        DIM = 256
        NUM_HEADS = 16
        DIM_HEAD = 64
        FEATURE_DIM = 64
        INNER = NUM_HEADS * DIM_HEAD
        EPS = 1e-06

        def _feature_map(t, proj):
            return jax.nn.relu(jnp.einsum('bhnd,df->bhnf', t, proj)) + EPS
        b, n, _ = x.shape

        def split_heads(t):
            return t.reshape(b, n, NUM_HEADS, DIM_HEAD).transpose(0, 2, 1, 3)
        q = split_heads(x @ Wq)
        k = split_heads(x @ Wk)
        v = split_heads(x @ Wv)
        qf = _feature_map(q, proj)
        kf = _feature_map(k, proj)
        kv = jnp.einsum('bhnf,bhnd->bhfd', kf, v)
        k_sum = kf.sum(axis=-2)
        num = jnp.einsum('bhnf,bhfd->bhnd', qf, kv)
        den = jnp.einsum('bhnf,bhf->bhn', qf, k_sum) + EPS
        out = num / den[..., None]
        out = out.transpose(0, 2, 1, 3).reshape(b, n, INNER)
        return out @ Wo + bo

    def _L0_ffn_ref(x, g1, g2, wq, wk, wv, wo, gate, w1, w2, w3):
        import jax, jax.numpy as jnp
        import numpy as np
        DIM = 256
        N_HEADS = 16
        N_KV_HEADS = 4
        HEAD_DIM = DIM // N_HEADS
        N_REP = N_HEADS // N_KV_HEADS
        N_EXPERTS = 4
        TOP_K = 2
        HIDDEN = 3 * DIM
        EPS = 1.1920928955078125e-07

        def _rmsnorm(x, g):
            var = jnp.mean(jnp.square(x), axis=-1, keepdims=True)
            return x * jax.lax.rsqrt(var + EPS) * g

        def _rotate_half(x):
            x1, x2 = jnp.split(x, 2, axis=-1)
            return jnp.concatenate([-x2, x1], axis=-1)

        def _rope_tables(S):
            inv_freq = 1.0 / 10000.0 ** (jnp.arange(0, HEAD_DIM, 2, dtype=jnp.float32) / HEAD_DIM)
            freqs = jnp.arange(S, dtype=jnp.float32)[:, None] * inv_freq[None, :]
            emb = jnp.concatenate([freqs, freqs], axis=-1)
            return (jnp.cos(emb), jnp.sin(emb))

        def _attention(x, wq, wk, wv, wo):
            B, S, D = x.shape
            q = (x @ wq).reshape(B, S, N_HEADS, HEAD_DIM).transpose(0, 2, 1, 3)
            k = (x @ wk).reshape(B, S, N_KV_HEADS, HEAD_DIM).transpose(0, 2, 1, 3)
            v = (x @ wv).reshape(B, S, N_KV_HEADS, HEAD_DIM).transpose(0, 2, 1, 3)
            cos, sin = _rope_tables(S)
            q = q * cos + _rotate_half(q) * sin
            k = k * cos + _rotate_half(k) * sin
            k = jnp.repeat(k, N_REP, axis=1)
            v = jnp.repeat(v, N_REP, axis=1)
            scores = jnp.einsum('bhqd,bhkd->bhqk', q, k) / jnp.sqrt(jnp.float32(HEAD_DIM))
            causal = jnp.tril(jnp.ones((S, S), dtype=bool))
            scores = jnp.where(causal, scores, -jnp.inf)
            attn = jax.nn.softmax(scores, axis=-1)
            out = jnp.einsum('bhqk,bhkd->bhqd', attn, v)
            return out.transpose(0, 2, 1, 3).reshape(B, S, D) @ wo

        def _moe(x, gate, w1, w2, w3):
            B, S, D = x.shape
            xf = x.reshape(-1, D)
            probs = jax.nn.softmax(xf @ gate, axis=-1)
            w, idx = jax.lax.top_k(probs, TOP_K)
            w = w / jnp.sum(w, axis=-1, keepdims=True)
            oh = jax.nn.one_hot(idx, N_EXPERTS, dtype=xf.dtype)
            comb = jnp.einsum('nk,nke->ne', w, oh)
            out = jnp.zeros_like(xf)
            for e in range(N_EXPERTS):
                h = jax.nn.silu(xf @ w1[e]) * (xf @ w3[e])
                out = out + comb[:, e:e + 1] * (h @ w2[e])
            return out.reshape(B, S, D)
        x = x + _attention(_rmsnorm(x, g1), wq, wk, wv, wo)
        x = x + _moe(_rmsnorm(x, g2), gate, w1, w2, w3)
        return x
    x = L0_attn_x
    xn = _layernorm(x, axis=-1)
    x = x + _L0_attn_ref(xn, L0_attn_Wq, L0_attn_Wk, L0_attn_Wv, L0_attn_proj, L0_attn_Wo, L0_attn_bo) + _L0_ffn_ref(xn, L0_ffn_g1, L0_ffn_g2, L0_ffn_wq, L0_ffn_wk, L0_ffn_wv, L0_ffn_wo, L0_ffn_gate, L0_ffn_w1, L0_ffn_w2, L0_ffn_w3)
    return x

_drawn_inputs = setup_inputs


def setup_inputs(seed=0):
    import zlib

    import numpy as np

    out = dict(_drawn_inputs(seed))
    spreads = {'L0_attn_bo': (0.0, 0.8), 'L0_ffn_g1': (1.0, 0.6), 'L0_ffn_g2': (1.0, 0.6)}
    factors = {'L0_attn_Wq': 38.296,
     'L0_attn_Wk': 33.312,
     'L0_attn_proj': 41.416,
     'L0_ffn_wq': 8.0,
     'L0_ffn_wk': 8.0,
     'L0_ffn_wv': 8.0,
     'L0_ffn_wo': 8.0,
     'L0_ffn_gate': 6.952,
     'L0_ffn_w1': 5.027,
     'L0_ffn_w2': 4.97,
     'L0_ffn_w3': 4.97,
     'L0_attn_Wv': 8.0,
     'L0_attn_Wo': 8.0}
    for name, (base, spread) in spreads.items():
        noise = np.random.default_rng([zlib.crc32(name.encode()), seed]).standard_normal(out[name].shape)
        drawn = base * np.exp(spread * noise) if base else spread * noise
        out[name] = jnp.asarray(drawn.astype(out[name].dtype))
    for name, factor in factors.items():
        out[name] = (out[name] * factor).astype(out[name].dtype)
    return out
```

```python
from contextlib import ExitStack

import concourse.bass as bass
from concourse import mybir

F32 = mybir.dt.float32
F32R = mybir.dt.float32r
BF16 = mybir.dt.bfloat16
ALU = mybir.AluOpType
ACT = mybir.ActivationFunctionType
AX = mybir.AxisListType.X

P = 128
B, S, D = 8, 512, 256
NJ = S // P
KT = D // P
LN_EPS = 1e-5
RMS_EPS = 1.1920928955078125e-07
LIN_EPS = 1e-6

NH, NKV, HD = 16, 4, 16
NU = NH // 2
NQ = NH // 4
PARTS_Q = ((0, 0), (16, 1), (48, 0))
PARTS_K = ((0, 0), (16, 0), (48, 1))
SHIFT_ROW = 32
P_OFF = (0, 512, 1024, 896)

LH, LD = 16, 64
INNER = LH * LD
NP_ = LH // 2
PW = 2 * LD + 2

NE, HID = 4, 768
NM = HID // P


class Steps:

    def __init__(self, sem, per):
        self.sem, self.per, self.b, self.k = sem, per, 0, 0

    def start(self, b):
        self.b, self.k = b, 0

    def link(self, eng, ins):
        self.k += 1
        assert self.k <= self.per, "more steps than counted"
        ins.then_inc(self.sem, 1)
        eng.wait_ge(self.sem, self.b * self.per + self.k)

    def end(self):
        assert self.k == self.per, (self.k, self.per)


def first(b):
    return isinstance(b, int) and b == 0


def mm3(nc, out, lh, ll, rh, rl, start, stop):
    nc.tensor.matmul(out, lh, rh, start=start, stop=False)
    nc.tensor.matmul(out, lh, rl, start=False, stop=False)
    return nc.tensor.matmul(out, ll, rh, start=False, stop=stop)


def softmax_attention(nc, x, g1, wq, wk, wv, wo, ident_d, mask_d, cos_d, sin_d, qk_d, y2_d):
    x_v = x.rearrange("b (j p) d -> b p j d", p=P)
    y2_v = y2_d.rearrange("b (j p) d -> b p j d", p=P)
    qk_v = qk_d.rearrange("h (T p) t -> p T h t", p=P)

    with ExitStack() as ctx:
        def sb(name, shape, dt=F32):
            return ctx.enter_context(nc.sbuf_tensor(name, shape, dt))

        def sem(name):
            return ctx.enter_context(nc.semaphore(name))

        ident = sb("ident", [P, P])
        identb = sb("identb", [P, P], BF16)
        maskM = sb("maskM", [P, P], BF16)
        maskE = sb("maskE", [P, P], BF16)
        cos = sb("cos", [P, S])
        sin = sb("sin", [P, S])
        g1c = sb("g1c", [P, KT])
        WQ, WK, WV = 2 * D, 4 * 64, NKV * HD
        wA = [sb(f"wA{i}", [P, KT, WQ + WK + WV], F32R) for i in range(2)]
        wO = [sb(f"wO{i}", [P, KT, D], F32R) for i in range(2)]
        zrow = sb("zrow", [2, 1, S])

        x_sb = sb("x_sb", [P, NJ, D])
        st = sb("st", [P, NJ, 6])
        mv = sb("mv", [P, NJ, 2])
        vin = sb("vin", [P, 2, NJ])
        inv = sb("inv", [P, 2, NJ])
        vt = sb("vt", [P, NJ])
        sc = sb("sc", [P, NJ])
        mhalf = sb("mhalf", [P, 2 * NJ])
        xr = sb("xr", [P, NJ, D])
        xrT = [sb(f"xrT{i}", [P, KT, S], F32R) for i in range(2)]
        rc = sb("rc", [P, 3, S])
        rs = sb("rs", [P, 3, S])
        raw = rc[:, 0:KT, :]
        mask = rs[:, 0, 0:P]
        qk = sb("qk", [P, 2, 3, S], F32R)
        qs = [sb(f"qs{i}", [P, NU, S], F32R) for i in range(2)]
        kp = [sb(f"kp{i}", [P, 2, NKV, S], F32R) for i in range(2)]
        v32 = [sb(f"v32{i}", [P, NJ, NKV, 32]) for i in range(2)]
        vnew = sb("vnew", [P, NJ, NKV, HD])
        negm = sb("negm", [P, NJ, P])
        negT = sb("negT", [NH, S], F32R)
        prob = sb("prob", [P, 2, 4, 1280])
        oT = sb("oT", [P, 2, S])
        rsum = sb("rsum", [P, NJ, 4])
        on2 = sb("on2", [P, NJ, D])
        o2T = [sb(f"o2T{i}", [P, KT, S], F32R) for i in range(2)]
        y2 = sb("y2", [P, NJ, D])

        ps = ctx.enter_context(nc.psum_tensor("ps", [P, 8, 512], F32))
        FRONT, MAXB, EXPB, PVB, TAILB = 0, 1, 4, 6, 7

        consts_loaded = sem("consts_loaded")
        weights_loaded = sem("weights_loaded")
        pool_prep = Steps(sem("pool_prep_step"), 1)
        dve_prep = Steps(sem("dve_prep_step"), 3)
        weights_ready = sem("weights_ready")
        zeros_ready = sem("zeros_ready")
        mask_turned = sem("mask_turned")
        x_loaded = sem("x_loaded")
        stats_ready = sem("stats_ready")
        roots_ready = sem("roots_ready")
        xr_ready = sem("xr_ready")
        ln_steps = Steps(sem("ln_step"), 6)
        front_psum = sem("front_psum")
        front_evac = sem("front_evac")
        front_hi = sem("front_hi")
        parts_ready = sem("parts_ready")
        parts_steps = Steps(sem("parts_step"), 6)
        parts_stored = sem("parts_stored")
        stacked = [sem(f"stacked{i}") for i in range(2)]
        shift_psum = sem("shift_psum")
        shift_evac = sem("shift_evac")
        v_ready = sem("v_ready")
        max_psum = sem("max_psum")
        max_evac = sem("max_evac")
        shift_loaded = sem("shift_loaded")
        exp_psum = sem("exp_psum")
        exp_done = sem("exp_done")
        pv_done = sem("pv_done")
        pv_evac = sem("pv_evac")
        ot_psum = sem("ot_psum")
        ot_recip = sem("ot_recip")
        ot_evac = sem("ot_evac")
        tail_psum = sem("tail_psum")
        tail_hi = sem("tail_hi")
        tail_evac = sem("tail_evac")
        y2_stored = sem("y2_stored")

        NF, NM_, NX, NT = 9, 6 * NU, 5 * NU, 4
        STACKS = 1 + 2 * 3 + 2 * 3
        MUNITS = [(3, (0,)), (3, (1,)), (2, (0,)), (2, (1,)), (1, (0, 1)), (0, (0, 1))]
        XUNITS = [[(0, 0)], [(0, 1), (0, 3)], [(1, 0)], [(1, 1), (1, 3)], [(0, 2), (1, 2)]]

        def order(f, m, e, t):
            E = [("exp", u, k) for u in range(NU) for k in range(5)] if e is not None else []
            out = []

            def exps(n):
                for _ in range(min(n, len(E))):
                    out.append(E.pop(0))
                    _, u, k = out[-1]
                    if k == 2 and u and u % 2 == 0:
                        out.append(("pv", u // 2 - 1, 0))
                    if k == 1 and u % 2 == 1 and u > 1:
                        out.append(("ot", u // 2 - 1, 0))

            if f is not None:
                out.append(("stats", 0, 0))
            for i in range(6 * NU):
                if m is not None:
                    out.append(("max", i // 6, i % 6))
                if t is not None and i % 2 and i // 2 < NT:
                    out.append(("tail", i // 2, 0))
                if f is not None and i == 7:
                    out.append(("rows", 0, 0))
                if i >= 6 and m is not None:
                    exps(1)
                if f is not None and i >= 10 and i % 3 == 1 and (i - 10) // 3 < NF:
                    out.append(("front", (i - 10) // 3, 0))
            if m is not None:
                out.append(("shift", 0, 0))
            exps(len(E))
            if e is not None:
                out += [("pv", NQ - 1, 0), ("ot", NQ - 1, 0)]
            return out

        def sync_part(sp, f, m, e, t, par):
            if f is not None:
                for T in range(3):
                    sp.wait_ge(parts_ready, 3 * f + 1 + T)
                    sp.dma_start(qk_v[:, T, :, :], qk[:, :, T, :].bitcast(F32)).then_inc(parts_stored, 16)
            if t is not None:
                sp.wait_ge(tail_evac, NT * t + NT)
                sp.dma_start(y2_v[t], y2[:]).then_inc(y2_stored, 16)
            if f is not None:
                load_stacks(sp, f, e, par, 0)
            if m is not None:
                sp.wait_ge(shift_evac, m + 1)
                for a in range(2):
                    r = 64 * a + SHIFT_ROW
                    sp.dma_start(qs[par][r:r + 1, :, :].bitcast(F32),
                                 negT[NU * a:NU * a + NU, :].bitcast(F32)).then_inc(shift_loaded, 16)
            if f is not None:
                load_stacks(sp, f, e, par, 1)

        def load_stacks(sp, f, e, par, half):
            q, k = qs[1 - par][:].bitcast(F32), kp[1 - par][:].bitcast(F32)
            us, gs = slice(4 * half, 4 * half + 4), slice(2 * half, 2 * half + 2)
            if e is not None:
                sp.wait_ge(exp_psum, NX * e + NX // 2 * (half + 1))
            elif first(f):
                sp.wait_ge(zeros_ready, 1)
            if half == 0:
                sp.wait_ge(parts_stored, 16 * 3 * (f + 1))
            sp.dma_start(q[SHIFT_ROW:SHIFT_ROW + 65:64, us, :],
                         zrow[:].broadcast_to([2, NU // 2, S])).then_inc(stacked[half], 16)
            for a in range(2):
                for r, h in PARTS_Q:
                    src = qk_d[h, 0:NH * HD, :].rearrange("(u a c) t -> a c u t", a=2, c=HD)
                    sp.dma_start(q[64 * a + r:64 * a + r + HD, us, :], src[a][:, us, :]).then_inc(stacked[half], 16)
                for r, h in PARTS_K:
                    src = qk_d[h, NH * HD:(NH + NKV) * HD, :].rearrange("(g c) t -> c g t", c=HD)
                    sp.dma_start(k[64 * a + r:64 * a + r + HD, a, gs, :], src[:, gs, :]).then_inc(stacked[half], 16)

        def pe_part(pe, f, m, e, t, par):
            for what, n, k in order(f, m, e, t):
                if what == "front":
                    bank = ps[:, FRONT, :]
                    if n:
                        pe.wait_ge(front_evac, NF * f + n)
                    elif m is not None:
                        if not first(m):
                            pe.wait_ge(shift_evac, m)
                        pe.wait_ge(front_evac, NF * f)
                    if n < KT:
                        pe.wait_ge(xr_ready, NJ * f + NJ)
                        for j in range(NJ):
                            last = nc.tensor.transpose(bank[:, j * P:(j + 1) * P], xr[:, j, n * P:(n + 1) * P], ident[:])
                    elif n < 8:
                        T, rot = (n - 2) // 2, n % 2
                        c = T * P + rot * D if T < 2 else WQ + rot * P
                        for kt in range(KT):
                            w = [wA[i][:, kt, c:c + P] for i in range(2)]
                            last = mm3(nc, bank, w[0], w[1], xrT[0][:, kt, :], xrT[1][:, kt, :], kt == 0, kt == KT - 1)
                    else:
                        for j in range(NJ):
                            for kt in range(KT):
                                l = [xrT[i][:, kt, j * P:(j + 1) * P] for i in range(2)]
                                w = [wA[i][:, kt, WQ + WK:] for i in range(2)]
                                last = mm3(nc, bank[:, j * WV:(j + 1) * WV], l[0], l[1], w[0], w[1],
                                           kt == 0, kt == KT - 1)
                    last.then_inc(front_psum, 1)
                elif what == "max":
                    j, heads = MUNITS[k]
                    i = 6 * n + k
                    if i % (6 * NU // 2) == 0:
                        pe.wait_ge(stacked[i // (6 * NU // 2)], 16 * STACKS * (m + 1))
                    if not (first(m) and i < 3):
                        pe.wait_ge(max_evac, NM_ * m + i - 2)
                    for x, a in enumerate(heads):
                        w = (j + 1) * P
                        o = ps[:, MAXB + i % 3, x * w:(x + 1) * w]
                        nc.tensor.matmul(o, qs[par][:, n, j * P:(j + 1) * P], kp[par][:, a, n // 2, 0:w],
                                         start=True, stop=False)
                        last = nc.tensor.matmul(o[:, w - P:w], identb[:], maskM[:], start=False, stop=True)
                    last.then_inc(max_psum, 1)
                elif what == "shift":
                    pe.wait_ge(front_evac, NF * ((f if f is not None else B - 1) + 1))
                    if not first(m):
                        pe.wait_ge(shift_evac, m)
                    pe.wait_ge(max_evac, NM_ * (m + 1))
                    for j in range(NJ):
                        last = nc.tensor.transpose(ps[:, FRONT, j * P:(j + 1) * P], negm[:, j, :], ident[:])
                    last.then_inc(shift_psum, 1)
                elif what == "exp":
                    i = 5 * n + k
                    if i == 0:
                        pe.wait_ge(shift_loaded, 32 * (e + 1))
                    if not (first(e) and i < 2):
                        pe.wait_ge(exp_done, NX * e + i - 1)
                    at = 0
                    for a, kt in XUNITS[k]:
                        w = S - kt * P
                        o = ps[:, EXPB + i % 2, at:at + w]
                        nc.tensor.matmul(o, kp[1 - par][:, a, n // 2, kt * P:(kt + 1) * P], qs[1 - par][:, n, kt * P:],
                                         start=True, stop=False)
                        last = nc.tensor.matmul(o[:, 0:P], identb[:], maskE[:], start=False, stop=True)
                        at += w
                    last.then_inc(exp_psum, 1)
                elif what == "pv":
                    pe.wait_ge(exp_done, NX * e + 10 * (n + 1))
                    if n == 0:
                        pe.wait_ge(v_ready, e + 1)
                    if not (first(e) and n == 0):
                        pe.wait_ge(pv_evac, NQ * e + n)
                    for i in range(NJ):
                        w = S - i * P
                        for s in range(4):
                            last = nc.tensor.matmul(ps[32 * s:32 * s + 32, PVB, i * P:], v32[1 - par][:, i, n, :],
                                                    prob[:, n % 2, s, P_OFF[i]:P_OFF[i] + w],
                                                    start=(i == 0), stop=(i == NJ - 1),
                                                    tile_position=(0, 32 * s))
                    last.then_inc(pv_done, 1)
                elif what == "ot":
                    pe.wait_ge(pv_evac, NQ * e + n + 1)
                    if n == 0 and t is not None:
                        pe.wait_ge(tail_evac, NT * (t + 1))
                    if n:
                        pe.wait_ge(ot_evac, NQ * e + n)
                    for j in range(NJ):
                        last = nc.tensor.transpose(ps[:, TAILB, j * P:(j + 1) * P], oT[:, n % 2, j * P:(j + 1) * P], ident[:])
                    last.then_inc(ot_psum, 1)
                elif what == "tail":
                    if n == 0:
                        pe.wait_ge(ot_evac, NQ * (t + 1))
                    else:
                        pe.wait_ge(tail_evac, NT * t + n)
                    if n < KT:
                        for j in range(NJ):
                            last = nc.tensor.transpose(ps[:, TAILB, j * P:(j + 1) * P], on2[:, j, n * P:(n + 1) * P], ident[:])
                    else:
                        for i in range(2):
                            j = 2 * (n - KT) + i
                            for kt in range(KT):
                                l = [o2T[h][:, kt, j * P:(j + 1) * P] for h in range(2)]
                                last = mm3(nc, ps[:, TAILB, i * D:(i + 1) * D], l[0], l[1],
                                           wO[0][:, kt, :], wO[1][:, kt, :], kt == 0, kt == KT - 1)
                    last.then_inc(tail_psum, 1)

        def act_part(act, f, m, e, t, par):
            for what, n, k in order(f, m, e, t):
                if what == "front" and n < KT:
                    act.wait_ge(front_psum, NF * f + n + 1)
                    nc.scalar.copy(xrT[0][:, n, :], ps[:, FRONT, :]).then_inc(front_hi, 1)
                elif what == "exp":
                    i = 5 * n + k
                    act.wait_ge(exp_psum, NX * e + i + 1)
                    q = n // 2
                    if n % 2 == 0 and k == 0 and not (first(e) and q < 2):
                        act.wait_ge(pv_done, NQ * e + q - 1)
                    s = 2 * (n % 2)
                    if k < 4:
                        h, kt = XUNITS[k][0]
                        o, w = prob[:, q % 2, s + h, P_OFF[kt]:P_OFF[kt] + 512], ps[:, EXPB + i % 2, :]
                    else:
                        o = prob[:, q % 2, s:s + 2, P_OFF[2]:P_OFF[2] + 256]
                        w = ps[:, EXPB + i % 2, :].rearrange("p (a q) -> p a q", a=2)
                    nc.scalar.activation(o, w, ACT.Exp, scale=HD ** -0.5).then_inc(exp_done, 1)
                elif what == "pv":
                    act.wait_ge(pv_done, NQ * e + n + 1)
                    if not (first(e) and n < 2):
                        act.wait_ge(ot_psum, NQ * e + n - 1)
                    nc.scalar.copy(oT[:, n % 2, :], ps[:, PVB, :]).then_inc(pv_evac, 1)
                elif what == "tail" and n < KT:
                    act.wait_ge(tail_psum, NT * t + n + 1)
                    nc.scalar.copy(o2T[0][:, n, :], ps[:, TAILB, :]).then_inc(tail_hi, 1)

        def dve_part(dve, f, m, e, t, par):
            if m is not None:
                if not (isinstance(m, int) and m < 2):
                    dve.wait_ge(pv_done, NQ * (m - 1))
                dve.wait_ge(front_evac, NF * (m + 1))
                nc.vector.tensor_copy(v32[par][:, :, :, 0:HD], vnew[:]).then_inc(v_ready, 1)
            for what, n, k in order(f, m, e, t):
                bank = ps[:, FRONT, :]
                if what == "stats":
                    ln_steps.start(f)
                    dve.wait_ge(x_loaded, 16 * (f + 1))
                    for j in range(NJ - 1):
                        nc.vector.bn_stats(st[:, j, :], x_sb[:, j, :])
                    ln_steps.link(dve, nc.vector.bn_stats(st[:, NJ - 1, :], x_sb[:, NJ - 1, :]))
                    nc.vector.memset(sc[:, 0:1], 0.0)
                    for j in range(NJ - 1):
                        nc.vector.bn_aggr(mv[:, j, :], st[:, j, :])
                    ln_steps.link(dve, nc.vector.bn_aggr(mv[:, NJ - 1, :], st[:, NJ - 1, :]))
                    var = mv[:, :, 1:2].rearrange("p j o -> p (j o)")
                    ln_steps.link(dve, nc.vector.tensor_scalar(vin[:, 0, :], var, LN_EPS, None, ALU.add))
                    ln_steps.link(dve, nc.vector.reciprocal(vt[:], vin[:, 0, :]))
                    ln_steps.link(dve, nc.vector.tensor_tensor(vt[:], vt[:], var, ALU.mult))
                    nc.vector.tensor_scalar(vin[:, 1, :], vt[:], RMS_EPS, None, ALU.add).then_inc(stats_ready, 1)
                elif what == "rows":
                    dve.wait_ge(roots_ready, f + 1)
                    ln_steps.link(dve, nc.vector.tensor_tensor(sc[:], inv[:, 0, :], inv[:, 1, :], ALU.mult))
                    ln_steps.end()
                    for j in range(NJ):
                        nc.vector.tensor_scalar(xr[:, j, :], x_sb[:, j, :], mv[:, j, 0:1], sc[:, j:j + 1],
                                                ALU.subtract, ALU.mult).then_inc(xr_ready, 1)
                elif what == "front":
                    if n < KT:
                        dve.wait_ge(front_hi, KT * f + n + 1)
                        nc.vector.tensor_tensor(xrT[1][:, n, :], bank, xrT[0][:, n, :].bitcast(F32),
                                                ALU.subtract).then_inc(front_evac, 1)
                    elif n < 8:
                        T, rot = (n - 2) // 2, n % 2
                        dve.wait_ge(front_psum, NF * f + n + 1)
                        if rot == 0 and T == 0 and not first(f):
                            dve.wait_ge(parts_ready, 3 * f)
                        nc.vector.tensor_tensor((rs if rot else rc)[:, T, :], bank, (sin if rot else cos)[:],
                                                ALU.mult).then_inc(front_evac, 1)
                    else:
                        dve.wait_ge(front_psum, NF * f + n + 1)
                        nc.vector.tensor_copy(vnew[:], bank[:, 0:NJ * WV].rearrange("p (j g c) -> p j g c", j=NJ, c=HD)
                                              ).then_inc(front_evac, 1)
                elif what == "max":
                    j, heads = MUNITS[k]
                    i = 6 * n + k
                    dve.wait_ge(max_psum, NM_ * m + i + 1)
                    w = (j + 1) * P
                    src = ps[:, MAXB + i % 3, 0:w * len(heads)].rearrange("p (a k) -> p a k", k=w)
                    if len(heads) == 2:
                        dst = negm[:, j, n:n + NU + 1:NU]
                    else:
                        dst = negm[:, j, heads[0] * NU + n:heads[0] * NU + n + 1]
                    nc.vector.tensor_reduce(dst, src, AX, ALU.max, negate=True).then_inc(max_evac, 1)
                elif what == "shift":
                    dve.wait_ge(shift_psum, m + 1)
                    if not first(m):
                        dve.wait_ge(shift_loaded, 32 * m)
                    nc.vector.tensor_copy(negT[:], ps[0:NH, FRONT, :]).then_inc(shift_evac, 1)
                elif what == "ot":
                    dve.wait_ge(ot_psum, NQ * e + n + 1)
                    o = ps[:, TAILB, :].rearrange("p (j s c) -> p j s c", j=NJ, s=4)
                    nc.vector.reciprocal(rsum[:], o[:, :, :, HD]).then_inc(ot_recip, 1)
                    dve.wait_ge(ot_recip, NQ * e + n + 1)
                    nc.vector.tensor_tensor(on2[:, :, n * 64:(n + 1) * 64].rearrange("p j (s c) -> p j s c", s=4),
                                            o[:, :, :, 0:HD], rsum[:].unsqueeze(3).broadcast_to([P, NJ, 4, HD]),
                                            ALU.mult).then_inc(ot_evac, 1)
                elif what == "tail":
                    if n < KT:
                        dve.wait_ge(tail_hi, KT * t + n + 1)
                        nc.vector.tensor_tensor(o2T[1][:, n, :], ps[:, TAILB, :], o2T[0][:, n, :].bitcast(F32),
                                                ALU.subtract).then_inc(tail_evac, 1)
                    else:
                        dve.wait_ge(tail_psum, NT * t + n + 1)
                        if n == KT and not first(t):
                            dve.wait_ge(y2_stored, 16 * t)
                        j = 2 * (n - KT)
                        nc.vector.tensor_copy(y2[:, j:j + 2, :],
                                              ps[:, TAILB, :].rearrange("p (j d) -> p j d", j=2)).then_inc(tail_evac, 1)

        def pool_part(pool, f, m, e, t, par):
            if f is None:
                return
            if not first(f):
                pool.wait_ge(xr_ready, NJ * f)
            pool.dma_start(x_sb[:], x_v[f]).then_inc(x_loaded, 16)
            pool.wait_ge(stats_ready, f + 1)
            nc.gpsimd.tensor_tensor(inv[:].rearrange("p a j -> p (a j)"), vin[:].rearrange("p a j -> p (a j)"),
                                    mhalf[:], ALU.pow).then_inc(roots_ready, 1)
            parts_steps.start(f)
            for T in range(3):
                pool.wait_ge(front_evac, NF * f + 2 * T + 4)
                if T == 0 and not first(f):
                    pool.wait_ge(parts_stored, 16 * 3 * f)
                parts_steps.link(pool, nc.gpsimd.tensor_tensor(qk[:, 0, T, :], rc[:, T, :], rs[:, T, :], ALU.add))
                parts_steps.link(pool, nc.gpsimd.tensor_tensor(rc[:, T, :], rc[:, T, :], rs[:, T, :], ALU.add))
                nc.gpsimd.tensor_tensor(qk[:, 1, T, :], rc[:, T, :], qk[:, 0, T, :].bitcast(F32),
                                        ALU.subtract).then_inc(parts_ready, 1)
            parts_steps.end()

        def program(eng, part):
            part(eng, 0, None, None, None, 1)
            part(eng, 1, 0, None, None, 0)
            part(eng, 2, 1, 0, None, 1)
            part(eng, 3, 2, 1, 0, 0)
            with eng.Fori(1, B // 2 - 1) as i:
                m = 2 * i + 1
                part(eng, m + 1, m, m - 1, m - 2, 1)
                part(eng, m + 2, m + 1, m, m - 1, 0)
            part(eng, None, B - 1, B - 2, B - 3, 1)
            part(eng, None, None, B - 1, B - 2, 0)
            part(eng, None, None, None, B - 1, 1)

        block = ctx.enter_context(nc.Block())

        @block.sync
        def _(sp):
            sp.dma_start(ident[:], ident_d).then_inc(consts_loaded, 16)
            sp.dma_start(mask, mask_d).then_inc(consts_loaded, 16)
            sp.dma_start(cos[:], cos_d).then_inc(consts_loaded, 16)
            sp.dma_start(sin[:], sin_d).then_inc(consts_loaded, 16)
            sp.dma_start(g1c[:], g1.rearrange("(k p) -> p k", p=P), allow_slow_non_contiguous=True).then_inc(consts_loaded, 16)
            sp.dma_start(raw[:, :, 0:D], wq.rearrange("(k p) n -> p k n", p=P)).then_inc(weights_loaded, 16)
            sp.dma_start(raw[:, :, D:D + WV], wk.rearrange("(k p) n -> p k n", p=P)).then_inc(weights_loaded, 16)
            sp.dma_start(raw[:, :, D + WV:D + 2 * WV], wv.rearrange("(k p) n -> p k n", p=P)).then_inc(weights_loaded, 16)
            sp.dma_start(on2[:, 0:KT, :], wo.rearrange("(k p) n -> p k n", p=P)).then_inc(weights_loaded, 16)
            program(sp, sync_part)
            sp.wait_ge(y2_stored, 16 * B)

        @block.tensor
        def _(pe):
            pe.wait_ge(consts_loaded, 16 * 5)
            nc.tensor.transpose(ps[:, TAILB, 0:P], mask, ident[:]).then_inc(mask_turned, 1)
            pe.wait_ge(weights_ready, 2)
            pe.wait_ge(zeros_ready, 1)
            program(pe, pe_part)

        @block.scalar
        def _(act):
            program(act, act_part)

        @block.gpsimd
        def _(pool):
            nc.gpsimd.memset(mhalf[:], -0.5)
            for i in range(2):
                nc.gpsimd.memset(v32[i][:], 0.0)
                nc.gpsimd.memset(qs[i][:].bitcast(F32), 0.0)
                nc.gpsimd.memset(kp[i][:].bitcast(F32), 0.0)
            nc.gpsimd.memset(negm[:], 0.0)
            pool_prep.link(pool, nc.gpsimd.memset(zrow[:], 0.0))
            for i in range(2):
                last = nc.gpsimd.memset(v32[i][:, :, :, HD:HD + 1], 1.0)
            last.then_inc(zeros_ready, 1)
            program(pool, pool_part)

        @block.vector
        def _(dve):
            dve.wait_ge(consts_loaded, 16 * 5)
            nc.vector.tensor_copy(identb[:], ident[:])
            nc.vector.tensor_copy(maskM[:], mask)
            dve.wait_ge(mask_turned, 1)
            nc.vector.tensor_copy(maskE[:], ps[:, TAILB, 0:P]).then_inc(weights_ready, 1)
            dve.wait_ge(weights_loaded, 16 * 4)
            for kt in range(KT):
                ins = nc.vector.tensor_scalar(raw[:, kt, 0:D + 2 * WV], raw[:, kt, 0:D + 2 * WV],
                                              g1c[:, kt:kt + 1], None, ALU.mult)
            dve_prep.link(dve, ins)
            hi, lo = wA
            q = raw[:, :, 0:D]

            def halves(ap):
                return ap.rearrange("p k (h c) -> p k h c", c=HD)

            for kt in range(KT):
                qv = raw[:, kt, 0:D].rearrange("p (h c) -> p h c", c=HD)
                kv = raw[:, kt, D:D + WV].rearrange("p (h c) -> p h c", c=HD)
                nc.vector.tensor_copy(hi[:, kt, 0:D], raw[:, kt, 0:D])
                nc.vector.tensor_copy(hi[:, kt, WQ + WK:], raw[:, kt, D + WV:D + 2 * WV])
                for src, at, n in ((qv, D, D), (kv, WQ + P, WV), (kv, WQ + P + WV, WV)):
                    dst = hi[:, kt, at:at + n].rearrange("p (h c) -> p h c", c=HD)
                    nc.vector.tensor_scalar(dst[:, :, 0:8], src[:, :, 8:16], -1.0, None, ALU.mult)
                    nc.vector.tensor_copy(dst[:, :, 8:16], src[:, :, 0:8])
                for at in (WQ, WQ + WV):
                    nc.vector.tensor_copy(hi[:, kt, at:at + WV], raw[:, kt, D:D + WV])
            dve_prep.link(dve, nc.vector.tensor_copy(wO[0][:], on2[:, 0:KT, :]))
            for kt in range(KT):
                h32 = hi[:, kt, :].bitcast(F32)
                qv = raw[:, kt, 0:D].rearrange("p (h c) -> p h c", c=HD)
                kv = raw[:, kt, D:D + WV].rearrange("p (h c) -> p h c", c=HD)
                for src, at, n in ((raw[:, kt, 0:D], 0, D), (raw[:, kt, D:D + WV], WQ, WV),
                                   (raw[:, kt, D:D + WV], WQ + WV, WV), (raw[:, kt, D + WV:D + 2 * WV], WQ + WK, WV)):
                    nc.vector.tensor_tensor(lo[:, kt, at:at + n], src, h32[:, at:at + n], ALU.subtract)
                for src, at, n in ((qv, D, D), (kv, WQ + P, WV), (kv, WQ + P + WV, WV)):
                    dst = lo[:, kt, at:at + n].rearrange("p (h c) -> p h c", c=HD)
                    h = h32[:, at:at + n].rearrange("p (h c) -> p h c", c=HD)
                    nc.vector.scalar_tensor_tensor(out=dst[:, :, 0:8], in0=src[:, :, 8:16], scalar=-1.0, in1=h[:, :, 0:8],
                                                   op0=ALU.mult, op1=ALU.subtract)
                    nc.vector.tensor_tensor(dst[:, :, 8:16], src[:, :, 0:8], h[:, :, 8:16], ALU.subtract)
            dve_prep.link(dve, nc.vector.tensor_tensor(wO[1][:], on2[:, 0:KT, :], wO[0][:].bitcast(F32), ALU.subtract))
            dve.wait_ge(zeros_ready, 1)
            for i in range(2):
                for a in range(2):
                    r = 64 * a + SHIFT_ROW
                    last = nc.vector.memset(kp[i][r:r + 1, a, :, :].bitcast(F32), 1.0)
            last.then_inc(weights_ready, 1)
            program(dve, dve_part)


def linear_attention(nc, x, wq, wk, wv, proj, wo, bo, ident_d, y2_d, z_d, r1_d):
    def tiles(ap):
        return ap.rearrange("b (j p) d -> b p j d", p=P)

    x_v, y2_v, z_v, r1_v = map(tiles, (x, y2_d, z_d, r1_d))

    with ExitStack() as ctx:
        def sb(name, shape, dt=F32):
            return ctx.enter_context(nc.sbuf_tensor(name, shape, dt))

        def sem(name):
            return ctx.enter_context(nc.semaphore(name))

        ident = sb("ident2", [P, P])
        pblk = sb("pblk", [P, P])
        bob = sb("bob", [P, D])
        mhalf = sb("mhalf2", [P, NJ])
        WQ, WK, WV = ([sb(f"{n}{i}", [P, KT, INNER], F32R) for i in range(2)] for n in ("WQ", "WK", "WV"))
        WO = [sb(f"WO{i}", [P, NP_, D], F32R) for i in range(2)]

        x_sb = sb("x2_sb", [P, NJ, D])
        xn = sb("xn", [P, NJ, D])
        st = sb("st2", [P, NJ, 6])
        pad = sb("pad2", [P, 1])
        mv = sb("mv2", [P, NJ, 2])
        vin = sb("vin2", [P, NJ])
        inv = sb("inv2", [P, NJ])
        xb = sb("xb", [P, NJ, D])
        r1 = sb("r1", [P, NJ, D])
        xnT = [sb(f"xnT{i}", [P, KT, S], F32R) for i in range(2)]
        kf = sb("kf", [P, NJ, INNER])
        va = sb("va", [P, NJ, NP_, PW])
        kvb = sb("kvb", [P, NP_, PW])
        qf = sb("qf", [P, NP_, S])
        den = sb("den", [P, NP_, 2])
        rden = sb("rden", [P, NP_, 2])
        on = sb("on", [P, 2, INNER])
        oT = [sb(f"loT{i}", [P, 2, NP_, P], F32R) for i in range(2)]

        ps = ctx.enter_context(nc.psum_tensor("ps2", [P, 8, 512], F32))
        RING, OTB, KVB, YB = 0, 2, 4, 7

        consts_loaded = sem("consts2_loaded")
        w_loaded = sem("w2_loaded")
        pblk_zero = sem("pblk_zero")
        turned = sem("w_turned")
        turned_copied = sem("w_turned_copied")
        folded = sem("w_folded")
        hi_made = sem("w_hi_made")
        lo_made = sem("w_lo_made")
        pool_lo_made = sem("w_pool_lo_made")
        zeros_ready = sem("zeros2_ready")
        x_loaded = sem("x2_loaded")
        y2_loaded = sem("y2_loaded")
        stats_ready = sem("stats2_ready")
        roots_ready = sem("roots2_ready")
        ln_steps = Steps(sem("ln2_step"), 2)
        xn_ready = sem("xn_ready")
        r1_ready = sem("r1_ready")
        r1_stored = sem("r1_stored")
        xb_ready = sem("xb_ready")
        ring_psum = sem("ring_psum")
        t_hi = sem("t_hi")
        ring_evac_dve = sem("ring_evac_dve")
        ring_evac_act = sem("ring_evac_act")
        kv_psum = sem("kv_psum")
        kv_evac = sem("kv_evac")
        num_psum = sem("num_psum")
        num_steps = Steps(sem("num_step"), 2 * NJ)
        num_evac = sem("num_evac")
        ot_psum = sem("ot2_psum")
        ot_hi = sem("ot2_hi")
        ot_evac = sem("ot2_evac")
        y_psum = sem("y_psum")
        y_evac = sem("y_evac")
        z_stored = sem("z_stored")

        NR = 16 + NP_ + KT
        NRD, NRA = 8 + NP_ + KT, 8
        NUM = [(KVB + i // 3, (i % 3) * PW) for i in range(NP_)]

        def ring_free(eng, base, u):
            u -= 2
            if u < 0:
                eng.wait_ge(ring_evac_dve, NRD * base + KT + u + 1)
            elif u < 16 and u % 4 >= 2:
                eng.wait_ge(ring_evac_act, NRA * base + 2 * (u // 4) + u % 4 - 1)
            elif u < 16:
                eng.wait_ge(ring_evac_dve, NRD * base + KT + 2 * (u // 4) + u % 4 + 1)
            else:
                eng.wait_ge(ring_evac_dve, NRD * base + KT + 8 + (u - 16) + 1)

        def pe_turn(pe, n):
            for kt in range(KT):
                if not first(n):
                    ring_free(pe, n - 1, NR - KT + kt)
                if kt == 0:
                    pe.wait_ge(xn_ready, NJ * n + NJ)
                for j in range(NJ):
                    last = nc.tensor.transpose(ps[:, RING + kt, j * P:(j + 1) * P], xn[:, j, kt * P:(kt + 1) * P], ident[:])
                last.then_inc(ring_psum, 1)

        def pe_part(pe, b, n):
            pe.wait_ge(ring_evac_dve, NRD * b + KT)
            for u in range(16):
                j, w, half = u // 4, (WK, WK, WV, WV)[u % 4], u % 2
                ring_free(pe, b, u)
                for kt in range(KT):
                    l = [xnT[i][:, kt, j * P:(j + 1) * P] for i in range(2)]
                    r = [w[i][:, kt, half * 512:(half + 1) * 512] for i in range(2)]
                    last = mm3(nc, ps[:, RING + u % 2, :], *l, *r, kt == 0, kt == KT - 1)
                last.then_inc(ring_psum, 1)
            pe.wait_ge(ring_evac_dve, NRD * b + KT + 8)
            pe.wait_ge(ring_evac_act, NRA * (b + 1))
            if not first(b):
                pe.wait_ge(num_evac, NJ * b)
            for p in range(NP_):
                bank, at = NUM[p]
                for j in range(NJ):
                    last = nc.tensor.matmul(ps[:, bank, at:at + PW], kf[:, j, p * P:(p + 1) * P], va[:, j, p, :],
                                            start=(j == 0), stop=(j == NJ - 1))
            last.then_inc(kv_psum, 1)
            for p in range(NP_):
                u = 16 + p
                ring_free(pe, b, u)
                for kt in range(KT):
                    l = [WQ[i][:, kt, p * P:(p + 1) * P] for i in range(2)]
                    last = mm3(nc, ps[:, RING + u % 2, :], *l, xnT[0][:, kt, :], xnT[1][:, kt, :], kt == 0, kt == KT - 1)
                last.then_inc(ring_psum, 1)
            pe.wait_ge(kv_evac, b + 1)
            pe.wait_ge(ring_evac_dve, NRD * b + KT + 8 + NP_)

            def num(j):
                if j:
                    pe.wait_ge(num_evac, NJ * b + j)
                for p in range(NP_):
                    bank, at = NUM[p]
                    last = nc.tensor.matmul(ps[:, bank, at:at + PW], qf[:, p, j * P:(j + 1) * P], kvb[:, p, :],
                                            start=True, stop=True)
                last.then_inc(num_psum, 1)

            def turn(j):
                pe.wait_ge(num_evac, NJ * b + j + 1)
                for h in range(2):
                    if not (first(b) and j == 0):
                        pe.wait_ge(ot_evac, 2 * NJ * b + 2 * j + h - 1)
                    for p in range(4):
                        pp = 4 * h + p
                        last = nc.tensor.transpose(ps[:, OTB + h, p * P:(p + 1) * P], on[:, j % 2, pp * P:(pp + 1) * P], ident[:])
                    last.then_inc(ot_psum, 1)

            def out(j):
                pe.wait_ge(ot_evac, 2 * NJ * b + 2 * j + 2)
                if j % 2 == 0 and not (first(b) and j == 0):
                    pe.wait_ge(y_evac, 2 * b + j // 2)
                for p in range(NP_):
                    l = [oT[i][:, j % 2, p, :] for i in range(2)]
                    last = mm3(nc, ps[:, YB, (j % 2) * D:(j % 2 + 1) * D], *l, WO[0][:, p, :], WO[1][:, p, :],
                               p == 0, p == NP_ - 1)
                last.then_inc(y_psum, 1)

            num(0)
            num(1)
            turn(0)
            out(0)
            num(2)
            turn(1)
            out(1)
            num(3)
            turn(2)
            out(2)
            turn(3)
            if n is not None:
                pe_turn(pe, n)
            out(3)

        def act_turn(act, n):
            for kt in range(KT):
                act.wait_ge(ring_psum, NR * n + kt + 1)
                nc.scalar.copy(xnT[0][:, kt, :], ps[:, RING + kt, :]).then_inc(t_hi, 1)

        def act_part(act, b, n):
            if not first(b):
                act.wait_ge(kv_psum, b)
            for j in range(NJ):
                for h in range(2):
                    act.wait_ge(ring_psum, NR * b + KT + 4 * j + 2 + h + 1)
                    nc.scalar.copy(va[:, j, 4 * h:4 * h + 4, 0:P],
                                   ps[:, RING + h, :].rearrange("p (q c) -> p q c", c=P)).then_inc(ring_evac_act, 1)
            act.wait_ge(kv_psum, b + 1)
            if not first(b):
                act.wait_ge(num_psum, NJ * b)
            for bank in range(3):
                m = min(3, NP_ - 3 * bank)
                for a in range(2):
                    r = slice(64 * a, 64 * a + 64)
                    src = ps[r, KVB + bank, 0:m * PW].rearrange("p (q c) -> p q c", c=PW)
                    dst = kvb[r, 3 * bank:3 * bank + m, :]
                    nc.scalar.copy(dst[:, :, LD * a:LD * a + LD], src[:, :, LD * a:LD * a + LD])
                    last = nc.scalar.copy(dst[:, :, P + a:P + a + 1], src[:, :, P + a:P + a + 1])
            last.then_inc(kv_evac, 1)
            for j in range(NJ):
                for h in range(2):
                    act.wait_ge(ot_psum, 2 * NJ * b + 2 * j + h + 1)
                    if j < 2:
                        if not first(b):
                            act.wait_ge(y_psum, NJ * b - 2 + j + 1)
                    else:
                        act.wait_ge(y_psum, NJ * b + j - 1)
                    nc.scalar.copy(oT[0][:, j % 2, 4 * h:4 * h + 4, :],
                                   ps[:, OTB + h, :].rearrange("p (q c) -> p q c", c=P)).then_inc(ot_hi, 1)
            if n is not None:
                act_turn(act, n)

        def dve_norm(dve, n):
            ln_steps.start(n)
            dve.wait_ge(x_loaded, 16 * (n + 1))
            for j in range(NJ):
                last = nc.vector.bn_stats(st[:, j, :], x_sb[:, j, :])
            ln_steps.link(dve, last)
            nc.vector.memset(pad[:], 0.0)
            for j in range(NJ):
                last = nc.vector.bn_aggr(mv[:, j, :], st[:, j, :])
            ln_steps.link(dve, last)
            nc.vector.tensor_scalar(vin[:], mv[:, :, 1:2].rearrange("p j o -> p (j o)"), LN_EPS, None,
                                    ALU.add).then_inc(stats_ready, 1)
            ln_steps.end()
            dve.wait_ge(roots_ready, n + 1)
            if not first(n):
                dve.wait_ge(ring_psum, NR * (n - 1) + KT)
            for j in range(NJ):
                nc.vector.tensor_scalar(xn[:, j, :], x_sb[:, j, :], mv[:, j, 0:1], inv[:, j:j + 1],
                                        ALU.subtract, ALU.mult).then_inc(xn_ready, 1)
            dve.wait_ge(xn_ready, NJ * (n + 1))
            dve.wait_ge(y2_loaded, 16 * (n + 1))
            nc.vector.tensor_tensor(r1[:], r1[:], xn[:], ALU.add).then_inc(r1_ready, 1)

        def dve_turn(dve, n):
            for kt in range(KT):
                dve.wait_ge(t_hi, KT * n + kt + 1)
                nc.vector.tensor_tensor(xnT[1][:, kt, :], ps[:, RING + kt, :], xnT[0][:, kt, :].bitcast(F32),
                                        ALU.subtract).then_inc(ring_evac_dve, 1)

        def dve_part(dve, b, n):
            if not first(b):
                dve.wait_ge(kv_psum, b)
            for j in range(NJ):
                for h in range(2):
                    dve.wait_ge(ring_psum, NR * b + KT + 4 * j + h + 1)
                    nc.vector.tensor_scalar(kf[:, j, h * 512:(h + 1) * 512], ps[:, RING + h, :], 0.0, LIN_EPS,
                                            ALU.max, ALU.add).then_inc(ring_evac_dve, 1)
            if not first(b):
                dve.wait_ge(num_psum, NJ * b)
            for p in range(NP_):
                dve.wait_ge(ring_psum, NR * b + KT + 16 + p + 1)
                nc.vector.tensor_scalar(qf[:, p, :], ps[:, RING + p % 2, :], 0.0, LIN_EPS,
                                        ALU.max, ALU.add).then_inc(ring_evac_dve, 1)
            if n is not None:
                dve_norm(dve, n)
            num_steps.start(b)

            def num(j):
                dve.wait_ge(num_psum, NJ * b + j + 1)
                if j > 1:
                    dve.wait_ge(ot_psum, 2 * NJ * b + 2 * (j - 1))
                elif not first(b):
                    dve.wait_ge(ot_psum, 2 * NJ * b - 2 * (1 - j))
                for bank in range(3):
                    m = min(3, NP_ - 3 * bank)
                    src = ps[:, KVB + bank, 0:m * PW].rearrange("p (q c) -> p q c", c=PW)
                    last = nc.vector.tensor_scalar(den[:, 3 * bank:3 * bank + m, :], src[:, :, P:PW], LIN_EPS, None, ALU.add)
                num_steps.link(dve, last)
                num_steps.link(dve, nc.vector.reciprocal(rden[:], den[:]))
                for bank in range(3):
                    m = min(3, NP_ - 3 * bank)
                    src = ps[:, KVB + bank, 0:m * PW].rearrange("p (q c) -> p q c", c=PW)
                    for a in range(2):
                        dst = on[:, j % 2, :].rearrange("p (q a c) -> p q a c", a=2, c=LD)[:, 3 * bank:3 * bank + m, a, :]
                        r = rden[:, 3 * bank:3 * bank + m, a:a + 1].broadcast_to([P, m, LD])
                        last = nc.vector.tensor_tensor(dst, src[:, :, LD * a:LD * a + LD], r, ALU.mult)
                last.then_inc(num_evac, 1)

            def low(j):
                for h in range(2):
                    dve.wait_ge(ot_hi, 2 * NJ * b + 2 * j + h + 1)
                    nc.vector.tensor_tensor(oT[1][:, j % 2, 4 * h:4 * h + 4, :],
                                            ps[:, OTB + h, :].rearrange("p (q c) -> p q c", c=P),
                                            oT[0][:, j % 2, 4 * h:4 * h + 4, :].bitcast(F32),
                                            ALU.subtract).then_inc(ot_evac, 1)

            def z(i):
                dve.wait_ge(y_psum, NJ * b + 2 * i + 2)
                dve.wait_ge(xb_ready, b + 1)
                nc.vector.tensor_tensor(xb[:, 2 * i:2 * i + 2, :], ps[:, YB, :].rearrange("p (j d) -> p j d", j=2),
                                        xb[:, 2 * i:2 * i + 2, :], ALU.add).then_inc(y_evac, 1)

            num(0)
            num(1)
            low(0)
            num(2)
            low(1)
            z(0)
            num(3)
            low(2)
            low(3)
            if n is not None:
                dve_turn(dve, n)
            z(1)
            num_steps.end()

        def pool_norm(pool, n):
            pool.wait_ge(stats_ready, n + 1)
            nc.gpsimd.tensor_tensor(inv[:], vin[:], mhalf[:], ALU.pow).then_inc(roots_ready, 1)

        def pool_bias(pool, b):
            if not first(b):
                pool.wait_ge(z_stored, 16 * b)
            pool.wait_ge(x_loaded, 16 * (b + 1))
            nc.gpsimd.tensor_tensor(xb[:], x_sb[:], bob[:].unsqueeze(1).broadcast_to([P, NJ, D]),
                                    ALU.add).then_inc(xb_ready, 1)

        def pool_load(pool, n):
            if not first(n):
                pool.wait_ge(xb_ready, n)
                pool.wait_ge(xn_ready, NJ * n)
            pool.dma_start(x_sb[:], x_v[n]).then_inc(x_loaded, 16)

        def sync_load(sp, n):
            if not first(n):
                sp.wait_ge(r1_stored, 16 * n)
            sp.dma_start(r1[:], y2_v[n]).then_inc(y2_loaded, 16)

        def sync_part(sp, b, n):
            sp.wait_ge(r1_ready, b + 1)
            sp.dma_start(r1_v[b], r1[:]).then_inc(r1_stored, 16)
            if n is not None:
                sync_load(sp, n)
            sp.wait_ge(y_evac, 2 * (b + 1))
            sp.dma_start(z_v[b], xb[:]).then_inc(z_stored, 16)

        def program(eng, part):
            part(eng, 0, 1)
            with eng.Fori(1, B - 1) as b:
                part(eng, b, b + 1)
            part(eng, B - 1, None)

        block = ctx.enter_context(nc.Block())

        @block.sync
        def _(sp):
            sp.dma_start(ident[:], ident_d).then_inc(consts_loaded, 16)
            sp.dma_start(bob[:], bo.rearrange("(a d) -> a d", a=1).broadcast_to([P, D])).then_inc(consts_loaded, 16)
            sp.wait_ge(pblk_zero, 1)
            for a in range(2):
                sp.dma_start(pblk[64 * a:64 * a + 64, 64 * a:64 * a + 64], proj).then_inc(consts_loaded, 16)
            for i, w in enumerate((wq, wk)):
                sp.dma_start(kf[:, 2 * i:2 * i + 2, :], w.rearrange("(k p) n -> p k n", p=P)).then_inc(w_loaded, 16)
            sp.dma_start(va[:, 0:2, :, :].rearrange("p j q c -> p (j q c)")[:, 0:KT * INNER].rearrange("p (k n) -> p k n", k=KT),
                         wv.rearrange("(k p) n -> p k n", p=P)).then_inc(w_loaded, 16)
            sp.dma_start(on[:].rearrange("p a n -> p (a n)").rearrange("p (k n) -> p k n", k=NP_),
                         wo.rearrange("(k p) n -> p k n", p=P)).then_inc(w_loaded, 16)
            sync_load(sp, 0)
            program(sp, sync_part)
            sp.wait_ge(z_stored, 16 * B)
            sp.wait_ge(r1_stored, 16 * B)

        @block.tensor
        def _(pe):
            pe.wait_ge(consts_loaded, 16 * 4)
            for i in range(2):
                pe.wait_ge(w_loaded, 16 * 4)
                for p in range(NP_):
                    for kt in range(KT):
                        c = p * D + kt * P
                        last = nc.tensor.transpose(ps[:, c // 512, c % 512:c % 512 + P],
                                                   kf[:, 2 * i + kt, p * P:(p + 1) * P], ident[:])
                last.then_inc(turned, 1)
                pe.wait_ge(turned_copied, i + 1)
                if i:
                    pe.wait_ge(lo_made, 1)
                for kt in range(KT):
                    for p in range(NP_):
                        c = p * P
                        last = nc.tensor.matmul(ps[:, 4 + 2 * kt + c // 512, c % 512:c % 512 + P],
                                                qf[:, p // 2, (p % 2) * D + kt * P:(p % 2) * D + (kt + 1) * P], pblk[:],
                                                start=True, stop=True)
                last.then_inc(folded, 1)
            pe.wait_ge(lo_made, 2)
            pe.wait_ge(zeros_ready, 1)
            pe.wait_ge(pool_lo_made, 2)
            pe_turn(pe, 0)
            program(pe, pe_part)

        @block.scalar
        def _(act):
            act.wait_ge(w_loaded, 16 * 4)
            nc.scalar.copy(WV[0][:], va[:, 0:2, :, :].rearrange("p j q c -> p (j q c)")[:, 0:KT * INNER]
                           .rearrange("p (k n) -> p k n", k=KT)).then_inc(hi_made, 1)
            nc.scalar.copy(WO[0][:], on[:].rearrange("p a n -> p (a n)").rearrange("p (k n) -> p k n", k=NP_)
                           ).then_inc(hi_made, 1)
            for i, w in enumerate((WQ, WK)):
                act.wait_ge(turned, i + 1)
                if i:
                    act.wait_ge(folded, 1)
                nc.scalar.copy(qf[:, 0:4, :], ps[:, 0:4, :]).then_inc(turned_copied, 1)
                act.wait_ge(folded, i + 1)
                for kt in range(KT):
                    nc.scalar.copy(w[0][:, kt, :].rearrange("p (b n) -> p b n", b=2),
                                   ps[:, 4 + 2 * kt:6 + 2 * kt, :]).then_inc(hi_made, 1)
            act.wait_ge(lo_made, 2)
            act.wait_ge(pool_lo_made, 2)
            act.wait_ge(zeros_ready, 1)
            act_turn(act, 0)
            program(act, act_part)

        @block.gpsimd
        def _(pool):
            nc.gpsimd.memset(pblk[:], 0.0).then_inc(pblk_zero, 1)
            nc.gpsimd.memset(mhalf[:], -0.5)
            nc.gpsimd.memset(kvb[:], 0.0)
            pool.wait_ge(hi_made, 2)
            nc.gpsimd.tensor_tensor(WO[1][:], on[:].rearrange("p a n -> p (a n)").rearrange("p (k n) -> p k n", k=NP_),
                                    WO[0][:].bitcast(F32), ALU.subtract).then_inc(pool_lo_made, 1)
            nc.gpsimd.tensor_tensor(WV[1][:], va[:, 0:2, :, :].rearrange("p j q c -> p (j q c)")[:, 0:KT * INNER]
                                    .rearrange("p (k n) -> p k n", k=KT), WV[0][:].bitcast(F32),
                                    ALU.subtract).then_inc(pool_lo_made, 1)
            pool.wait_ge(pool_lo_made, 2)
            nc.gpsimd.memset(va[:, :, :, P:PW].rearrange("p j q c -> p (j q) c"), 1.0).then_inc(zeros_ready, 1)
            pool_load(pool, 0)
            pool_norm(pool, 0)
            pool.wait_ge(consts_loaded, 16 * 4)
            pool_bias(pool, 0)

            def pool_part(pool, b, n):
                if n is not None:
                    pool_load(pool, n)
                    pool_norm(pool, n)
                    pool_bias(pool, n)

            program(pool, pool_part)

        @block.vector
        def _(dve):
            for i, w in enumerate((WQ, WK)):
                for kt in range(KT):
                    dve.wait_ge(hi_made, 2 + 2 * i + kt + 1)
                    last = nc.vector.tensor_tensor(w[1][:, kt, :].rearrange("p (b n) -> p b n", b=2),
                                                   ps[:, 4 + 2 * kt:6 + 2 * kt, :],
                                                   w[0][:, kt, :].rearrange("p (b n) -> p b n", b=2).bitcast(F32),
                                                   ALU.subtract)
                last.then_inc(lo_made, 1)
            dve_norm(dve, 0)
            dve_turn(dve, 0)
            program(dve, dve_part)


def experts(nc, g2, gate, w1, w2, w3, ident_d, z_d, r1_d, out):
    def tiles(ap):
        return ap.rearrange("b (j p) d -> b p j d", p=P)

    z_v, r1_v, out_v = map(tiles, (z_d, r1_d, out))

    with ExitStack() as ctx:
        def sb(name, shape, dt=F32):
            return ctx.enter_context(nc.sbuf_tensor(name, shape, dt))

        def sem(name):
            return ctx.enter_context(nc.semaphore(name))

        ident = sb("ident3", [P, P])
        g2c = sb("g2c", [P, KT])
        mhalf = sb("mhalf3", [P, NJ])
        graw = sb("graw", [P, KT, NE])
        W1, W3 = ([sb(f"{n}{i}", [P, NE, KT, HID], F32R) for i in range(2)] for n in ("W1_", "W3_"))
        W2 = [sb(f"W2_{i}", [P, NE, NM, D], F32R) for i in range(2)]
        G = [sb(f"G{i}", [P, KT, NE], F32R) for i in range(2)]

        WC = KT * HID
        work = sb("work", [P, 5 * 1024])
        r1 = work[:, 0:1024].rearrange("p (j d) -> p j d", j=NJ)
        xf = work[:, 1024:2048].rearrange("p (j d) -> p j d", j=NJ)
        acc = work[:, 2048:3072].rearrange("p (j d) -> p j d", j=NJ)
        sl = work[:, 3072:4096].rearrange("p (i n) -> p i n", i=2)
        h32 = work[:, 4096:5120].rearrange("p (i n) -> p i n", i=2)
        st = sb("st3", [P, NJ, 6])
        pad = sb("pad3", [P, 1])
        mv = sb("mv3", [P, NJ, 2])
        ms = sb("ms", [P, NJ])
        inv = sb("inv3", [P, NJ])
        xfT = [sb(f"xfT{i}", [P, KT, S], F32R) for i in range(2)]
        NHR = 3
        hT = [sb(f"hT{i}", [P, NHR, S], F32R) for i in range(2)]
        lg = sb("lg", [P, NJ, NE])
        lmax = sb("lmax", [P, NJ])
        le = sb("le", [P, NJ, NE])
        lsum = sb("lsum", [P, NJ])
        pr = sb("pr", [P, NJ, NE])
        over = sb("over", [P, NJ, NE, NE])
        rank = sb("rank", [P, NJ, NE])
        comb = sb("comb", [P, NJ, NE])

        ps = ctx.enter_context(nc.psum_tensor("ps3", [P, 8, 512], F32))
        YB = 4

        consts_loaded = sem("consts3_loaded")
        w_loaded = [sem(f"w3_loaded{i}") for i in range(3)]
        hi_steps = Steps(sem("w3_hi"), 3 * NE)
        w_split = sem("w3_split")
        gate_steps0 = Steps(sem("gate_prep"), 2)
        zeros_ready = sem("zeros3_ready")
        r1_loaded = sem("r1_loaded")
        z_loaded = sem("z_loaded")
        n_steps = Steps(sem("norm3_step"), 3)
        ms_ready = sem("ms_ready")
        roots_ready = sem("roots3_ready")
        xf_ready = sem("xf_ready")
        acc_ready = sem("acc_ready")
        xt_psum = sem("xt_psum")
        xt_hi = sem("xt_hi")
        xt_lo = sem("xt_lo")
        gate_psum = sem("gate_psum")
        gate_steps = Steps(sem("gate_step"), 10)
        lmax_ready = sem("lmax_ready")
        le_ready = sem("le_ready")
        ab_psum = sem("ab_psum")
        silu_done = sem("silu_done")
        h_ready = sem("h_ready")
        h_hi = sem("h_hi")
        h_lo = sem("h_lo")
        y_psum = sem("y3_psum")
        y_used = sem("y3_used")
        y_evac = sem("y3_evac")
        out_stored = sem("out_stored")

        NH_ = NE * NM


        def pe_turn(pe, n):
            if not first(n):
                pe.wait_ge(h_ready, NH_ * n)
            pe.wait_ge(xf_ready, NJ * (n + 1))
            for kt in range(KT):
                for j in range(NJ):
                    last = nc.tensor.transpose(ps[:, kt, j * P:(j + 1) * P], xf[:, j, kt * P:(kt + 1) * P], ident[:])
                last.then_inc(xt_psum, 1)

        def pe_gate(pe, n):
            pe.wait_ge(xt_lo, KT * (n + 1))
            for j in range(NJ):
                for kt in range(KT):
                    l = [xfT[i][:, kt, j * P:(j + 1) * P] for i in range(2)]
                    last = mm3(nc, ps[:, 2, j * NE:(j + 1) * NE], *l, G[0][:, kt, :], G[1][:, kt, :],
                               kt == 0, kt == KT - 1)
            last.then_inc(gate_psum, 1)

        def pe_part(pe, b, n):
            def hidden(i):
                e, m = divmod(i, NM)
                if i == 0:
                    pe.wait_ge(gate_steps.sem, gate_steps.per * b + 1)
                elif i == 1:
                    pass
                else:
                    pe.wait_ge(h_ready, NH_ * b + i - 1)
                for w, bank in ((W1, 2 * (i % 2)), (W3, 2 * (i % 2) + 1)):
                    for kt in range(KT):
                        l = [w[h][:, e, kt, m * P:(m + 1) * P] for h in range(2)]
                        last = mm3(nc, ps[:, bank, :], *l, xfT[0][:, kt, :], xfT[1][:, kt, :], kt == 0, kt == KT - 1)
                last.then_inc(ab_psum, 1)

            def down(i):
                e, m = divmod(i, NM)
                pe.wait_ge(h_lo, NH_ * b + i + 1)
                if m == 0 and not (first(b) and e == 0):
                    pe.wait_ge(y_evac, NE * b + e)
                for j in range(NJ):
                    l = [hT[h][:, i % NHR, j * P:(j + 1) * P] for h in range(2)]
                    last = mm3(nc, ps[:, YB + j, 0:D], *l, W2[0][:, e, m, :], W2[1][:, e, m, :], m == 0, m == NM - 1)
                last.then_inc(y_used, 1)

            for i in range(NH_):
                hidden(i)
                if i >= 2:
                    down(i - 2)
            if n is not None:
                pe_turn(pe, n)
            down(NH_ - 2)
            down(NH_ - 1)
            if n is not None:
                pe_gate(pe, n)

        def act_turn(act, n):
            for kt in range(KT):
                act.wait_ge(xt_psum, KT * n + kt + 1)
                nc.scalar.copy(xfT[0][:, kt, :], ps[:, kt, :]).then_inc(xt_hi, 1)

        def act_gate(act, n):
            act.wait_ge(lmax_ready, n + 1)
            nc.scalar.activation(le[:], lg[:], ACT.Exp).then_inc(le_ready, 1)

        def act_part(act, b, n):
            for i in range(NH_ + 1):
                if i < NH_:
                    act.wait_ge(ab_psum, NH_ * b + i + 1)
                    if i >= 2:
                        act.wait_ge(h_ready, NH_ * b + i - 1)
                    elif not first(b):
                        act.wait_ge(h_ready, NH_ * b)
                    nc.scalar.activation(sl[:, i % 2, :], ps[:, 2 * (i % 2), :], ACT.Silu).then_inc(silu_done, 1)
                if i:
                    k = i - 1
                    act.wait_ge(h_ready, NH_ * b + k + 1)
                    if k >= NHR:
                        act.wait_ge(y_used, NH_ * b + k - NHR + 1)
                    elif not first(b):
                        act.wait_ge(y_used, NH_ * b - NHR + k + 1)
                    nc.scalar.copy(hT[0][:, k % NHR, :], h32[:, k % 2, :]).then_inc(h_hi, 1)
            if n is not None:
                act_turn(act, n)
                act_gate(act, n)

        def dve_norm(dve, n):
            n_steps.start(n)
            dve.wait_ge(r1_loaded, 16 * (n + 1))
            for j in range(NJ):
                last = nc.vector.bn_stats(st[:, j, :], r1[:, j, :])
            n_steps.link(dve, last)
            nc.vector.memset(pad[:], 0.0)
            for j in range(NJ):
                last = nc.vector.bn_aggr(mv[:, j, :], st[:, j, :])
            n_steps.link(dve, last)
            mean, var = (mv[:, :, i:i + 1].rearrange("p j o -> p (j o)") for i in range(2))
            n_steps.link(dve, nc.vector.tensor_tensor(ms[:], mean, mean, ALU.mult))
            nc.vector.scalar_tensor_tensor(out=ms[:], in0=ms[:], scalar=RMS_EPS, in1=var,
                                           op0=ALU.add, op1=ALU.add).then_inc(ms_ready, 1)
            n_steps.end()
            dve.wait_ge(roots_ready, n + 1)
            if not first(n):
                dve.wait_ge(xt_psum, KT * n)
            for j in range(NJ):
                nc.vector.tensor_scalar(xf[:, j, :], r1[:, j, :], inv[:, j:j + 1], None, ALU.mult).then_inc(xf_ready, 1)

        def dve_turn(dve, n):
            for kt in range(KT):
                dve.wait_ge(xt_hi, KT * n + kt + 1)
                nc.vector.tensor_tensor(xfT[1][:, kt, :], ps[:, kt, :], xfT[0][:, kt, :].bitcast(F32),
                                        ALU.subtract).then_inc(xt_lo, 1)

        def dve_gate(dve, n):
            def wide(ap):
                return ap.unsqueeze(2).broadcast_to([P, NJ, NE])

            s = gate_steps
            s.start(n)
            dve.wait_ge(gate_psum, n + 1)
            s.link(dve, nc.vector.tensor_copy(lg[:], ps[:, 2, 0:NJ * NE].rearrange("p (j e) -> p j e", e=NE)))
            s.link(dve, nc.vector.tensor_reduce(lmax[:], lg[:], AX, ALU.max))
            nc.vector.tensor_tensor(lg[:], lg[:], wide(lmax[:]), ALU.subtract).then_inc(lmax_ready, 1)
            dve.wait_ge(le_ready, n + 1)
            s.link(dve, nc.vector.reduce_sum(lsum[:], le[:], AX))
            s.link(dve, nc.vector.reciprocal(lsum[:], lsum[:]))
            s.link(dve, nc.vector.tensor_tensor(pr[:], le[:], wide(lsum[:]), ALU.mult))
            for r in range(NE):
                if r:
                    last = nc.vector.tensor_tensor(over[:, :, 0:r, r], pr[:, :, r:r + 1].broadcast_to([P, NJ, r]),
                                                   pr[:, :, 0:r], ALU.is_gt)
                if r < NE - 1:
                    k = NE - 1 - r
                    last = nc.vector.tensor_tensor(over[:, :, r + 1:NE, r], pr[:, :, r:r + 1].broadcast_to([P, NJ, k]),
                                                   pr[:, :, r + 1:NE], ALU.is_ge)
            s.link(dve, last)
            s.link(dve, nc.vector.reduce_sum(rank[:], over[:], AX))
            s.link(dve, nc.vector.scalar_tensor_tensor(out=comb[:], in0=rank[:], scalar=1.5, in1=pr[:],
                                                       op0=ALU.is_lt, op1=ALU.mult))
            s.link(dve, nc.vector.reduce_sum(lsum[:], comb[:], AX))
            s.link(dve, nc.vector.reciprocal(lsum[:], lsum[:]))
            nc.vector.tensor_tensor(comb[:], comb[:], wide(lsum[:]), ALU.mult).then_inc(comb_ready, 1)
            s.end()

        comb_ready = sem("comb_ready")

        def dve_part(dve, b, n):
            def weigh(e):
                if e == 0:
                    dve.wait_ge(comb_ready, b + 1)
                    dve.wait_ge(acc_ready, b + 1)
                else:
                    dve.wait_ge(y_evac, NE * b + e)
                dve.wait_ge(y_used, NH_ * b + NM * (e + 1))
                for j in range(NJ):
                    last = nc.vector.scalar_tensor_tensor(out=acc[:, j, :], in0=ps[:, YB + j, 0:D], scalar=comb[:, j, e:e + 1],
                                                          in1=acc[:, j, :], op0=ALU.mult, op1=ALU.add)
                last.then_inc(y_evac, 1)

            for i in range(NH_):
                dve.wait_ge(silu_done, NH_ * b + i + 1)
                if i >= 2:
                    dve.wait_ge(h_lo, NH_ * b + i - 1)
                elif not first(b):
                    dve.wait_ge(h_lo, NH_ * b - 1 + i)
                nc.vector.tensor_tensor(h32[:, i % 2, :], sl[:, i % 2, :], ps[:, 2 * (i % 2) + 1, :],
                                        ALU.mult).then_inc(h_ready, 1)
                if i % NM == 1 and i > NM:
                    weigh(i // NM - 1)
                if i == 12 and n is not None:
                    dve_norm(dve, n)
            if n is not None:
                dve_turn(dve, n)
            weigh(NE - 1)
            if n is not None:
                dve_gate(dve, n)

        def pool_norm(pool, n):
            pool.wait_ge(ms_ready, n + 1)
            nc.gpsimd.tensor_tensor(inv[:], ms[:], mhalf[:], ALU.pow).then_inc(roots_ready, 1)

        def pool_part(pool, b, n):
            if n is not None:
                pool_load(pool, n)
            for i in range(NH_):
                pool.wait_ge(h_hi, NH_ * b + i + 1)
                nc.gpsimd.tensor_tensor(hT[1][:, i % NHR, :], h32[:, i % 2, :], hT[0][:, i % NHR, :].bitcast(F32),
                                        ALU.subtract).then_inc(h_lo, 1)
                if i == 11 and n is not None:
                    pool_norm(pool, n)
            if n is not None:
                pool_acc(pool, n)

        def pool_acc(pool, n):
            pool.wait_ge(z_loaded, 16 * (n + 1))
            pool.wait_ge(r1_loaded, 16 * (n + 1))
            nc.gpsimd.tensor_tensor(acc, acc, r1, ALU.add).then_inc(acc_ready, 1)

        def pool_load(pool, n):
            if not first(n):
                pool.wait_ge(acc_ready, n)
                pool.wait_ge(xf_ready, NJ * n)
            pool.dma_start(r1, r1_v[n]).then_inc(r1_loaded, 16)

        def sync_part(sp, b, n):
            sp.wait_ge(y_evac, NE * (b + 1))
            sp.dma_start(out_v[b], acc).then_inc(out_stored, 16)
            sp.wait_ge(out_stored, 16 * (b + 1))
            if n is not None:
                sp.dma_start(acc, z_v[n]).then_inc(z_loaded, 16)

        def program(eng, part):
            part(eng, 0, 1)
            with eng.Fori(1, B - 1) as b:
                part(eng, b, b + 1)
            part(eng, B - 1, None)

        CH = [(e, k) for e in range(NE) for k in range(3)]

        def chunk(i):
            return work[:, (i % 3) * WC:(i % 3 + 1) * WC]

        block = ctx.enter_context(nc.Block())

        @block.sync
        def _(sp):
            sp.dma_start(ident[:], ident_d).then_inc(consts_loaded, 16)
            sp.dma_start(g2c[:], g2.rearrange("(k p) -> p k", p=P), allow_slow_non_contiguous=True).then_inc(consts_loaded, 16)
            sp.dma_start(graw[:], gate.rearrange("(k p) e -> p k e", p=P)).then_inc(consts_loaded, 16)
            for i, (e, k) in enumerate(CH):
                if i >= 3:
                    sp.wait_ge(w_split, i - 2)
                w = (w1, w3, w2)[k]
                sp.dma_start(chunk(i).rearrange("p (k n) -> p k n", n=D if k == 2 else HID),
                             w[e].rearrange("(k p) n -> p k n", p=P)).then_inc(w_loaded[i % 3], 16)
            sp.wait_ge(w_split, len(CH))
            sp.dma_start(acc, z_v[0]).then_inc(z_loaded, 16)
            program(sp, sync_part)

        @block.tensor
        def _(pe):
            pe.wait_ge(consts_loaded, 16 * 3)
            pe.wait_ge(w_split, len(CH))
            pe_turn(pe, 0)
            pe_gate(pe, 0)
            program(pe, pe_part)

        @block.scalar
        def _(act):
            act_turn(act, 0)
            act_gate(act, 0)
            program(act, act_part)

        @block.gpsimd
        def _(pool):
            nc.gpsimd.memset(mhalf[:], -0.5).then_inc(zeros_ready, 1)
            pool.wait_ge(zeros_ready, 1)
            pool.wait_ge(w_split, len(CH))
            pool_load(pool, 0)
            pool_norm(pool, 0)
            pool_acc(pool, 0)
            program(pool, pool_part)

        @block.vector
        def _(dve):
            nc.vector.memset(over[:], 0.0)
            dve.wait_ge(consts_loaded, 16 * 3)
            for kt in range(KT):
                last = nc.vector.tensor_scalar(G[0][:, kt, :], graw[:, kt, :], g2c[:, kt:kt + 1], None, ALU.mult)
            gate_steps0.link(dve, last)
            for kt in range(KT):
                last = nc.vector.scalar_tensor_tensor(out=G[1][:, kt, :], in0=graw[:, kt, :], scalar=g2c[:, kt:kt + 1],
                                                      in1=G[0][:, kt, :].bitcast(F32), op0=ALU.mult, op1=ALU.subtract)
            gate_steps0.link(dve, last)
            for i, (e, k) in enumerate(CH):
                dve.wait_ge(w_loaded[i % 3], 16 * (i // 3 + 1))
                if k < 2:
                    w = (W1, W3)[k]
                    src = chunk(i).rearrange("p (k n) -> p k n", n=HID)
                    for kt in range(KT):
                        last = nc.vector.tensor_scalar(w[0][:, e, kt, :], src[:, kt, :], g2c[:, kt:kt + 1], None, ALU.mult)
                    hi_steps.link(dve, last)
                    for kt in range(KT):
                        last = nc.vector.scalar_tensor_tensor(out=w[1][:, e, kt, :], in0=src[:, kt, :],
                                                              scalar=g2c[:, kt:kt + 1], in1=w[0][:, e, kt, :].bitcast(F32),
                                                              op0=ALU.mult, op1=ALU.subtract)
                else:
                    src = chunk(i).rearrange("p (k n) -> p k n", n=D)
                    hi_steps.link(dve, nc.vector.tensor_copy(W2[0][:, e, :, :], src))
                    last = nc.vector.tensor_tensor(W2[1][:, e, :, :], src, W2[0][:, e, :, :].bitcast(F32), ALU.subtract)
                last.then_inc(w_split, 1)
            dve_norm(dve, 0)
            dve_turn(dve, 0)
            dve_gate(dve, 0)
            program(dve, dve_part)


_INS = ['L0_attn_x', 'L0_attn_Wq', 'L0_attn_Wk', 'L0_attn_Wv', 'L0_attn_proj', 'L0_attn_Wo', 'L0_attn_bo',
        'L0_ffn_g1', 'L0_ffn_g2', 'L0_ffn_wq', 'L0_ffn_wk', 'L0_ffn_wv', 'L0_ffn_wo', 'L0_ffn_gate',
        'L0_ffn_w1', 'L0_ffn_w2', 'L0_ffn_w3']


def build(nc, t, out):
    qk_d = nc.dram_tensor("qk_scratch", (2, 3 * P, S), F32).ap()
    y2_d = nc.dram_tensor("y2_scratch", (B, S, D), F32).ap()
    z_d = nc.dram_tensor("z_scratch", (B, S, D), F32).ap()
    r1_d = nc.dram_tensor("r1_scratch", (B, S, D), F32).ap()
    softmax_attention(nc, t['L0_attn_x'], t['L0_ffn_g1'], t['L0_ffn_wq'], t['L0_ffn_wk'], t['L0_ffn_wv'],
                      t['L0_ffn_wo'], t['ident'], t['mask'], t['cos'], t['sin'], qk_d, y2_d)
    linear_attention(nc, t['L0_attn_x'], t['L0_attn_Wq'], t['L0_attn_Wk'], t['L0_attn_Wv'], t['L0_attn_proj'],
                     t['L0_attn_Wo'], t['L0_attn_bo'], t['ident'], y2_d, z_d, r1_d)
    experts(nc, t['L0_ffn_g2'], t['L0_ffn_gate'], t['L0_ffn_w1'], t['L0_ffn_w2'], t['L0_ffn_w3'], t['ident'],
            z_d, r1_d, out)


def constants():
    import numpy as np
    q, k = np.arange(P)[:, None], np.arange(P)[None, :]
    inv_freq = (np.float32(1.0) / np.float32(10000.0) ** (np.arange(0, HD, 2, dtype=np.float32) / np.float32(HD)))
    angle = (np.arange(S, dtype=np.float32)[:, None] * inv_freq.astype(np.float32)[None, :]).astype(np.float32)
    angle = np.tile(np.concatenate([angle, angle], axis=-1).T, (P // HD, 1))
    return {
        'ident': np.eye(P, dtype=np.float32),
        'mask': np.where(k > q, np.float32(-1e30), np.float32(0.0)).astype(np.float32),
        'cos': np.ascontiguousarray(np.cos(angle), dtype=np.float32),
        'sin': np.ascontiguousarray(np.sin(angle), dtype=np.float32),
    }


def kernel(**inputs):
    import numpy as np
    import concourse.bacc as bacc
    from concourse.bass_utils import run_bass_kernel_spmd

    nc = bacc.Bacc("TRN2", target_bir_lowering=False, num_devices=1)
    arrays = {f"in_{n}": np.ascontiguousarray(inputs[n]) for n in _INS}
    arrays |= {f"in_{n}": a for n, a in constants().items()}
    t = {n[3:]: nc.dram_tensor(n, a.shape, mybir.dt.from_np(a.dtype), kind="ExternalInput").ap()
         for n, a in arrays.items()}
    out = nc.dram_tensor("out", (B, S, D), F32, kind="ExternalOutput").ap()
    build(nc, t, out)
    r = run_bass_kernel_spmd(nc, [arrays], core_ids=[0])
    return r.results[0]["out"]
```

```python
from contextlib import ExitStack

import concourse.bass as bass
from concourse import mybir

F32 = mybir.dt.float32
F32R = mybir.dt.float32r
BF16 = mybir.dt.bfloat16
ALU = mybir.AluOpType
ACT = mybir.ActivationFunctionType
AX = mybir.AxisListType.X

P = 128
B, S, D = 8, 512, 256
NJ = S // P
KT = D // P
LN_EPS = 1e-5
RMS_EPS = 1.1920928955078125e-07
LIN_EPS = 1e-6

NH, NKV, HD = 16, 4, 16
NU = NH // 2
NQ = NH // 4
PARTS_Q = ((0, 0), (16, 1), (48, 0))
PARTS_K = ((0, 0), (16, 0), (48, 1))
SHIFT_ROW = 32
P_OFF = (0, 512, 1024, 896)

LH, LD = 16, 64
INNER = LH * LD
NP_ = LH // 2
PW = 2 * LD + 1
CT = 32

NE, HID = 4, 768
NM = HID // P


class Steps:

    def __init__(self, sem, per):
        self.sem, self.per, self.b, self.k = sem, per, 0, 0

    def start(self, b):
        self.b, self.k = b, 0

    def link(self, eng, ins):
        self.k += 1
        assert self.k <= self.per, "more steps than counted"
        ins.then_inc(self.sem, 1)
        eng.wait_ge(self.sem, self.b * self.per + self.k)

    def end(self):
        assert self.k == self.per, (self.k, self.per)


def first(b):
    return isinstance(b, int) and b == 0


def mm3(nc, out, lh, ll, rh, rl, start, stop):
    nc.tensor.matmul(out, lh, rh, start=start, stop=False)
    nc.tensor.matmul(out, lh, rl, start=False, stop=False)
    return nc.tensor.matmul(out, ll, rh, start=False, stop=stop)


def softmax_attention(nc, x, g1, wq, wk, wv, wo, ident_d, mask_d, cos_d, sin_d, qk_d, y2_d):
    x_v = x.rearrange("b (j p) d -> b p j d", p=P)
    y2_v = y2_d.rearrange("b (j p) d -> b p j d", p=P)
    qk_v = qk_d.rearrange("h (T p) t -> p T h t", p=P)

    with ExitStack() as ctx:
        def sb(name, shape, dt=F32):
            return ctx.enter_context(nc.sbuf_tensor(name, shape, dt))

        def sem(name):
            return ctx.enter_context(nc.semaphore(name))

        ident = sb("ident", [P, P])
        identb = sb("identb", [P, P], BF16)
        maskM = sb("maskM", [P, P], BF16)
        maskE = sb("maskE", [P, P], BF16)
        cos = sb("cos", [P, S])
        sin = sb("sin", [P, S])
        g1c = sb("g1c", [P, KT])
        WQ, WK, WV = 2 * D, 4 * 64, NKV * HD
        wA = [sb(f"wA{i}", [P, KT, WQ + WK + WV], F32R) for i in range(2)]
        wO = [sb(f"wO{i}", [P, KT, D], F32R) for i in range(2)]
        zrow = sb("zrow", [2, 1, S])

        x_sb = sb("x_sb", [P, NJ, D])
        st = sb("st", [P, NJ, 6])
        mv = sb("mv", [P, NJ, 2])
        vin = sb("vin", [P, 2, NJ])
        inv = sb("inv", [P, 2, NJ])
        vt = sb("vt", [P, NJ])
        sc = sb("sc", [P, NJ])
        mhalf = sb("mhalf", [P, 2 * NJ])
        xr = sb("xr", [P, NJ, D])
        xrT = [sb(f"xrT{i}", [P, KT, S], F32R) for i in range(2)]
        rc = sb("rc", [P, 3, S])
        rs = sb("rs", [P, 3, S])
        raw = rc[:, 0:KT, :]
        mask = rs[:, 0, 0:P]
        qk = sb("qk", [P, 2, 3, S], F32R)
        qs = [sb(f"qs{i}", [P, NU, S], F32R) for i in range(2)]
        kp = [sb(f"kp{i}", [P, 2, NKV, S], F32R) for i in range(2)]
        v32 = [sb(f"v32{i}", [P, NJ, NKV, 32]) for i in range(2)]
        vnew = sb("vnew", [P, NJ, NKV, HD])
        negm = sb("negm", [P, NJ, P])
        negT = sb("negT", [NH, S], F32R)
        prob = sb("prob", [P, 2, 4, 1280])
        oT = sb("oT", [P, 2, S])
        rsum = sb("rsum", [P, NJ, 4])
        on2 = sb("on2", [P, NJ, D])
        o2T = [sb(f"o2T{i}", [P, KT, S], F32R) for i in range(2)]
        y2 = sb("y2", [P, NJ, D])

        ps = ctx.enter_context(nc.psum_tensor("ps", [P, 8, 512], F32))
        FRONT, MAXB, EXPB, PVB, TAILB = 0, 1, 4, 6, 7

        consts_loaded = sem("consts_loaded")
        weights_loaded = sem("weights_loaded")
        pool_prep = Steps(sem("pool_prep_step"), 1)
        dve_prep = Steps(sem("dve_prep_step"), 3)
        weights_ready = sem("weights_ready")
        zeros_ready = sem("zeros_ready")
        mask_turned = sem("mask_turned")
        x_loaded = sem("x_loaded")
        stats_ready = sem("stats_ready")
        roots_ready = sem("roots_ready")
        xr_ready = sem("xr_ready")
        ln_steps = Steps(sem("ln_step"), 6)
        front_psum = sem("front_psum")
        front_evac = sem("front_evac")
        front_hi = sem("front_hi")
        parts_ready = sem("parts_ready")
        parts_steps = Steps(sem("parts_step"), 6)
        parts_stored = sem("parts_stored")
        stacked = [sem(f"stacked{i}") for i in range(2)]
        shift_psum = sem("shift_psum")
        shift_evac = sem("shift_evac")
        v_ready = sem("v_ready")
        max_psum = sem("max_psum")
        max_evac = sem("max_evac")
        shift_loaded = sem("shift_loaded")
        exp_psum = sem("exp_psum")
        exp_done = sem("exp_done")
        pv_done = sem("pv_done")
        pv_evac = sem("pv_evac")
        ot_psum = sem("ot_psum")
        ot_recip = sem("ot_recip")
        ot_evac = sem("ot_evac")
        tail_psum = sem("tail_psum")
        tail_hi = sem("tail_hi")
        tail_evac = sem("tail_evac")
        y2_stored = sem("y2_stored")

        NF, NM_, NX, NT = 9, 6 * NU, 5 * NU, 4
        STACKS = 1 + 2 * 3 + 2 * 3
        MUNITS = [(3, (0,)), (3, (1,)), (2, (0,)), (2, (1,)), (1, (0, 1)), (0, (0, 1))]
        XUNITS = [[(0, 0)], [(0, 1), (0, 3)], [(1, 0)], [(1, 1), (1, 3)], [(0, 2), (1, 2)]]

        def order(f, m, e, t):
            E = [("exp", u, k) for u in range(NU) for k in range(5)] if e is not None else []
            out = []

            def exps(n):
                for _ in range(min(n, len(E))):
                    out.append(E.pop(0))
                    _, u, k = out[-1]
                    if k == 2 and u and u % 2 == 0:
                        out.append(("pv", u // 2 - 1, 0))
                    if k == 1 and u % 2 == 1 and u > 1:
                        out.append(("ot", u // 2 - 1, 0))

            if f is not None:
                out.append(("stats", 0, 0))
            for i in range(6 * NU):
                if m is not None:
                    out.append(("max", i // 6, i % 6))
                if t is not None and i % 2 and i // 2 < NT:
                    out.append(("tail", i // 2, 0))
                if f is not None and i == 7:
                    out.append(("rows", 0, 0))
                if i >= 6 and m is not None:
                    exps(1)
                if f is not None and i >= 10 and i % 3 == 1 and (i - 10) // 3 < NF:
                    out.append(("front", (i - 10) // 3, 0))
            if m is not None:
                out.append(("shift", 0, 0))
            exps(len(E))
            if e is not None:
                out += [("pv", NQ - 1, 0), ("ot", NQ - 1, 0)]
            return out

        def sync_part(sp, f, m, e, t, par):
            if f is not None:
                for T in range(3):
                    sp.wait_ge(parts_ready, 3 * f + 1 + T)
                    sp.dma_start(qk_v[:, T, :, :], qk[:, :, T, :].bitcast(F32)).then_inc(parts_stored, 16)
            if t is not None:
                sp.wait_ge(tail_evac, NT * t + NT)
                sp.dma_start(y2_v[t], y2[:]).then_inc(y2_stored, 16)
            if f is not None:
                load_stacks(sp, f, e, par, 0)
            if m is not None:
                sp.wait_ge(shift_evac, m + 1)
                for a in range(2):
                    r = 64 * a + SHIFT_ROW
                    sp.dma_start(qs[par][r:r + 1, :, :].bitcast(F32),
                                 negT[NU * a:NU * a + NU, :].bitcast(F32)).then_inc(shift_loaded, 16)
            if f is not None:
                load_stacks(sp, f, e, par, 1)

        def load_stacks(sp, f, e, par, half):
            q, k = qs[1 - par][:].bitcast(F32), kp[1 - par][:].bitcast(F32)
            us, gs = slice(4 * half, 4 * half + 4), slice(2 * half, 2 * half + 2)
            if e is not None:
                sp.wait_ge(exp_psum, NX * e + NX // 2 * (half + 1))
            elif first(f):
                sp.wait_ge(zeros_ready, 1)
            if half == 0:
                sp.wait_ge(parts_stored, 16 * 3 * (f + 1))
            sp.dma_start(q[SHIFT_ROW:SHIFT_ROW + 65:64, us, :],
                         zrow[:].broadcast_to([2, NU // 2, S])).then_inc(stacked[half], 16)
            for a in range(2):
                for r, h in PARTS_Q:
                    src = qk_d[h, 0:NH * HD, :].rearrange("(u a c) t -> a c u t", a=2, c=HD)
                    sp.dma_start(q[64 * a + r:64 * a + r + HD, us, :], src[a][:, us, :]).then_inc(stacked[half], 16)
                for r, h in PARTS_K:
                    src = qk_d[h, NH * HD:(NH + NKV) * HD, :].rearrange("(g c) t -> c g t", c=HD)
                    sp.dma_start(k[64 * a + r:64 * a + r + HD, a, gs, :], src[:, gs, :]).then_inc(stacked[half], 16)

        def pe_part(pe, f, m, e, t, par):
            for what, n, k in order(f, m, e, t):
                if what == "front":
                    bank = ps[:, FRONT, :]
                    if n:
                        pe.wait_ge(front_evac, NF * f + n)
                    elif m is not None:
                        if not first(m):
                            pe.wait_ge(shift_evac, m)
                        pe.wait_ge(front_evac, NF * f)
                    if n < KT:
                        pe.wait_ge(xr_ready, NJ * f + NJ)
                        for j in range(NJ):
                            last = nc.tensor.transpose(bank[:, j * P:(j + 1) * P], xr[:, j, n * P:(n + 1) * P], ident[:])
                    elif n < 8:
                        T, rot = (n - 2) // 2, n % 2
                        c = T * P + rot * D if T < 2 else WQ + rot * P
                        for kt in range(KT):
                            w = [wA[i][:, kt, c:c + P] for i in range(2)]
                            last = mm3(nc, bank, w[0], w[1], xrT[0][:, kt, :], xrT[1][:, kt, :], kt == 0, kt == KT - 1)
                    else:
                        for j in range(NJ):
                            for kt in range(KT):
                                l = [xrT[i][:, kt, j * P:(j + 1) * P] for i in range(2)]
                                w = [wA[i][:, kt, WQ + WK:] for i in range(2)]
                                last = mm3(nc, bank[:, j * WV:(j + 1) * WV], l[0], l[1], w[0], w[1],
                                           kt == 0, kt == KT - 1)
                    last.then_inc(front_psum, 1)
                elif what == "max":
                    j, heads = MUNITS[k]
                    i = 6 * n + k
                    if i % (6 * NU // 2) == 0:
                        pe.wait_ge(stacked[i // (6 * NU // 2)], 16 * STACKS * (m + 1))
                    if not (first(m) and i < 3):
                        pe.wait_ge(max_evac, NM_ * m + i - 2)
                    for x, a in enumerate(heads):
                        w = (j + 1) * P
                        o = ps[:, MAXB + i % 3, x * w:(x + 1) * w]
                        nc.tensor.matmul(o, qs[par][:, n, j * P:(j + 1) * P], kp[par][:, a, n // 2, 0:w],
                                         start=True, stop=False)
                        last = nc.tensor.matmul(o[:, w - P:w], identb[:], maskM[:], start=False, stop=True)
                    last.then_inc(max_psum, 1)
                elif what == "shift":
                    pe.wait_ge(front_evac, NF * ((f if f is not None else B - 1) + 1))
                    if not first(m):
                        pe.wait_ge(shift_evac, m)
                    pe.wait_ge(max_evac, NM_ * (m + 1))
                    for j in range(NJ):
                        last = nc.tensor.transpose(ps[:, FRONT, j * P:(j + 1) * P], negm[:, j, :], ident[:])
                    last.then_inc(shift_psum, 1)
                elif what == "exp":
                    i = 5 * n + k
                    if i == 0:
                        pe.wait_ge(shift_loaded, 32 * (e + 1))
                    if not (first(e) and i < 2):
                        pe.wait_ge(exp_done, NX * e + i - 1)
                    at = 0
                    for a, kt in XUNITS[k]:
                        w = S - kt * P
                        o = ps[:, EXPB + i % 2, at:at + w]
                        nc.tensor.matmul(o, kp[1 - par][:, a, n // 2, kt * P:(kt + 1) * P], qs[1 - par][:, n, kt * P:],
                                         start=True, stop=False)
                        last = nc.tensor.matmul(o[:, 0:P], identb[:], maskE[:], start=False, stop=True)
                        at += w
                    last.then_inc(exp_psum, 1)
                elif what == "pv":
                    pe.wait_ge(exp_done, NX * e + 10 * (n + 1))
                    if n == 0:
                        pe.wait_ge(v_ready, e + 1)
                    if not (first(e) and n == 0):
                        pe.wait_ge(pv_evac, NQ * e + n)
                    for i in range(NJ):
                        w = S - i * P
                        for s in range(4):
                            last = nc.tensor.matmul(ps[32 * s:32 * s + 32, PVB, i * P:], v32[1 - par][:, i, n, :],
                                                    prob[:, n % 2, s, P_OFF[i]:P_OFF[i] + w],
                                                    start=(i == 0), stop=(i == NJ - 1),
                                                    tile_position=(0, 32 * s))
                    last.then_inc(pv_done, 1)
                elif what == "ot":
                    pe.wait_ge(pv_evac, NQ * e + n + 1)
                    if n == 0 and t is not None:
                        pe.wait_ge(tail_evac, NT * (t + 1))
                    if n:
                        pe.wait_ge(ot_evac, NQ * e + n)
                    for j in range(NJ):
                        last = nc.tensor.transpose(ps[:, TAILB, j * P:(j + 1) * P], oT[:, n % 2, j * P:(j + 1) * P], ident[:])
                    last.then_inc(ot_psum, 1)
                elif what == "tail":
                    if n == 0:
                        pe.wait_ge(ot_evac, NQ * (t + 1))
                    else:
                        pe.wait_ge(tail_evac, NT * t + n)
                    if n < KT:
                        for j in range(NJ):
                            last = nc.tensor.transpose(ps[:, TAILB, j * P:(j + 1) * P], on2[:, j, n * P:(n + 1) * P], ident[:])
                    else:
                        for i in range(2):
                            j = 2 * (n - KT) + i
                            for kt in range(KT):
                                l = [o2T[h][:, kt, j * P:(j + 1) * P] for h in range(2)]
                                last = mm3(nc, ps[:, TAILB, i * D:(i + 1) * D], l[0], l[1],
                                           wO[0][:, kt, :], wO[1][:, kt, :], kt == 0, kt == KT - 1)
                    last.then_inc(tail_psum, 1)

        def act_part(act, f, m, e, t, par):
            for what, n, k in order(f, m, e, t):
                if what == "front" and n < KT:
                    act.wait_ge(front_psum, NF * f + n + 1)
                    nc.scalar.copy(xrT[0][:, n, :], ps[:, FRONT, :]).then_inc(front_hi, 1)
                elif what == "exp":
                    i = 5 * n + k
                    act.wait_ge(exp_psum, NX * e + i + 1)
                    q = n // 2
                    if n % 2 == 0 and k == 0 and not (first(e) and q < 2):
                        act.wait_ge(pv_done, NQ * e + q - 1)
                    s = 2 * (n % 2)
                    if k < 4:
                        h, kt = XUNITS[k][0]
                        o, w = prob[:, q % 2, s + h, P_OFF[kt]:P_OFF[kt] + 512], ps[:, EXPB + i % 2, :]
                    else:
                        o = prob[:, q % 2, s:s + 2, P_OFF[2]:P_OFF[2] + 256]
                        w = ps[:, EXPB + i % 2, :].rearrange("p (a q) -> p a q", a=2)
                    nc.scalar.activation(o, w, ACT.Exp, scale=HD ** -0.5).then_inc(exp_done, 1)
                elif what == "pv":
                    act.wait_ge(pv_done, NQ * e + n + 1)
                    if not (first(e) and n < 2):
                        act.wait_ge(ot_psum, NQ * e + n - 1)
                    nc.scalar.copy(oT[:, n % 2, :], ps[:, PVB, :]).then_inc(pv_evac, 1)
                elif what == "tail" and n < KT:
                    act.wait_ge(tail_psum, NT * t + n + 1)
                    nc.scalar.copy(o2T[0][:, n, :], ps[:, TAILB, :]).then_inc(tail_hi, 1)

        def dve_part(dve, f, m, e, t, par):
            if m is not None:
                if not (isinstance(m, int) and m < 2):
                    dve.wait_ge(pv_done, NQ * (m - 1))
                dve.wait_ge(front_evac, NF * (m + 1))
                nc.vector.tensor_copy(v32[par][:, :, :, 0:HD], vnew[:]).then_inc(v_ready, 1)
            for what, n, k in order(f, m, e, t):
                bank = ps[:, FRONT, :]
                if what == "stats":
                    ln_steps.start(f)
                    dve.wait_ge(x_loaded, 16 * (f + 1))
                    for j in range(NJ - 1):
                        nc.vector.bn_stats(st[:, j, :], x_sb[:, j, :])
                    ln_steps.link(dve, nc.vector.bn_stats(st[:, NJ - 1, :], x_sb[:, NJ - 1, :]))
                    nc.vector.memset(sc[:, 0:1], 0.0)
                    for j in range(NJ - 1):
                        nc.vector.bn_aggr(mv[:, j, :], st[:, j, :])
                    ln_steps.link(dve, nc.vector.bn_aggr(mv[:, NJ - 1, :], st[:, NJ - 1, :]))
                    var = mv[:, :, 1:2].rearrange("p j o -> p (j o)")
                    ln_steps.link(dve, nc.vector.tensor_scalar(vin[:, 0, :], var, LN_EPS, None, ALU.add))
                    ln_steps.link(dve, nc.vector.reciprocal(vt[:], vin[:, 0, :]))
                    ln_steps.link(dve, nc.vector.tensor_tensor(vt[:], vt[:], var, ALU.mult))
                    nc.vector.tensor_scalar(vin[:, 1, :], vt[:], RMS_EPS, None, ALU.add).then_inc(stats_ready, 1)
                elif what == "rows":
                    dve.wait_ge(roots_ready, f + 1)
                    ln_steps.link(dve, nc.vector.tensor_tensor(sc[:], inv[:, 0, :], inv[:, 1, :], ALU.mult))
                    ln_steps.end()
                    for j in range(NJ):
                        nc.vector.tensor_scalar(xr[:, j, :], x_sb[:, j, :], mv[:, j, 0:1], sc[:, j:j + 1],
                                                ALU.subtract, ALU.mult).then_inc(xr_ready, 1)
                elif what == "front":
                    if n < KT:
                        dve.wait_ge(front_hi, KT * f + n + 1)
                        nc.vector.tensor_tensor(xrT[1][:, n, :], bank, xrT[0][:, n, :].bitcast(F32),
                                                ALU.subtract).then_inc(front_evac, 1)
                    elif n < 8:
                        T, rot = (n - 2) // 2, n % 2
                        dve.wait_ge(front_psum, NF * f + n + 1)
                        if rot == 0 and T == 0 and not first(f):
                            dve.wait_ge(parts_ready, 3 * f)
                        nc.vector.tensor_tensor((rs if rot else rc)[:, T, :], bank, (sin if rot else cos)[:],
                                                ALU.mult).then_inc(front_evac, 1)
                    else:
                        dve.wait_ge(front_psum, NF * f + n + 1)
                        nc.vector.tensor_copy(vnew[:], bank[:, 0:NJ * WV].rearrange("p (j g c) -> p j g c", j=NJ, c=HD)
                                              ).then_inc(front_evac, 1)
                elif what == "max":
                    j, heads = MUNITS[k]
                    i = 6 * n + k
                    dve.wait_ge(max_psum, NM_ * m + i + 1)
                    w = (j + 1) * P
                    src = ps[:, MAXB + i % 3, 0:w * len(heads)].rearrange("p (a k) -> p a k", k=w)
                    if len(heads) == 2:
                        dst = negm[:, j, n:n + NU + 1:NU]
                    else:
                        dst = negm[:, j, heads[0] * NU + n:heads[0] * NU + n + 1]
                    nc.vector.tensor_reduce(dst, src, AX, ALU.max, negate=True).then_inc(max_evac, 1)
                elif what == "shift":
                    dve.wait_ge(shift_psum, m + 1)
                    if not first(m):
                        dve.wait_ge(shift_loaded, 32 * m)
                    nc.vector.tensor_copy(negT[:], ps[0:NH, FRONT, :]).then_inc(shift_evac, 1)
                elif what == "ot":
                    dve.wait_ge(ot_psum, NQ * e + n + 1)
                    o = ps[:, TAILB, :].rearrange("p (j s c) -> p j s c", j=NJ, s=4)
                    nc.vector.reciprocal(rsum[:], o[:, :, :, HD]).then_inc(ot_recip, 1)
                    dve.wait_ge(ot_recip, NQ * e + n + 1)
                    nc.vector.tensor_tensor(on2[:, :, n * 64:(n + 1) * 64].rearrange("p j (s c) -> p j s c", s=4),
                                            o[:, :, :, 0:HD], rsum[:].unsqueeze(3).broadcast_to([P, NJ, 4, HD]),
                                            ALU.mult).then_inc(ot_evac, 1)
                elif what == "tail":
                    if n < KT:
                        dve.wait_ge(tail_hi, KT * t + n + 1)
                        nc.vector.tensor_tensor(o2T[1][:, n, :], ps[:, TAILB, :], o2T[0][:, n, :].bitcast(F32),
                                                ALU.subtract).then_inc(tail_evac, 1)
                    else:
                        dve.wait_ge(tail_psum, NT * t + n + 1)
                        if n == KT and not first(t):
                            dve.wait_ge(y2_stored, 16 * t)
                        j = 2 * (n - KT)
                        nc.vector.tensor_copy(y2[:, j:j + 2, :],
                                              ps[:, TAILB, :].rearrange("p (j d) -> p j d", j=2)).then_inc(tail_evac, 1)

        def pool_part(pool, f, m, e, t, par):
            if f is None:
                return
            if not first(f):
                pool.wait_ge(xr_ready, NJ * f)
            pool.dma_start(x_sb[:], x_v[f]).then_inc(x_loaded, 16)
            pool.wait_ge(stats_ready, f + 1)
            nc.gpsimd.tensor_tensor(inv[:].rearrange("p a j -> p (a j)"), vin[:].rearrange("p a j -> p (a j)"),
                                    mhalf[:], ALU.pow).then_inc(roots_ready, 1)
            parts_steps.start(f)
            for T in range(3):
                pool.wait_ge(front_evac, NF * f + 2 * T + 4)
                if T == 0 and not first(f):
                    pool.wait_ge(parts_stored, 16 * 3 * f)
                parts_steps.link(pool, nc.gpsimd.tensor_tensor(qk[:, 0, T, :], rc[:, T, :], rs[:, T, :], ALU.add))
                parts_steps.link(pool, nc.gpsimd.tensor_tensor(rc[:, T, :], rc[:, T, :], rs[:, T, :], ALU.add))
                nc.gpsimd.tensor_tensor(qk[:, 1, T, :], rc[:, T, :], qk[:, 0, T, :].bitcast(F32),
                                        ALU.subtract).then_inc(parts_ready, 1)
            parts_steps.end()

        def program(eng, part):
            part(eng, 0, None, None, None, 1)
            part(eng, 1, 0, None, None, 0)
            part(eng, 2, 1, 0, None, 1)
            part(eng, 3, 2, 1, 0, 0)
            with eng.Fori(1, B // 2 - 1) as i:
                m = 2 * i + 1
                part(eng, m + 1, m, m - 1, m - 2, 1)
                part(eng, m + 2, m + 1, m, m - 1, 0)
            part(eng, None, B - 1, B - 2, B - 3, 1)
            part(eng, None, None, B - 1, B - 2, 0)
            part(eng, None, None, None, B - 1, 1)

        block = ctx.enter_context(nc.Block())

        @block.sync
        def _(sp):
            sp.dma_start(ident[:], ident_d).then_inc(consts_loaded, 16)
            sp.dma_start(mask, mask_d).then_inc(consts_loaded, 16)
            sp.dma_start(cos[:], cos_d).then_inc(consts_loaded, 16)
            sp.dma_start(sin[:], sin_d).then_inc(consts_loaded, 16)
            sp.dma_start(g1c[:], g1.rearrange("(k p) -> p k", p=P), allow_slow_non_contiguous=True).then_inc(consts_loaded, 16)
            sp.dma_start(raw[:, :, 0:D], wq.rearrange("(k p) n -> p k n", p=P)).then_inc(weights_loaded, 16)
            sp.dma_start(raw[:, :, D:D + WV], wk.rearrange("(k p) n -> p k n", p=P)).then_inc(weights_loaded, 16)
            sp.dma_start(raw[:, :, D + WV:D + 2 * WV], wv.rearrange("(k p) n -> p k n", p=P)).then_inc(weights_loaded, 16)
            sp.dma_start(on2[:, 0:KT, :], wo.rearrange("(k p) n -> p k n", p=P)).then_inc(weights_loaded, 16)
            program(sp, sync_part)
            sp.wait_ge(y2_stored, 16 * B)

        @block.tensor
        def _(pe):
            pe.wait_ge(consts_loaded, 16 * 5)
            nc.tensor.transpose(ps[:, TAILB, 0:P], mask, ident[:]).then_inc(mask_turned, 1)
            pe.wait_ge(weights_ready, 2)
            pe.wait_ge(zeros_ready, 1)
            program(pe, pe_part)

        @block.scalar
        def _(act):
            program(act, act_part)

        @block.gpsimd
        def _(pool):
            nc.gpsimd.memset(mhalf[:], -0.5)
            for i in range(2):
                nc.gpsimd.memset(v32[i][:], 0.0)
                nc.gpsimd.memset(qs[i][:].bitcast(F32), 0.0)
                nc.gpsimd.memset(kp[i][:].bitcast(F32), 0.0)
            nc.gpsimd.memset(negm[:], 0.0)
            pool_prep.link(pool, nc.gpsimd.memset(zrow[:], 0.0))
            for i in range(2):
                last = nc.gpsimd.memset(v32[i][:, :, :, HD:HD + 1], 1.0)
            last.then_inc(zeros_ready, 1)
            program(pool, pool_part)

        @block.vector
        def _(dve):
            dve.wait_ge(consts_loaded, 16 * 5)
            nc.vector.tensor_copy(identb[:], ident[:])
            nc.vector.tensor_copy(maskM[:], mask)
            dve.wait_ge(mask_turned, 1)
            nc.vector.tensor_copy(maskE[:], ps[:, TAILB, 0:P]).then_inc(weights_ready, 1)
            dve.wait_ge(weights_loaded, 16 * 4)
            for kt in range(KT):
                ins = nc.vector.tensor_scalar(raw[:, kt, 0:D + 2 * WV], raw[:, kt, 0:D + 2 * WV],
                                              g1c[:, kt:kt + 1], None, ALU.mult)
            dve_prep.link(dve, ins)
            hi, lo = wA
            q = raw[:, :, 0:D]

            def halves(ap):
                return ap.rearrange("p k (h c) -> p k h c", c=HD)

            for kt in range(KT):
                qv = raw[:, kt, 0:D].rearrange("p (h c) -> p h c", c=HD)
                kv = raw[:, kt, D:D + WV].rearrange("p (h c) -> p h c", c=HD)
                nc.vector.tensor_copy(hi[:, kt, 0:D], raw[:, kt, 0:D])
                nc.vector.tensor_copy(hi[:, kt, WQ + WK:], raw[:, kt, D + WV:D + 2 * WV])
                for src, at, n in ((qv, D, D), (kv, WQ + P, WV), (kv, WQ + P + WV, WV)):
                    dst = hi[:, kt, at:at + n].rearrange("p (h c) -> p h c", c=HD)
                    nc.vector.tensor_scalar(dst[:, :, 0:8], src[:, :, 8:16], -1.0, None, ALU.mult)
                    nc.vector.tensor_copy(dst[:, :, 8:16], src[:, :, 0:8])
                for at in (WQ, WQ + WV):
                    nc.vector.tensor_copy(hi[:, kt, at:at + WV], raw[:, kt, D:D + WV])
            dve_prep.link(dve, nc.vector.tensor_copy(wO[0][:], on2[:, 0:KT, :]))
            for kt in range(KT):
                h32 = hi[:, kt, :].bitcast(F32)
                qv = raw[:, kt, 0:D].rearrange("p (h c) -> p h c", c=HD)
                kv = raw[:, kt, D:D + WV].rearrange("p (h c) -> p h c", c=HD)
                for src, at, n in ((raw[:, kt, 0:D], 0, D), (raw[:, kt, D:D + WV], WQ, WV),
                                   (raw[:, kt, D:D + WV], WQ + WV, WV), (raw[:, kt, D + WV:D + 2 * WV], WQ + WK, WV)):
                    nc.vector.tensor_tensor(lo[:, kt, at:at + n], src, h32[:, at:at + n], ALU.subtract)
                for src, at, n in ((qv, D, D), (kv, WQ + P, WV), (kv, WQ + P + WV, WV)):
                    dst = lo[:, kt, at:at + n].rearrange("p (h c) -> p h c", c=HD)
                    h = h32[:, at:at + n].rearrange("p (h c) -> p h c", c=HD)
                    nc.vector.scalar_tensor_tensor(out=dst[:, :, 0:8], in0=src[:, :, 8:16], scalar=-1.0, in1=h[:, :, 0:8],
                                                   op0=ALU.mult, op1=ALU.subtract)
                    nc.vector.tensor_tensor(dst[:, :, 8:16], src[:, :, 0:8], h[:, :, 8:16], ALU.subtract)
            dve_prep.link(dve, nc.vector.tensor_tensor(wO[1][:], on2[:, 0:KT, :], wO[0][:].bitcast(F32), ALU.subtract))
            dve.wait_ge(zeros_ready, 1)
            for i in range(2):
                for a in range(2):
                    r = 64 * a + SHIFT_ROW
                    last = nc.vector.memset(kp[i][r:r + 1, a, :, :].bitcast(F32), 1.0)
            last.then_inc(weights_ready, 1)
            program(dve, dve_part)


def linear_attention(nc, x, wq, wk, wv, proj, wo, bo, ident_d, sel_d, y2_d, z_d, r1_d):
    def tiles(ap):
        return ap.rearrange("b (j p) d -> b p j d", p=P)

    x_v, y2_v, z_v, r1_v = map(tiles, (x, y2_d, z_d, r1_d))

    with ExitStack() as ctx:
        def sb(name, shape, dt=F32):
            return ctx.enter_context(nc.sbuf_tensor(name, shape, dt))

        def sem(name):
            return ctx.enter_context(nc.semaphore(name))

        ident = sb("ident2", [P, P])
        pblk = sb("pblk", [P, P])
        bob = sb("bob", [P, D])
        mhalf = sb("mhalf2", [P, NJ])
        WQ, WK, WV = ([sb(f"{n}{i}", [P, KT, INNER], F32R) for i in range(2)] for n in ("WQ", "WK", "WV"))
        WO = [sb(f"WO{i}", [P, NP_, D], F32R) for i in range(2)]

        xn = sb("xn", [P, NJ, D])
        st = sb("st2", [P, NJ, 6])
        pad = sb("pad2", [P, 1])
        mv = sb("mv2", [P, NJ, 2])
        vin = sb("vin2", [P, NJ])
        inv = sb("inv2", [P, NJ])
        xb = sb("xb", [P, NJ, D])
        r1 = sb("r1", [P, NJ, D])
        xnT = [sb(f"xnT{i}", [P, KT, S], F32R) for i in range(2)]
        kf = sb("kf", [P, NJ, INNER])
        va = sb("va", [P, NJ, NP_, PW])
        epsb = sb("epsb", [P, 1])
        hm = sb("hm", [P, NP_, CT])
        SEL = sb("SEL", [P, NP_, P], F32R)
        lowm = sb("lowm", [P, 1])
        KV = [sb(f"KV{i}", [P, NP_, P], F32R) for i in range(2)]
        KW = [sb(f"KW{i}", [P, NP_, D], F32R) for i in range(2)]
        kss = sb("kss", [P, NP_, CT])
        qf = sb("qf", [P, NP_, S])
        rdT = sb("rdT", [P, S], F32R)
        NQR = 4
        qs = sb("qs", [P, NQR, S])
        kvf = qs[:, 0:2, :].rearrange("p a (q c) -> p (a q) c", c=P)
        rd, rh = qs[:, 3, :], qs[:, 2, :].bitcast(F32R)
        QS = [sb(f"QS{i}", [P, NP_, S], F32R) for i in range(2)]

        ps = ctx.enter_context(nc.psum_tensor("ps2", [P, 8, 512], F32))
        RING, KVB, DENB, DB, YB = 0, 2, 4, 5, 7
        NUM = [(KVB + i // 3, (i % 3) * PW) for i in range(NP_)]

        consts_loaded = sem("consts2_loaded")
        w_loaded = sem("w2_loaded")
        pblk_zero = sem("pblk_zero")
        turned = sem("w_turned")
        turned_copied = sem("w_turned_copied")
        folded = sem("w_folded")
        hi_made = sem("w_hi_made")
        lo_made = sem("w_lo_made")
        pool_lo_made = sem("w_pool_lo_made")
        zeros_ready = sem("zeros2_ready")
        mhalf_ready = sem("mhalf2_ready")
        ones_ready = sem("ones2_ready")
        x_loaded = sem("x2_loaded")
        y2_loaded = sem("y2_loaded")
        xb_loaded = sem("xb_loaded")
        stats_ready = sem("stats2_ready")
        roots_ready = sem("roots2_ready")
        ln_steps = Steps(sem("ln2_step"), 2)
        xn_ready = sem("xn_ready")
        r1_ready = sem("r1_ready")
        r1_stored = sem("r1_stored")
        xb_ready = sem("xb_ready")
        ring_psum = sem("ring_psum")
        t_hi = sem("t_hi")
        ring_evac_dve = sem("ring_evac_dve")
        ring_evac_act = sem("ring_evac_act")
        kv_psum = sem("kv_psum")
        kv_evac = sem("kv_evac")
        kvt_psum = sem("kvt_psum")
        kv_hi = sem("kv_hi")
        kv_lo = sem("kv_lo")
        kss_ready = sem("kss_ready")
        den_psum = sem("den_psum")
        den_evac = sem("den_evac")
        rd_ready = sem("rd_ready")
        rd_hi = sem("rd_hi")
        rdt_ready = sem("rdt_ready")
        spread_psum = sem("spread_psum")
        qs_ready = sem("qs_ready")
        qs_hi = sem("qs_hi")
        qs_lo = sem("qs_lo")
        kw_psum = sem("kw_psum")
        kw_hi = sem("kw_hi")
        kw_lo = sem("kw_lo")
        y_psum = sem("y_psum")
        y_evac = sem("y_evac")
        z_stored = sem("z_stored")

        NR = 16 + NP_ + KT
        NRD, NRA = 8 + NP_ + KT, 8
        SPREAD_AFTER = range(4, 4 + NP_)
        OUT_AFTER = range(13, 16)
        NKW = NP_ // 2

        def ring_free(eng, base, u):
            u -= 2
            if u < 0:
                eng.wait_ge(ring_evac_dve, NRD * base + KT + u + 1)
            elif u < 16 and u % 4 >= 2:
                eng.wait_ge(ring_evac_act, NRA * base + 2 * (u // 4) + u % 4 - 1)
            elif u < 16:
                eng.wait_ge(ring_evac_dve, NRD * base + KT + 2 * (u // 4) + u % 4 + 1)
            else:
                eng.wait_ge(ring_evac_dve, NRD * base + KT + 8 + (u - 16) + 1)

        def pe_turn(pe, n):
            for kt in range(KT):
                if not first(n):
                    ring_free(pe, n - 1, NR - KT + kt)
                if kt == 0:
                    pe.wait_ge(xn_ready, NJ * n + NJ)
                for j in range(NJ):
                    last = nc.tensor.transpose(ps[:, RING + kt, j * P:(j + 1) * P], xn[:, j, kt * P:(kt + 1) * P], ident[:])
                last.then_inc(ring_psum, 1)

        def pe_out(pe, e, j):
            if j == 0:
                pe.wait_ge(qs_lo, NP_ * (e + 1))
                pe.wait_ge(kw_lo, NKW * (e + 1))
            elif j == 2:
                pe.wait_ge(y_evac, 2 * e + 1)
            for p in range(NP_):
                l = [QS[i][:, p, j * P:(j + 1) * P] for i in range(2)]
                last = mm3(nc, ps[:, YB, (j % 2) * D:(j % 2 + 1) * D], *l, KW[0][:, p, :], KW[1][:, p, :],
                           p == 0, p == NP_ - 1)
            last.then_inc(y_psum, 1)

        def pe_spread(pe, e, p):
            if p == 0:
                pe.wait_ge(rdt_ready, e + 1)
            if p < 2:
                pe.wait_ge(kw_lo, NKW * (e + 1) - 1 + p)
            else:
                pe.wait_ge(qs_ready, NP_ * e + p - 1)
            nc.tensor.matmul(ps[:, DB + p % 2, :], SEL[:, p, :], rdT[:], start=True, stop=True).then_inc(spread_psum, 1)

        def pe_part(pe, b, n):
            pe.wait_ge(ring_evac_dve, NRD * b + KT)
            for u in range(16):
                j, w, half = u // 4, (WK, WK, WV, WV)[u % 4], u % 2
                ring_free(pe, b, u)
                for kt in range(KT):
                    l = [xnT[i][:, kt, j * P:(j + 1) * P] for i in range(2)]
                    r = [w[i][:, kt, half * 512:(half + 1) * 512] for i in range(2)]
                    last = mm3(nc, ps[:, RING + u % 2, :], *l, *r, kt == 0, kt == KT - 1)
                last.then_inc(ring_psum, 1)
                if first(b):
                    continue
                if u in SPREAD_AFTER:
                    pe_spread(pe, b - 1, SPREAD_AFTER.index(u))
                elif u in OUT_AFTER:
                    pe_out(pe, b - 1, OUT_AFTER.index(u))

            def query(p):
                ring_free(pe, b, 16 + p)
                for kt in range(KT):
                    l = [WQ[i][:, kt, p * P:(p + 1) * P] for i in range(2)]
                    last = mm3(nc, ps[:, RING + p % 2, :], *l, xnT[0][:, kt, :], xnT[1][:, kt, :], kt == 0, kt == KT - 1)
                last.then_inc(ring_psum, 1)

            def kw(i):
                if i == 0:
                    pe.wait_ge(kv_lo, 2 * (b + 1))
                if i >= 2:
                    pe.wait_ge(kw_lo, NKW * b + i - 1)
                elif not first(b):
                    pe.wait_ge(qs_ready, NP_ * b - 1 + i)
                for a in range(2):
                    p = 2 * i + a
                    last = mm3(nc, ps[:, DB + i % 2, a * D:(a + 1) * D], KV[0][:, p, :], KV[1][:, p, :],
                               WO[0][:, p, :], WO[1][:, p, :], True, True)
                last.then_inc(kw_psum, 1)

            query(0)
            query(1)
            if not first(b):
                pe_out(pe, b - 1, NJ - 1)
            pe.wait_ge(ring_evac_dve, NRD * b + KT + 8)
            pe.wait_ge(ring_evac_act, NRA * (b + 1))
            for p in range(NP_):
                bank, at = NUM[p]
                for j in range(NJ):
                    last = nc.tensor.matmul(ps[:, bank, at:at + PW], kf[:, j, p * P:(p + 1) * P], va[:, j, p, :],
                                            start=(j == 0), stop=(j == NJ - 1))
            last.then_inc(kv_psum, 1)
            query(2)
            query(3)
            pe.wait_ge(kv_evac, b + 1)
            pe.wait_ge(kss_ready, b + 1)
            for p in range(NP_):
                last = nc.tensor.transpose(ps[:, KVB + p // 4, (p % 4) * P:(p % 4 + 1) * P], kvf[:, p, :], ident[:])
            last.then_inc(kvt_psum, 1)
            for p in range(4, NP_):
                query(p)
            kw(0)
            if n is not None:
                pe_turn(pe, n)
            kw(1)
            pe.wait_ge(ring_evac_dve, NRD * b + KT + 8 + NP_)
            for g in range(2):
                for c in range(4):
                    p = 4 * g + c
                    last = nc.tensor.matmul(ps[CT * c:CT * c + CT, DENB, :], kss[:, p, :], qf[:, p, :],
                                            start=(g == 0), stop=(g == 1), tile_position=(0, CT * c))
            last.then_inc(den_psum, 1)
            for i in range(2, NKW):
                kw(i)

        def pe_finish(pe, e):
            for p in range(NP_):
                pe_spread(pe, e, p)
            for j in range(NJ):
                pe_out(pe, e, j)

        def act_turn(act, n):
            for kt in range(KT):
                act.wait_ge(ring_psum, NR * n + kt + 1)
                nc.scalar.copy(xnT[0][:, kt, :], ps[:, RING + kt, :]).then_inc(t_hi, 1)

        def act_high(act, e, p):
            act.wait_ge(qs_ready, NP_ * e + p + 1)
            nc.scalar.copy(QS[0][:, p, :], qs[:, p % NQR, :]).then_inc(qs_hi, 1)

        HIGH_BEFORE = ((), (), (0, 1), (2,), (3, 4, 5), (6,), (7,), ())

        def act_part(act, b, n):
            if not first(b):
                act.wait_ge(kv_psum, b)
            for j in range(NJ):
                for h in range(2):
                    if not first(b):
                        for p in HIGH_BEFORE[2 * j + h]:
                            act_high(act, b - 1, p)
                    act.wait_ge(ring_psum, NR * b + KT + 4 * j + 2 + h + 1)
                    nc.scalar.copy(va[:, j, 4 * h:4 * h + 4, 0:P],
                                   ps[:, RING + h, :].rearrange("p (q c) -> p q c", c=P)).then_inc(ring_evac_act, 1)
                if j == 0 and not first(b):
                    act_rd(act, b - 1)
            act.wait_ge(kv_psum, b + 1)
            for bank in range(3):
                m = min(3, NP_ - 3 * bank)
                last = nc.scalar.copy(kvf[:, 3 * bank:3 * bank + m, :],
                                      ps[:, KVB + bank, 0:m * PW].rearrange("p (q c) -> p q c", c=PW)[:, :, 0:P])
            last.then_inc(kv_evac, 1)
            act.wait_ge(kvt_psum, b + 1)
            for a in range(2):
                nc.scalar.copy(diagonal(KV[0], a), diagonal(kvt, a)).then_inc(kv_hi, 1)
            for i in range(NKW):
                if i == 1 and n is not None:
                    act_turn(act, n)
                if i == 2:
                    act.wait_ge(den_psum, b + 1)
                    nc.scalar.activation(rd, ps[:, DENB, :], ACT.Identity, bias=epsb[:]).then_inc(den_evac, 1)
                act.wait_ge(kw_psum, NKW * b + i + 1)
                nc.scalar.copy(KW[0][:, 2 * i:2 * i + 2, :], ps[:, DB + i % 2, :].rearrange("p (a d) -> p a d", a=2)
                               ).then_inc(kw_hi, 1)

        def act_finish(act, e):
            act_rd(act, e)
            for p in range(NP_):
                act_high(act, e, p)

        def act_rd(act, e):
            act.wait_ge(rd_ready, e + 1)
            nc.scalar.copy(rh, rd).then_inc(rd_hi, 1)

        va_k = va[:, 0:2, :, :].rearrange("p j q c -> p (j q c)")[:, 0:KT * INNER].rearrange("p (k n) -> p k n", k=KT)
        kvt = ps[:, KVB:KVB + 2, :].rearrange("p b (q c) -> p (b q) c", c=P)

        def diagonal(t, a):
            return t[64 * a:64 * a + 64, :, LD * a:LD * a + LD]

        def dve_stats(dve, n):
            ln_steps.start(n)
            dve.wait_ge(x_loaded, 16 * (n + 1))
            for j in range(NJ):
                last = nc.vector.bn_stats(st[:, j, :], xn[:, j, :])
            ln_steps.link(dve, last)
            nc.vector.memset(pad[:], 0.0)
            for j in range(NJ):
                last = nc.vector.bn_aggr(mv[:, j, :], st[:, j, :])
            ln_steps.link(dve, last)
            nc.vector.tensor_scalar(vin[:], mv[:, :, 1:2].rearrange("p j o -> p (j o)"), LN_EPS, None,
                                    ALU.add).then_inc(stats_ready, 1)
            ln_steps.end()

        def dve_xn(dve, n):
            dve.wait_ge(roots_ready, n + 1)
            for j in range(NJ):
                nc.vector.tensor_scalar(xn[:, j, :], xn[:, j, :], mv[:, j, 0:1], inv[:, j:j + 1],
                                        ALU.subtract, ALU.mult).then_inc(xn_ready, 1)

        def dve_r1(dve, n):
            dve.wait_ge(xn_ready, NJ * (n + 1))
            dve.wait_ge(y2_loaded, 16 * (n + 1))
            nc.vector.tensor_tensor(r1[:], r1[:], xn[:], ALU.add).then_inc(r1_ready, 1)

        def dve_turn(dve, n):
            for kt in range(KT):
                dve.wait_ge(t_hi, KT * n + kt + 1)
                nc.vector.tensor_tensor(xnT[1][:, kt, :], ps[:, RING + kt, :], xnT[0][:, kt, :].bitcast(F32),
                                        ALU.subtract).then_inc(ring_evac_dve, 1)

        def dve_z(dve, e, i):
            dve.wait_ge(y_psum, NJ * e + 2 * i + 2)
            dve.wait_ge(xb_ready, e + 1)
            nc.vector.tensor_tensor(xb[:, 2 * i:2 * i + 2, :], ps[:, YB, :].rearrange("p (j d) -> p j d", j=2),
                                    xb[:, 2 * i:2 * i + 2, :], ALU.add).then_inc(y_evac, 1)

        def dve_scale(dve, e, p):
            dve.wait_ge(spread_psum, NP_ * e + p + 1)
            if p >= NQR:
                dve.wait_ge(qs_lo, NP_ * e + p - NQR + 1)
            nc.vector.tensor_tensor(qs[:, p % NQR, :], ps[:, DB + p % 2, :], qf[:, p, :], ALU.mult).then_inc(qs_ready, 1)

        SCALE_AFTER = ((), (), (0,), (1, 2, 3), (4,), (5, 6, 7), (), ())

        def dve_part(dve, b, n):
            if not first(b):
                dve.wait_ge(kv_psum, b)
            for j in range(NJ):
                for h in range(2):
                    dve.wait_ge(ring_psum, NR * b + KT + 4 * j + h + 1)
                    nc.vector.tensor_scalar(kf[:, j, h * 512:(h + 1) * 512], ps[:, RING + h, :], 0.0, LIN_EPS,
                                            ALU.max, ALU.add).then_inc(ring_evac_dve, 1)
                    if not first(b):
                        if j == 1 and h == 0:
                            dve_rdt(dve, b - 1)
                        for p in SCALE_AFTER[2 * j + h]:
                            dve_scale(dve, b - 1, p)
                    if h and j == 0 and not first(b):
                        dve_rd(dve, b - 1)
                if n is not None and j:
                    (dve_stats, dve_xn, dve_r1)[j - 1](dve, n)
            if not first(b):
                dve_z(dve, b - 1, 0)

            def query(p):
                if p == 0 and not first(b):
                    dve.wait_ge(qs_ready, NP_ * b)
                    dve.wait_ge(den_psum, b)
                dve.wait_ge(ring_psum, NR * b + KT + 16 + p + 1)
                nc.vector.tensor_scalar(qf[:, p, :], ps[:, RING + p % 2, :], 0.0, LIN_EPS,
                                        ALU.max, ALU.add).then_inc(ring_evac_dve, 1)

            def kw(i):
                dve.wait_ge(kw_hi, NKW * b + i + 1)
                nc.vector.tensor_tensor(KW[1][:, 2 * i:2 * i + 2, :], ps[:, DB + i % 2, :].rearrange("p (a d) -> p a d", a=2),
                                        KW[0][:, 2 * i:2 * i + 2, :].bitcast(F32), ALU.subtract).then_inc(kw_lo, 1)

            query(0)
            query(1)
            if not first(b):
                dve_z(dve, b - 1, 1)
            dve.wait_ge(kv_evac, b + 1)
            for bank in range(3):
                m = min(3, NP_ - 3 * bank)
                sums = ps[:, KVB + bank, 0:m * PW].rearrange("p (q c) -> p q c", c=PW)[:, :, P:P + 1]
                last = nc.vector.tensor_tensor(kss[:, 3 * bank:3 * bank + m, :], hm[:, 3 * bank:3 * bank + m, :],
                                               sums.broadcast_to([P, m, CT]), ALU.mult)
            last.then_inc(kss_ready, 1)
            query(2)
            query(3)
            for a in range(2):
                dve.wait_ge(kv_hi, 2 * b + a + 1)
                nc.vector.tensor_tensor(diagonal(KV[1], a), diagonal(kvt, a), diagonal(KV[0], a).bitcast(F32),
                                        ALU.subtract).then_inc(kv_lo, 1)
            for p in range(4, NP_):
                query(p)
            for i in range(NKW):
                if i == 1 and n is not None:
                    dve_turn(dve, n)
                kw(i)

        def dve_rd(dve, e):
            dve.wait_ge(den_evac, e + 1)
            nc.vector.reciprocal(rd, rd).then_inc(rd_ready, 1)

        def dve_rdt(dve, e):
            dve.wait_ge(rd_hi, e + 1)
            nc.vector.scalar_tensor_tensor(out=rdT[:], in0=rh.bitcast(F32), scalar=lowm[:, 0:1], in1=rd,
                                           op0=ALU.mult, op1=ALU.add).then_inc(rdt_ready, 1)
        def dve_finish(dve, e):
            dve_rd(dve, e)
            dve_rdt(dve, e)
            for p in range(NP_):
                dve_scale(dve, e, p)
            for i in range(2):
                dve_z(dve, e, i)

        def pool_norm(pool, n):
            pool.wait_ge(stats_ready, n + 1)
            nc.gpsimd.tensor_tensor(inv[:], vin[:], mhalf[:], ALU.pow).then_inc(roots_ready, 1)

        def pool_bias(pool, b):
            pool.wait_ge(xb_loaded, 16 * (b + 1))
            nc.gpsimd.tensor_tensor(xb[:], xb[:], bob[:].unsqueeze(1).broadcast_to([P, NJ, D]),
                                    ALU.add).then_inc(xb_ready, 1)

        def pool_load(pool, n):
            if not first(n):
                pool.wait_ge(r1_ready, n)
                pool.wait_ge(ring_psum, NR * (n - 1) + KT)
            pool.dma_start(xn[:], x_v[n]).then_inc(x_loaded, 16)

        def pool_part(pool, b, n):
            if n is not None:
                pool_load(pool, n)
            if not first(b):
                pool_low(pool, b - 1)
            if n is not None:
                pool_norm(pool, n)
            pool_bias(pool, b)

        def pool_low(pool, e):
            for p in range(NP_):
                pool.wait_ge(qs_hi, NP_ * e + p + 1)
                nc.gpsimd.tensor_tensor(QS[1][:, p, :], qs[:, p % NQR, :], QS[0][:, p, :].bitcast(F32),
                                        ALU.subtract).then_inc(qs_lo, 1)

        def sync_load(sp, n):
            if not first(n):
                sp.wait_ge(r1_stored, 16 * n)
            sp.dma_start(r1[:], y2_v[n]).then_inc(y2_loaded, 16)

        def sync_part(sp, b, n):
            sp.wait_ge(r1_ready, b + 1)
            sp.dma_start(r1_v[b], r1[:]).then_inc(r1_stored, 16)
            if n is not None:
                sync_load(sp, n)
            if not first(b):
                sync_z(sp, b - 1)
                sp.wait_ge(z_stored, 16 * b)
            sp.dma_start(xb[:], x_v[b]).then_inc(xb_loaded, 16)

        def sync_z(sp, e):
            sp.wait_ge(y_evac, 2 * (e + 1))
            sp.dma_start(z_v[e], xb[:]).then_inc(z_stored, 16)

        def program(eng, part):
            part(eng, 0, 1)
            with eng.Fori(1, B - 1) as b:
                part(eng, b, b + 1)
            part(eng, B - 1, None)

        block = ctx.enter_context(nc.Block())

        @block.sync
        def _(sp):
            sp.dma_start(ident[:], ident_d).then_inc(consts_loaded, 16)
            sp.dma_start(bob[:], bo.rearrange("(a d) -> a d", a=1).broadcast_to([P, D])).then_inc(consts_loaded, 16)
            sp.dma_start(qf[:, 4:7, :].rearrange("p a n -> p (a n)")[:, 0:NP_ * P + 1], sel_d).then_inc(consts_loaded, 16)
            sp.wait_ge(pblk_zero, 1)
            for a in range(2):
                sp.dma_start(pblk[64 * a:64 * a + 64, 64 * a:64 * a + 64], proj).then_inc(consts_loaded, 16)
            for i, w in enumerate((wq, wk)):
                sp.dma_start(kf[:, 2 * i:2 * i + 2, :], w.rearrange("(k p) n -> p k n", p=P)).then_inc(w_loaded, 16)
            sp.dma_start(va_k,
                         wv.rearrange("(k p) n -> p k n", p=P)).then_inc(w_loaded, 16)
            sp.dma_start(qs[:].rearrange("p a n -> p (a n)").rearrange("p (k n) -> p k n", k=NP_),
                         wo.rearrange("(k p) n -> p k n", p=P)).then_inc(w_loaded, 16)
            sync_load(sp, 0)
            program(sp, sync_part)
            sync_z(sp, B - 1)
            sp.wait_ge(z_stored, 16 * B)
            sp.wait_ge(r1_stored, 16 * B)

        @block.tensor
        def _(pe):
            pe.wait_ge(consts_loaded, 16 * 5)
            for i in range(2):
                pe.wait_ge(w_loaded, 16 * 4)
                for p in range(NP_):
                    for kt in range(KT):
                        c = p * D + kt * P
                        last = nc.tensor.transpose(ps[:, c // 512, c % 512:c % 512 + P],
                                                   kf[:, 2 * i + kt, p * P:(p + 1) * P], ident[:])
                last.then_inc(turned, 1)
                pe.wait_ge(turned_copied, i + 1)
                if i:
                    pe.wait_ge(lo_made, 1)
                for kt in range(KT):
                    for p in range(NP_):
                        c = p * P
                        last = nc.tensor.matmul(ps[:, 4 + 2 * kt + c // 512, c % 512:c % 512 + P],
                                                qf[:, p // 2, (p % 2) * D + kt * P:(p % 2) * D + (kt + 1) * P], pblk[:],
                                                start=True, stop=True)
                last.then_inc(folded, 1)
            pe.wait_ge(lo_made, 2)
            pe.wait_ge(zeros_ready, 3)
            pe.wait_ge(ones_ready, 1)
            pe.wait_ge(pool_lo_made, 2)
            pe_turn(pe, 0)
            program(pe, pe_part)
            pe_finish(pe, B - 1)

        @block.scalar
        def _(act):
            act.wait_ge(w_loaded, 16 * 4)
            nc.scalar.copy(WV[0][:], va_k).then_inc(hi_made, 1)
            nc.scalar.copy(WO[0][:], qs[:].rearrange("p a n -> p (a n)").rearrange("p (k n) -> p k n", k=NP_)
                           ).then_inc(hi_made, 1)
            for i, w in enumerate((WQ, WK)):
                act.wait_ge(turned, i + 1)
                if i:
                    act.wait_ge(folded, 1)
                nc.scalar.copy(qf[:, 0:4, :], ps[:, 0:4, :]).then_inc(turned_copied, 1)
                act.wait_ge(folded, i + 1)
                for kt in range(KT):
                    nc.scalar.copy(w[0][:, kt, :].rearrange("p (b n) -> p b n", b=2),
                                   ps[:, 4 + 2 * kt:6 + 2 * kt, :]).then_inc(hi_made, 1)
            act.wait_ge(lo_made, 2)
            act.wait_ge(pool_lo_made, 2)
            act.wait_ge(zeros_ready, 3)
            act_turn(act, 0)
            program(act, act_part)
            act_finish(act, B - 1)

        @block.gpsimd
        def _(pool):
            nc.gpsimd.memset(pblk[:], 0.0).then_inc(pblk_zero, 1)
            nc.gpsimd.memset(mhalf[:], -0.5).then_inc(mhalf_ready, 1)
            pool.wait_ge(mhalf_ready, 1)
            pool.wait_ge(hi_made, 2)
            nc.gpsimd.tensor_tensor(WO[1][:], qs[:].rearrange("p a n -> p (a n)").rearrange("p (k n) -> p k n", k=NP_),
                                    WO[0][:].bitcast(F32), ALU.subtract).then_inc(pool_lo_made, 1)
            nc.gpsimd.tensor_tensor(WV[1][:], va_k, WV[0][:].bitcast(F32),
                                    ALU.subtract).then_inc(pool_lo_made, 1)
            pool.wait_ge(pool_lo_made, 2)
            nc.gpsimd.memset(va[:, :, :, P:PW].rearrange("p j q c -> p (j q) c"), 1.0).then_inc(ones_ready, 1)
            pool_load(pool, 0)
            pool_norm(pool, 0)
            pool.wait_ge(consts_loaded, 16 * 5)
            program(pool, pool_part)
            pool_low(pool, B - 1)

        @block.vector
        def _(dve):
            nc.vector.memset(epsb[:], LIN_EPS)
            nc.vector.memset(hm[:], 0.0).then_inc(zeros_ready, 1)
            dve.wait_ge(zeros_ready, 1)
            for i in range(2):
                for c in range(0, P, CT):
                    last = nc.vector.tensor_copy(KV[i][:, :, c:c + CT], hm[:])
            last.then_inc(zeros_ready, 1)
            dve.wait_ge(zeros_ready, 2)
            for g in range(2):
                for a in range(2):
                    r = 2 * g + a
                    nc.vector.memset(hm[64 * a:64 * a + 64, 4 * g:4 * g + 4, r:r + CT // 2 + 1:CT // 2], 1.0)
            dve.wait_ge(consts_loaded, 16 * 5)
            nc.vector.tensor_copy(lowm[:], qf[:, 6, 0:1])
            nc.vector.tensor_copy(SEL[:].rearrange("p q c -> p (q c)"), qf[:, 4:6, :].rearrange("p a n -> p (a n)")
                                  ).then_inc(zeros_ready, 1)
            dve.wait_ge(zeros_ready, 3)
            for i, w in enumerate((WQ, WK)):
                for kt in range(KT):
                    dve.wait_ge(hi_made, 2 + 2 * i + kt + 1)
                    last = nc.vector.tensor_tensor(w[1][:, kt, :].rearrange("p (b n) -> p b n", b=2),
                                                   ps[:, 4 + 2 * kt:6 + 2 * kt, :],
                                                   w[0][:, kt, :].rearrange("p (b n) -> p b n", b=2).bitcast(F32),
                                                   ALU.subtract)
                last.then_inc(lo_made, 1)
            dve_stats(dve, 0)
            dve_xn(dve, 0)
            dve_r1(dve, 0)
            dve_turn(dve, 0)
            program(dve, dve_part)
            dve_finish(dve, B - 1)


def experts(nc, g2, gate, w1, w2, w3, ident_d, z_d, r1_d, out):
    def tiles(ap):
        return ap.rearrange("b (j p) d -> b p j d", p=P)

    z_v, r1_v, out_v = map(tiles, (z_d, r1_d, out))

    with ExitStack() as ctx:
        def sb(name, shape, dt=F32):
            return ctx.enter_context(nc.sbuf_tensor(name, shape, dt))

        def sem(name):
            return ctx.enter_context(nc.semaphore(name))

        ident = sb("ident3", [P, P])
        g2c = sb("g2c", [P, KT])
        mhalf = sb("mhalf3", [P, NJ])
        graw = sb("graw", [P, KT, NE])
        W1, W3 = ([sb(f"{n}{i}", [P, NE, KT, HID], F32R) for i in range(2)] for n in ("W1_", "W3_"))
        W2 = [sb(f"W2_{i}", [P, NE, NM, D], F32R) for i in range(2)]
        G = [sb(f"G{i}", [P, KT, NE], F32R) for i in range(2)]

        WC, NST = KT * HID, 3
        staged = sb("staged", [P, NST, WC])
        work = sb("work", [P, 5 * 1024])
        r1 = work[:, 0:1024].rearrange("p (j d) -> p j d", j=NJ)
        xf = work[:, 1024:2048].rearrange("p (j d) -> p j d", j=NJ)
        acc = work[:, 2048:3072].rearrange("p (j d) -> p j d", j=NJ)
        sl = work[:, 3072:4096].rearrange("p (i n) -> p i n", i=2)
        h32 = work[:, 4096:5120].rearrange("p (i n) -> p i n", i=2)
        st = sb("st3", [P, NJ, 6])
        pad = sb("pad3", [P, 1])
        mv = sb("mv3", [P, NJ, 2])
        ms = sb("ms", [P, NJ])
        inv = sb("inv3", [P, NJ])
        xfT = [sb(f"xfT{i}", [P, KT, S], F32R) for i in range(2)]
        NHR = 3
        hT = [sb(f"hT{i}", [P, NHR, S], F32R) for i in range(2)]
        lg = sb("lg", [P, NJ, NE])
        lmax = sb("lmax", [P, NJ])
        le = sb("le", [P, NJ, NE])
        lsum = sb("lsum", [P, NJ])
        pr = sb("pr", [P, NJ, NE])
        over = sb("over", [P, NJ, NE, NE])
        rank = sb("rank", [P, NJ, NE])
        comb = sb("comb", [P, NJ, NE])

        ps = ctx.enter_context(nc.psum_tensor("ps3", [P, 8, 512], F32))
        YB = 4

        consts_loaded = sem("consts3_loaded")
        w_loaded = [sem(f"w3_loaded{i}") for i in range(NST)]
        hi_steps = Steps(sem("w3_hi"), 3 * NE)
        w_split = sem("w3_split")
        gate_steps0 = Steps(sem("gate_prep"), 2)
        zeros_ready = sem("zeros3_ready")
        r1_loaded = sem("r1_loaded")
        z_loaded = sem("z_loaded")
        n_steps = Steps(sem("norm3_step"), 3)
        ms_ready = sem("ms_ready")
        roots_ready = sem("roots3_ready")
        xf_ready = sem("xf_ready")
        acc_ready = sem("acc_ready")
        xt_psum = sem("xt_psum")
        xt_hi = sem("xt_hi")
        xt_lo = sem("xt_lo")
        gate_psum = sem("gate_psum")
        gate_steps = Steps(sem("gate_step"), 10)
        lmax_ready = sem("lmax_ready")
        le_ready = sem("le_ready")
        ab_psum = sem("ab_psum")
        silu_done = sem("silu_done")
        h_ready = sem("h_ready")
        h_hi = sem("h_hi")
        h_lo = sem("h_lo")
        y_psum = sem("y3_psum")
        y_used = sem("y3_used")
        y_evac = sem("y3_evac")
        out_stored = sem("out_stored")

        NH_ = NE * NM


        def pe_turn(pe, n):
            if not first(n):
                pe.wait_ge(h_ready, NH_ * n)
            pe.wait_ge(xf_ready, NJ * (n + 1))
            for kt in range(KT):
                for j in range(NJ):
                    last = nc.tensor.transpose(ps[:, kt, j * P:(j + 1) * P], xf[:, j, kt * P:(kt + 1) * P], ident[:])
                last.then_inc(xt_psum, 1)

        def pe_gate(pe, n):
            pe.wait_ge(xt_lo, KT * (n + 1))
            for j in range(NJ):
                for kt in range(KT):
                    l = [xfT[i][:, kt, j * P:(j + 1) * P] for i in range(2)]
                    last = mm3(nc, ps[:, 2, j * NE:(j + 1) * NE], *l, G[0][:, kt, :], G[1][:, kt, :],
                               kt == 0, kt == KT - 1)
            last.then_inc(gate_psum, 1)

        def pe_part(pe, b, n):
            def hidden(i):
                e, m = divmod(i, NM)
                if first(b) and m == 0:
                    pe.wait_ge(w_split, 3 * (e + 1))
                if i == 0:
                    pe.wait_ge(gate_steps.sem, gate_steps.per * b + 1)
                elif i == 1:
                    pass
                else:
                    pe.wait_ge(h_ready, NH_ * b + i - 1)
                for w, bank in ((W1, 2 * (i % 2)), (W3, 2 * (i % 2) + 1)):
                    for kt in range(KT):
                        l = [w[h][:, e, kt, m * P:(m + 1) * P] for h in range(2)]
                        last = mm3(nc, ps[:, bank, :], *l, xfT[0][:, kt, :], xfT[1][:, kt, :], kt == 0, kt == KT - 1)
                last.then_inc(ab_psum, 1)

            def down(i):
                e, m = divmod(i, NM)
                pe.wait_ge(h_lo, NH_ * b + i + 1)
                if m == 0 and not (first(b) and e == 0):
                    pe.wait_ge(y_evac, NE * b + e)
                for j in range(NJ):
                    l = [hT[h][:, i % NHR, j * P:(j + 1) * P] for h in range(2)]
                    last = mm3(nc, ps[:, YB + j, 0:D], *l, W2[0][:, e, m, :], W2[1][:, e, m, :], m == 0, m == NM - 1)
                last.then_inc(y_used, 1)

            for i in range(NH_):
                hidden(i)
                if i >= 2:
                    down(i - 2)
            if n is not None:
                pe_turn(pe, n)
            down(NH_ - 2)
            down(NH_ - 1)
            if n is not None:
                pe_gate(pe, n)

        def act_turn(act, n):
            for kt in range(KT):
                act.wait_ge(xt_psum, KT * n + kt + 1)
                nc.scalar.copy(xfT[0][:, kt, :], ps[:, kt, :]).then_inc(xt_hi, 1)

        def act_gate(act, n):
            act.wait_ge(lmax_ready, n + 1)
            nc.scalar.activation(le[:], lg[:], ACT.Exp).then_inc(le_ready, 1)

        def act_part(act, b, n):
            for i in range(NH_ + 1):
                if i < NH_:
                    act.wait_ge(ab_psum, NH_ * b + i + 1)
                    if i >= 2:
                        act.wait_ge(h_ready, NH_ * b + i - 1)
                    elif not first(b):
                        act.wait_ge(h_ready, NH_ * b)
                    nc.scalar.activation(sl[:, i % 2, :], ps[:, 2 * (i % 2), :], ACT.Silu).then_inc(silu_done, 1)
                if i:
                    k = i - 1
                    act.wait_ge(h_ready, NH_ * b + k + 1)
                    if k >= NHR:
                        act.wait_ge(y_used, NH_ * b + k - NHR + 1)
                    elif not first(b):
                        act.wait_ge(y_used, NH_ * b - NHR + k + 1)
                    nc.scalar.copy(hT[0][:, k % NHR, :], h32[:, k % 2, :]).then_inc(h_hi, 1)
            if n is not None:
                act_turn(act, n)
                act_gate(act, n)

        def dve_norm(dve, n):
            n_steps.start(n)
            dve.wait_ge(r1_loaded, 16 * (n + 1))
            for j in range(NJ):
                last = nc.vector.bn_stats(st[:, j, :], r1[:, j, :])
            n_steps.link(dve, last)
            nc.vector.memset(pad[:], 0.0)
            for j in range(NJ):
                last = nc.vector.bn_aggr(mv[:, j, :], st[:, j, :])
            n_steps.link(dve, last)
            mean, var = (mv[:, :, i:i + 1].rearrange("p j o -> p (j o)") for i in range(2))
            n_steps.link(dve, nc.vector.tensor_tensor(ms[:], mean, mean, ALU.mult))
            nc.vector.scalar_tensor_tensor(out=ms[:], in0=ms[:], scalar=RMS_EPS, in1=var,
                                           op0=ALU.add, op1=ALU.add).then_inc(ms_ready, 1)
            n_steps.end()
            dve.wait_ge(roots_ready, n + 1)
            if not first(n):
                dve.wait_ge(xt_psum, KT * n)
            for j in range(NJ):
                nc.vector.tensor_scalar(xf[:, j, :], r1[:, j, :], inv[:, j:j + 1], None, ALU.mult).then_inc(xf_ready, 1)

        def dve_turn(dve, n):
            for kt in range(KT):
                dve.wait_ge(xt_hi, KT * n + kt + 1)
                nc.vector.tensor_tensor(xfT[1][:, kt, :], ps[:, kt, :], xfT[0][:, kt, :].bitcast(F32),
                                        ALU.subtract).then_inc(xt_lo, 1)

        def dve_gate(dve, n):
            def wide(ap):
                return ap.unsqueeze(2).broadcast_to([P, NJ, NE])

            s = gate_steps
            s.start(n)
            dve.wait_ge(gate_psum, n + 1)
            s.link(dve, nc.vector.tensor_copy(lg[:], ps[:, 2, 0:NJ * NE].rearrange("p (j e) -> p j e", e=NE)))
            s.link(dve, nc.vector.tensor_reduce(lmax[:], lg[:], AX, ALU.max))
            nc.vector.tensor_tensor(lg[:], lg[:], wide(lmax[:]), ALU.subtract).then_inc(lmax_ready, 1)
            dve.wait_ge(le_ready, n + 1)
            s.link(dve, nc.vector.reduce_sum(lsum[:], le[:], AX))
            s.link(dve, nc.vector.reciprocal(lsum[:], lsum[:]))
            s.link(dve, nc.vector.tensor_tensor(pr[:], le[:], wide(lsum[:]), ALU.mult))
            for r in range(NE):
                if r:
                    last = nc.vector.tensor_tensor(over[:, :, 0:r, r], pr[:, :, r:r + 1].broadcast_to([P, NJ, r]),
                                                   pr[:, :, 0:r], ALU.is_gt)
                if r < NE - 1:
                    k = NE - 1 - r
                    last = nc.vector.tensor_tensor(over[:, :, r + 1:NE, r], pr[:, :, r:r + 1].broadcast_to([P, NJ, k]),
                                                   pr[:, :, r + 1:NE], ALU.is_ge)
            s.link(dve, last)
            s.link(dve, nc.vector.reduce_sum(rank[:], over[:], AX))
            s.link(dve, nc.vector.scalar_tensor_tensor(out=comb[:], in0=rank[:], scalar=1.5, in1=pr[:],
                                                       op0=ALU.is_lt, op1=ALU.mult))
            s.link(dve, nc.vector.reduce_sum(lsum[:], comb[:], AX))
            s.link(dve, nc.vector.reciprocal(lsum[:], lsum[:]))
            nc.vector.tensor_tensor(comb[:], comb[:], wide(lsum[:]), ALU.mult).then_inc(comb_ready, 1)
            s.end()

        comb_ready = sem("comb_ready")

        def dve_part(dve, b, n):
            def weigh(e):
                if e == 0:
                    dve.wait_ge(comb_ready, b + 1)
                    dve.wait_ge(acc_ready, b + 1)
                else:
                    dve.wait_ge(y_evac, NE * b + e)
                dve.wait_ge(y_used, NH_ * b + NM * (e + 1))
                for j in range(NJ):
                    last = nc.vector.scalar_tensor_tensor(out=acc[:, j, :], in0=ps[:, YB + j, 0:D], scalar=comb[:, j, e:e + 1],
                                                          in1=acc[:, j, :], op0=ALU.mult, op1=ALU.add)
                last.then_inc(y_evac, 1)

            for i in range(NH_):
                dve.wait_ge(silu_done, NH_ * b + i + 1)
                if i >= 2:
                    dve.wait_ge(h_lo, NH_ * b + i - 1)
                elif not first(b):
                    dve.wait_ge(h_lo, NH_ * b - 1 + i)
                nc.vector.tensor_tensor(h32[:, i % 2, :], sl[:, i % 2, :], ps[:, 2 * (i % 2) + 1, :],
                                        ALU.mult).then_inc(h_ready, 1)
                if i % NM == 1 and i > NM:
                    weigh(i // NM - 1)
                if first(b) and i % 2 == 0 and i < NH_ - NM:
                    dve_split(dve, 3 + i // 2)
                if i == 12 and n is not None:
                    dve_norm(dve, n)
            if n is not None:
                dve_turn(dve, n)
            weigh(NE - 1)
            if n is not None:
                dve_gate(dve, n)

        def pool_norm(pool, n):
            pool.wait_ge(ms_ready, n + 1)
            nc.gpsimd.tensor_tensor(inv[:], ms[:], mhalf[:], ALU.pow).then_inc(roots_ready, 1)

        def pool_part(pool, b, n):
            if n is not None:
                pool_load(pool, n)
            for i in range(NH_):
                pool.wait_ge(h_hi, NH_ * b + i + 1)
                nc.gpsimd.tensor_tensor(hT[1][:, i % NHR, :], h32[:, i % 2, :], hT[0][:, i % NHR, :].bitcast(F32),
                                        ALU.subtract).then_inc(h_lo, 1)
                if i == 11 and n is not None:
                    pool_norm(pool, n)
            if n is not None:
                pool_acc(pool, n)

        def pool_acc(pool, n):
            pool.wait_ge(z_loaded, 16 * (n + 1))
            pool.wait_ge(r1_loaded, 16 * (n + 1))
            nc.gpsimd.tensor_tensor(acc, acc, r1, ALU.add).then_inc(acc_ready, 1)

        def pool_load(pool, n):
            if not first(n):
                pool.wait_ge(acc_ready, n)
                pool.wait_ge(xf_ready, NJ * n)
            pool.dma_start(r1, r1_v[n]).then_inc(r1_loaded, 16)

        def sync_part(sp, b, n):
            sp.wait_ge(y_evac, NE * (b + 1))
            sp.dma_start(out_v[b], acc).then_inc(out_stored, 16)
            sp.wait_ge(out_stored, 16 * (b + 1))
            if n is not None:
                sp.dma_start(acc, z_v[n]).then_inc(z_loaded, 16)

        def program(eng, part):
            part(eng, 0, 1)
            with eng.Fori(1, B - 1) as b:
                part(eng, b, b + 1)
            part(eng, B - 1, None)

        CH = [(e, k) for e in range(NE) for k in range(3)]

        def sync_weights(sp, chunks):
            for i in chunks:
                e, k = CH[i]
                if i >= NST:
                    sp.wait_ge(w_split, i - NST + 1)
                w = (w1, w3, w2)[k]
                sp.dma_start(staged[:, i % NST, :].rearrange("p (k n) -> p k n", n=D if k == 2 else HID),
                             w[e].rearrange("(k p) n -> p k n", p=P)).then_inc(w_loaded[i % NST], 16)

        def dve_split(dve, i):
            e, k = CH[i]
            dve.wait_ge(w_loaded[i % NST], 16 * (i // NST + 1))
            if k < 2:
                w = (W1, W3)[k]
                src = staged[:, i % NST, :].rearrange("p (k n) -> p k n", n=HID)
                for kt in range(KT):
                    last = nc.vector.tensor_scalar(w[0][:, e, kt, :], src[:, kt, :], g2c[:, kt:kt + 1], None, ALU.mult)
                hi_steps.link(dve, last)
                for kt in range(KT):
                    last = nc.vector.scalar_tensor_tensor(out=w[1][:, e, kt, :], in0=src[:, kt, :],
                                                          scalar=g2c[:, kt:kt + 1], in1=w[0][:, e, kt, :].bitcast(F32),
                                                          op0=ALU.mult, op1=ALU.subtract)
            else:
                src = staged[:, i % NST, :].rearrange("p (k n) -> p k n", n=D)
                hi_steps.link(dve, nc.vector.tensor_copy(W2[0][:, e, :, :], src))
                last = nc.vector.tensor_tensor(W2[1][:, e, :, :], src, W2[0][:, e, :, :].bitcast(F32), ALU.subtract)
            last.then_inc(w_split, 1)

        block = ctx.enter_context(nc.Block())

        @block.sync
        def _(sp):
            sp.dma_start(ident[:], ident_d).then_inc(consts_loaded, 16)
            sp.dma_start(g2c[:], g2.rearrange("(k p) -> p k", p=P), allow_slow_non_contiguous=True).then_inc(consts_loaded, 16)
            sp.dma_start(graw[:], gate.rearrange("(k p) e -> p k e", p=P)).then_inc(consts_loaded, 16)
            sp.dma_start(acc, z_v[0]).then_inc(z_loaded, 16)
            sync_weights(sp, range(len(CH)))
            program(sp, sync_part)

        @block.tensor
        def _(pe):
            pe.wait_ge(consts_loaded, 16 * 3)
            pe_turn(pe, 0)
            pe_gate(pe, 0)
            program(pe, pe_part)

        @block.scalar
        def _(act):
            act_turn(act, 0)
            act_gate(act, 0)
            program(act, act_part)

        @block.gpsimd
        def _(pool):
            nc.gpsimd.memset(mhalf[:], -0.5).then_inc(zeros_ready, 1)
            pool.wait_ge(zeros_ready, 1)
            pool_load(pool, 0)
            pool_norm(pool, 0)
            pool_acc(pool, 0)
            program(pool, pool_part)

        @block.vector
        def _(dve):
            nc.vector.memset(over[:], 0.0)
            dve.wait_ge(consts_loaded, 16 * 3)
            for kt in range(KT):
                last = nc.vector.tensor_scalar(G[0][:, kt, :], graw[:, kt, :], g2c[:, kt:kt + 1], None, ALU.mult)
            gate_steps0.link(dve, last)
            for kt in range(KT):
                last = nc.vector.scalar_tensor_tensor(out=G[1][:, kt, :], in0=graw[:, kt, :], scalar=g2c[:, kt:kt + 1],
                                                      in1=G[0][:, kt, :].bitcast(F32), op0=ALU.mult, op1=ALU.subtract)
            gate_steps0.link(dve, last)
            dve_norm(dve, 0)
            for i in range(3):
                dve_split(dve, i)
            dve_turn(dve, 0)
            dve_gate(dve, 0)
            program(dve, dve_part)


_INS = ['L0_attn_x', 'L0_attn_Wq', 'L0_attn_Wk', 'L0_attn_Wv', 'L0_attn_proj', 'L0_attn_Wo', 'L0_attn_bo',
        'L0_ffn_g1', 'L0_ffn_g2', 'L0_ffn_wq', 'L0_ffn_wk', 'L0_ffn_wv', 'L0_ffn_wo', 'L0_ffn_gate',
        'L0_ffn_w1', 'L0_ffn_w2', 'L0_ffn_w3']


def build(nc, t, out):
    qk_d = nc.dram_tensor("qk_scratch", (2, 3 * P, S), F32).ap()
    y2_d = nc.dram_tensor("y2_scratch", (B, S, D), F32).ap()
    z_d = nc.dram_tensor("z_scratch", (B, S, D), F32).ap()
    r1_d = nc.dram_tensor("r1_scratch", (B, S, D), F32).ap()
    softmax_attention(nc, t['L0_attn_x'], t['L0_ffn_g1'], t['L0_ffn_wq'], t['L0_ffn_wk'], t['L0_ffn_wv'],
                      t['L0_ffn_wo'], t['ident'], t['mask'], t['cos'], t['sin'], qk_d, y2_d)
    linear_attention(nc, t['L0_attn_x'], t['L0_attn_Wq'], t['L0_attn_Wk'], t['L0_attn_Wv'], t['L0_attn_proj'],
                     t['L0_attn_Wo'], t['L0_attn_bo'], t['ident'], t['sel'], y2_d, z_d, r1_d)
    experts(nc, t['L0_ffn_g2'], t['L0_ffn_gate'], t['L0_ffn_w1'], t['L0_ffn_w2'], t['L0_ffn_w3'], t['ident'],
            z_d, r1_d, out)


def constants():
    import numpy as np
    q, k = np.arange(P)[:, None], np.arange(P)[None, :]
    sel = np.zeros((P, NP_ * P + 1), dtype=np.float32)
    for p in range(NP_):
        for a in range(2):
            r, c = CT * (p % 4) + 2 * (p // 4) + a, p * P + a * LD
            sel[[r, r + CT // 2], c:c + LD] = 1.0
    sel[np.arange(P) % CT >= CT // 2, NP_ * P] = -1.0
    inv_freq = (np.float32(1.0) / np.float32(10000.0) ** (np.arange(0, HD, 2, dtype=np.float32) / np.float32(HD)))
    angle = (np.arange(S, dtype=np.float32)[:, None] * inv_freq.astype(np.float32)[None, :]).astype(np.float32)
    angle = np.tile(np.concatenate([angle, angle], axis=-1).T, (P // HD, 1))
    return {
        'ident': np.eye(P, dtype=np.float32),
        'sel': sel,
        'mask': np.where(k > q, np.float32(-1e30), np.float32(0.0)).astype(np.float32),
        'cos': np.ascontiguousarray(np.cos(angle), dtype=np.float32),
        'sin': np.ascontiguousarray(np.sin(angle), dtype=np.float32),
    }


def kernel(**inputs):
    import numpy as np
    import concourse.bacc as bacc
    from concourse.bass_utils import run_bass_kernel_spmd

    nc = bacc.Bacc("TRN2", target_bir_lowering=False, num_devices=1)
    arrays = {f"in_{n}": np.ascontiguousarray(inputs[n]) for n in _INS}
    arrays |= {f"in_{n}": a for n, a in constants().items()}
    t = {n[3:]: nc.dram_tensor(n, a.shape, mybir.dt.from_np(a.dtype), kind="ExternalInput").ap()
         for n, a in arrays.items()}
    out = nc.dram_tensor("out", (B, S, D), F32, kind="ExternalOutput").ap()
    build(nc, t, out)
    r = run_bass_kernel_spmd(nc, [arrays], core_ids=[0])
    return r.results[0]["out"]
```

```python
from contextlib import ExitStack

import concourse.bass as bass
from concourse import mybir

F32 = mybir.dt.float32
F32R = mybir.dt.float32r
BF16 = mybir.dt.bfloat16
ALU = mybir.AluOpType
ACT = mybir.ActivationFunctionType
AX = mybir.AxisListType.X

P = 128
B, S, D = 8, 512, 256
NJ = S // P
KT = D // P
LN_EPS = 1e-5
RMS_EPS = 1.1920928955078125e-07
LIN_EPS = 1e-6

NH, NKV, HD = 16, 4, 16
NU = NH // 2
NQ = NH // 4
PARTS_Q = ((0, 0), (16, 1), (48, 0))
PARTS_K = ((0, 0), (16, 0), (48, 1))
SHIFT_ROW = 32
P_OFF = (0, 512, 1024, 896)

LH, LD = 16, 64
INNER = LH * LD
NP_ = LH // 2
PW = 2 * LD + 1
CT = 32

NE, HID = 4, 768
NM = HID // P


class Steps:

    def __init__(self, sem, per):
        self.sem, self.per, self.b, self.k = sem, per, 0, 0

    def start(self, b):
        self.b, self.k = b, 0

    def link(self, eng, ins):
        self.k += 1
        assert self.k <= self.per, "more steps than counted"
        ins.then_inc(self.sem, 1)
        eng.wait_ge(self.sem, self.b * self.per + self.k)

    def end(self):
        assert self.k == self.per, (self.k, self.per)


def first(b):
    return isinstance(b, int) and b == 0


def mm3(nc, out, lh, ll, rh, rl, start, stop):
    nc.tensor.matmul(out, lh, rh, start=start, stop=False)
    nc.tensor.matmul(out, lh, rl, start=False, stop=False)
    return nc.tensor.matmul(out, ll, rh, start=False, stop=stop)


def softmax_attention(nc, x, g1, wq, wk, wv, wo, ident_d, mask_d, cos_d, sin_d, qk_d, y2_d, y2_stored, ident, load_ahead, zero_ahead):
    x_v = x.rearrange("b (j p) d -> b p j d", p=P)
    y2_v = y2_d.rearrange("b (j p) d -> b p j d", p=P)
    qk_v = [d.rearrange("h (T p) t -> p T h t", p=P) for d in qk_d]

    with ExitStack() as ctx:
        def sb(name, shape, dt=F32):
            return ctx.enter_context(nc.sbuf_tensor(name, shape, dt))

        def sem(name):
            return ctx.enter_context(nc.semaphore(name))

        identb = sb("identb", [P, P], BF16)
        maskM = sb("maskM", [P, P], BF16)
        maskE = sb("maskE", [P, P], BF16)
        cos = sb("cos", [P, S])
        sin = sb("sin", [P, S])
        g1c = sb("g1c", [P, KT])
        WQ, WK, WV = 2 * D, 4 * 64, NKV * HD
        wA = [sb(f"wA{i}", [P, KT, WQ + WK + WV], F32R) for i in range(2)]
        wO = [sb(f"wO{i}", [P, KT, D], F32R) for i in range(2)]
        zrow = sb("zrow", [2, 1, S])

        x_sb = sb("x_sb", [P, NJ, D])
        st = sb("st", [P, NJ, 6])
        mv = sb("mv", [P, NJ, 2])
        vin = sb("vin", [P, 2, NJ])
        inv = sb("inv", [P, 2, NJ])
        vt = sb("vt", [P, NJ])
        sc = sb("sc", [P, NJ])
        mhalf = sb("mhalf", [P, 2 * NJ])
        xr = sb("xr", [P, NJ, D])
        xrT = [sb(f"xrT{i}", [P, KT, S], F32R) for i in range(2)]
        rc = sb("rc", [P, 3, S])
        rs = sb("rs", [P, 3, S])
        raw = rc[:, 0:KT, :]
        mask = rs[:, 0, 0:P]
        qk = sb("qk", [P, 2, 3, S], F32R)
        qs = [sb(f"qs{i}", [P, NU, S], F32R) for i in range(2)]
        kp = [sb(f"kp{i}", [P, 2, NKV, S], F32R) for i in range(2)]
        v32 = [sb(f"v32{i}", [P, NJ, NKV, 32]) for i in range(2)]
        vnew = sb("vnew", [P, NJ, NKV, HD])
        negm = sb("negm", [P, NJ, P])
        negT = sb("negT", [NH, S], F32R)
        prob = sb("prob", [P, 2, 4, 1280])
        oT = sb("oT", [P, 2, S])
        rsum = sb("rsum", [P, NJ, 4])
        on2 = sb("on2", [P, NJ, D])
        o2T = [sb(f"o2T{i}", [P, KT, S], F32R) for i in range(2)]
        y2 = sb("y2", [P, NJ, D])
        ones = y2[0:1, 0:2, :].rearrange("p j d -> p (j d)").unsqueeze(1)

        ps = ctx.enter_context(nc.psum_tensor("ps", [P, 8, 512], F32))
        FRONT, MAXB, EXPB, PVB, TAILB = 0, 1, 4, 6, 7

        ident_loaded = sem("ident_loaded")
        consts_loaded = sem("consts_loaded")
        weights_loaded = sem("weights_loaded")
        pool_prep = Steps(sem("pool_prep_step"), 2)
        dve_prep = Steps(sem("dve_prep_step"), 2)
        weights_ready = sem("weights_ready")
        zeros_ready = sem("zeros_ready")
        ones_loaded = [sem(f"ones_loaded{i}") for i in range(2)]
        mask_turned = sem("mask_turned")
        x_loaded = sem("x_loaded")
        stats_ready = sem("stats_ready")
        roots_ready = sem("roots_ready")
        xr_ready = sem("xr_ready")
        ln_steps = Steps(sem("ln_step"), 7)
        front_psum = sem("front_psum")
        front_evac = sem("front_evac")
        front_hi = sem("front_hi")
        parts_ready = sem("parts_ready")
        parts_steps = Steps(sem("parts_step"), 6)
        parts_stored = sem("parts_stored")
        stacked = [sem(f"stacked{i}") for i in range(2)]
        shift_psum = sem("shift_psum")
        shift_evac = sem("shift_evac")
        v_ready = sem("v_ready")
        max_psum = sem("max_psum")
        max_evac = sem("max_evac")
        shift_loaded = sem("shift_loaded")
        exp_psum = sem("exp_psum")
        exp_done = sem("exp_done")
        pv_done = sem("pv_done")
        pv_evac = sem("pv_evac")
        ot_psum = sem("ot_psum")
        ot_recip = sem("ot_recip")
        ot_evac = sem("ot_evac")
        tail_psum = sem("tail_psum")
        tail_hi = sem("tail_hi")
        tail_evac = sem("tail_evac")

        NF, NM_, NX, NT = 9, 6 * NU, 5 * NU, 4
        STACKS = 1 + 2 * 3 + 2 * 3
        MUNITS = [(3, (0,)), (3, (1,)), (2, (0,)), (2, (1,)), (1, (0, 1)), (0, (0, 1))]
        XUNITS = [[(0, 0)], [(0, 1), (0, 3)], [(1, 0)], [(1, 1), (1, 3)], [(0, 2), (1, 2)]]

        T_ORDER = (2, 0, 1)
        STATS_AT, VALUES_AT, EXP_FROM = (0, 1, 3), 5, 8
        LAST_QUAD_AT = (0, 1, 2, 4)
        TAIL_AT = [6, 7, 9, 10, 12, 13, 15, 16]
        PV_PIECES = ((0,), (1,), (2, 3))

        def order(f, m, e, t):
            E = [("exp", u, k) for u in range(NU) for k in range(5)] if e is not None else []
            out, ready = [], []
            rows_at = (9, 10) if e is not None else (6, 7)
            front_at = [rows_at[1] + 2 + (7 * n // 2 if e is not None else 3 * n) + k for n in range(NF) for k in range(2)]

            def quad(n, last=""):
                return [("pv" + last, n, k) for k in range(len(PV_PIECES))] + [("ot" + last, n, 0)]

            def exp():
                if E:
                    _, u, k = E.pop(0)
                    while k == 0 and u % 2 == 0 and any(n <= u // 2 - 2 for _, n, _ in ready):
                        out.append(ready.pop(0))
                    out.append(("exp", u, k))
                    if k == 2 and u and u % 2 == 0:
                        ready.extend(quad(u // 2 - 1))

            for i in range(NM_):
                if f is not None and i in STATS_AT:
                    out.append(("stats", 0, STATS_AT.index(i)))
                if m is not None:
                    out.append(("max", i // 6, i % 6))
                if t is not None and e is not None and i in LAST_QUAD_AT:
                    out.append(quad(NQ - 1, "_last")[LAST_QUAD_AT.index(i)])
                if m is not None and i == VALUES_AT:
                    out.append(("values", 0, 0))
                if t is not None and i in TAIL_AT:
                    out.append(("tail", *divmod(TAIL_AT.index(i), 2)))
                if f is not None and i in rows_at:
                    out.append(("rows", 0, rows_at.index(i)))
                if i >= (EXP_FROM if m is not None else 3):
                    exp()
                if f is not None and i in front_at:
                    out.append(("front", *divmod(front_at.index(i), 2)))
                elif ready:
                    out.append(ready.pop(0))
                if len(ready) > 3:
                    out.append(ready.pop(0))
            while E:
                exp()
                if ready:
                    out.append(ready.pop(0))
            out += ready
            if m is not None:
                out.append(("shift", 0, 0))
            elif e is not None:
                out += quad(NQ - 1)
            return out

        def quad_batch(what, e, t, par):
            return (t, par) if what.endswith("_last") else (e, 1 - par)

        def front_bank(e, n):
            return ps[:, FRONT if e is not None or n % 2 == 0 else EXPB, :]

        def exp_banks(m):
            return (EXPB, EXPB + 1) if m is not None else (EXPB, EXPB + 1, MAXB, MAXB + 1, MAXB + 2)

        def sync_part(sp, f, m, e, t, par):
            if f is not None and e is None:
                sp.wait_ge(zeros_ready, 2 - par)
                for a in range(2):
                    r = 64 * a + SHIFT_ROW
                    sp.dma_start(kp[1 - par][r:r + 1, a, :, :].bitcast(F32), ones.broadcast_to([1, NKV, S])).then_inc(ones_loaded[1 - par], 16)
            if f is not None:
                for i, T in enumerate(T_ORDER):
                    sp.wait_ge(parts_ready, 3 * f + 1 + i)
                    sp.dma_start(qk_v[1 - par][:, T, :, :], qk[:, :, T, :].bitcast(F32)).then_inc(parts_stored, 16)
                    if i == 1:
                        load_stacks(sp, f, e, par, 0)
            if t is not None:
                sp.wait_ge(tail_evac, NT * t + NT)
                sp.dma_start(y2_v[t], y2[:]).then_inc(y2_stored, 16)
            if m is not None:
                sp.wait_ge(shift_evac, m + 1)
                for a in range(2):
                    r = 64 * a + SHIFT_ROW
                    sp.dma_start(qs[par][r:r + 1, :, :].bitcast(F32),
                                 negT[NU * a:NU * a + NU, :].bitcast(F32)).then_inc(shift_loaded, 16)
            if f is not None:
                load_stacks(sp, f, e, par, 1)

        def load_stacks(sp, f, e, par, half):
            q, k = qs[1 - par][:].bitcast(F32), kp[1 - par][:].bitcast(F32)
            us, gs = slice(4 * half, 4 * half + 4), slice(2 * half, 2 * half + 2)
            if e is not None:
                sp.wait_ge(exp_psum, NX * e + NX // 2 * (half + 1))
            sp.dma_start(q[SHIFT_ROW:SHIFT_ROW + 65:64, us, :],
                         zrow[:].broadcast_to([2, NU // 2, S])).then_inc(stacked[half], 16)
            sp.wait_ge(parts_stored, 16 * (3 * f + 2 + half))
            for a in range(2):
                for r, h in PARTS_Q:
                    src = qk_d[1 - par][h, 0:NH * HD, :].rearrange("(u a c) t -> a c u t", a=2, c=HD)
                    sp.dma_start(q[64 * a + r:64 * a + r + HD, us, :], src[a][:, us, :]).then_inc(stacked[half], 16)
                for r, h in PARTS_K:
                    src = qk_d[1 - par][h, NH * HD:(NH + NKV) * HD, :].rearrange("(g c) t -> c g t", c=HD)
                    sp.dma_start(k[64 * a + r:64 * a + r + HD, a, gs, :], src[:, gs, :]).then_inc(stacked[half], 16)

        def pe_part(pe, f, m, e, t, par):
            for what, n, k in order(f, m, e, t):
                if what == "front":
                    bank = front_bank(e, n)
                    if k:
                        pass
                    elif n and e is None:
                        if n > 1:
                            pe.wait_ge(front_evac, NF * f + (KT if n == KT else n - 1))
                        if n == KT and first(f):
                            pe.wait_ge(weights_ready, 2)
                    elif n:
                        pe.wait_ge(front_evac, NF * f + n)
                    elif m is not None:
                        if not first(m):
                            pe.wait_ge(shift_evac, m)
                        pe.wait_ge(front_evac, NF * f)
                    if n < KT:
                        pe.wait_ge(xr_ready, NJ * f + NJ)
                        for j in (2 * k, 2 * k + 1):
                            last = nc.tensor.transpose(bank[:, j * P:(j + 1) * P], xr[:, j, n * P:(n + 1) * P], ident[:])
                    elif n < 8:
                        T, rot = T_ORDER[(n - 2) // 2], n % 2
                        c = T * P + rot * D if T < 2 else WQ + rot * P
                        w = [wA[i][:, k, c:c + P] for i in range(2)]
                        last = mm3(nc, bank, w[0], w[1], xrT[0][:, k, :], xrT[1][:, k, :], k == 0, k == KT - 1)
                    else:
                        for j in (2 * k, 2 * k + 1):
                            for kt in range(KT):
                                l = [xrT[i][:, kt, j * P:(j + 1) * P] for i in range(2)]
                                w = [wA[i][:, kt, WQ + WK:] for i in range(2)]
                                last = mm3(nc, bank[:, j * WV:(j + 1) * WV], l[0], l[1], w[0], w[1],
                                           kt == 0, kt == KT - 1)
                    if k:
                        last.then_inc(front_psum, 1)
                elif what == "max":
                    j, heads = MUNITS[k]
                    i = 6 * n + k
                    if i == 0 and isinstance(m, int) and m < 2:
                        pe.wait_ge(ones_loaded[par], 32)
                    if i % (6 * NU // 2) == 0:
                        pe.wait_ge(stacked[i // (6 * NU // 2)], 16 * STACKS * (m + 1))
                    if not (first(m) and i < 3):
                        pe.wait_ge(max_evac, NM_ * m + i - 2)
                    for x, a in enumerate(heads):
                        w = (j + 1) * P
                        o = ps[:, MAXB + i % 3, x * w:(x + 1) * w]
                        nc.tensor.matmul(o, qs[par][:, n, j * P:(j + 1) * P], kp[par][:, a, n // 2, 0:w],
                                         start=True, stop=False)
                        last = nc.tensor.matmul(o[:, w - P:w], identb[:], maskM[:], start=False, stop=True)
                    last.then_inc(max_psum, 1)
                elif what == "shift":
                    pe.wait_ge(front_evac, NF * ((f if f is not None else B - 1) + 1))
                    if not first(m):
                        pe.wait_ge(shift_evac, m)
                    pe.wait_ge(max_evac, NM_ * (m + 1))
                    for j in range(NJ):
                        last = nc.tensor.transpose(ps[:, FRONT, j * P:(j + 1) * P], negm[:, j, :], ident[:])
                    last.then_inc(shift_psum, 1)
                elif what == "exp":
                    i = 5 * n + k
                    if i == 0:
                        pe.wait_ge(shift_loaded, 32 * (e + 1))
                    banks = exp_banks(m)
                    if not (first(e) and i < 2):
                        pe.wait_ge(exp_done, NX * e + max(i + 1 - len(banks), 0))
                    at = 0
                    for a, kt in XUNITS[k]:
                        w = S - kt * P
                        o = ps[:, banks[i % len(banks)], at:at + w]
                        nc.tensor.matmul(o, kp[1 - par][:, a, n // 2, kt * P:(kt + 1) * P], qs[1 - par][:, n, kt * P:],
                                         start=True, stop=False)
                        last = nc.tensor.matmul(o[:, 0:P], identb[:], maskE[:], start=False, stop=True)
                        at += w
                    last.then_inc(exp_psum, 1)
                elif what in ("pv", "pv_last"):
                    b, vp = quad_batch(what, e, t, par)
                    if k == 0:
                        pe.wait_ge(exp_done, NX * b + 10 * (n + 1))
                        if n == 0:
                            pe.wait_ge(v_ready, b + 1)
                        if not (first(b) and n == 0):
                            pe.wait_ge(pv_evac, NQ * b + n)
                    for i in PV_PIECES[k]:
                        w = S - i * P
                        for s in range(4):
                            last = nc.tensor.matmul(ps[32 * s:32 * s + 32, PVB, i * P:], v32[vp][:, i, n, :],
                                                    prob[:, n % 2, s, P_OFF[i]:P_OFF[i] + w],
                                                    start=(i == 0), stop=(i == NJ - 1),
                                                    tile_position=(0, 32 * s))
                    if k == len(PV_PIECES) - 1:
                        last.then_inc(pv_done, 1)
                elif what in ("ot", "ot_last"):
                    b, _ = quad_batch(what, e, t, par)
                    pe.wait_ge(pv_evac, NQ * b + n + 1)
                    if n == 0 and t is not None:
                        pe.wait_ge(tail_evac, NT * (t + 1))
                    if n:
                        pe.wait_ge(ot_evac, NQ * b + n)
                    for j in range(NJ):
                        last = nc.tensor.transpose(ps[:, TAILB, j * P:(j + 1) * P], oT[:, n % 2, j * P:(j + 1) * P], ident[:])
                    last.then_inc(ot_psum, 1)
                elif what == "tail":
                    if k:
                        pass
                    elif n == 0:
                        pe.wait_ge(ot_evac, NQ * (t + 1))
                    else:
                        pe.wait_ge(tail_evac, NT * t + n)
                    if n < KT:
                        for j in (2 * k, 2 * k + 1):
                            last = nc.tensor.transpose(ps[:, TAILB, j * P:(j + 1) * P], on2[:, j, n * P:(n + 1) * P], ident[:])
                    else:
                        j = 2 * (n - KT) + k
                        for kt in range(KT):
                            l = [o2T[h][:, kt, j * P:(j + 1) * P] for h in range(2)]
                            last = mm3(nc, ps[:, TAILB, k * D:(k + 1) * D], l[0], l[1],
                                       wO[0][:, kt, :], wO[1][:, kt, :], kt == 0, kt == KT - 1)
                    if k:
                        last.then_inc(tail_psum, 1)

        def act_part(act, f, m, e, t, par):
            for what, n, k in order(f, m, e, t):
                if what == "front" and n < KT and k:
                    act.wait_ge(front_psum, NF * f + n + 1)
                    nc.scalar.copy(xrT[0][:, n, :], front_bank(e, n)).then_inc(front_hi, 1)
                elif what == "exp":
                    i = 5 * n + k
                    act.wait_ge(exp_psum, NX * e + i + 1)
                    q = n // 2
                    if n % 2 == 0 and k == 0 and not (first(e) and q < 2):
                        act.wait_ge(pv_done, NQ * e + q - 1)
                    s, banks = 2 * (n % 2), exp_banks(m)
                    bank = ps[:, banks[i % len(banks)], :]
                    if k < 4:
                        h, kt = XUNITS[k][0]
                        o, w = prob[:, q % 2, s + h, P_OFF[kt]:P_OFF[kt] + 512], bank
                    else:
                        o = prob[:, q % 2, s:s + 2, P_OFF[2]:P_OFF[2] + 256]
                        w = bank.rearrange("p (a q) -> p a q", a=2)
                    nc.scalar.activation(o, w, ACT.Exp, scale=HD ** -0.5).then_inc(exp_done, 1)
                elif what in ("pv", "pv_last") and k == len(PV_PIECES) - 1:
                    b, _ = quad_batch(what, e, t, par)
                    act.wait_ge(pv_done, NQ * b + n + 1)
                    if not (first(b) and n < 2):
                        act.wait_ge(ot_psum, NQ * b + n - 1)
                    nc.scalar.copy(oT[:, n % 2, :], ps[:, PVB, :]).then_inc(pv_evac, 1)
                elif what == "tail" and n < KT and k:
                    act.wait_ge(tail_psum, NT * t + n + 1)
                    nc.scalar.copy(o2T[0][:, n, :], ps[:, TAILB, :]).then_inc(tail_hi, 1)

        def dve_part(dve, f, m, e, t, par):
            for what, n, k in order(f, m, e, t):
                bank = front_bank(e, n)
                if what == "values":
                    if first(m):
                        dve.wait_ge(zeros_ready, 1)
                    if not (isinstance(m, int) and m < 2):
                        dve.wait_ge(pv_done, NQ * (m - 1))
                    dve.wait_ge(front_evac, NF * (m + 1))
                    nc.vector.tensor_copy(v32[par][:, :, :, 0:HD], vnew[:]).then_inc(v_ready, 1)
                elif what == "stats" and k < 2:
                    if k == 0:
                        ln_steps.start(f)
                        dve.wait_ge(x_loaded, 16 * (f + 1))
                    for j in (2 * k, 2 * k + 1):
                        last = nc.vector.bn_stats(st[:, j, :], x_sb[:, j, :])
                    ln_steps.link(dve, last)
                    nc.vector.memset(sc[:, 0:1], 0.0)
                elif what == "stats":
                    for j in range(NJ - 1):
                        nc.vector.bn_aggr(mv[:, j, :], st[:, j, :])
                    ln_steps.link(dve, nc.vector.bn_aggr(mv[:, NJ - 1, :], st[:, NJ - 1, :]))
                    var = mv[:, :, 1:2].rearrange("p j o -> p (j o)")
                    ln_steps.link(dve, nc.vector.tensor_scalar(vin[:, 0, :], var, LN_EPS, None, ALU.add))
                    ln_steps.link(dve, nc.vector.reciprocal(vt[:], vin[:, 0, :]))
                    ln_steps.link(dve, nc.vector.tensor_tensor(vt[:], vt[:], var, ALU.mult))
                    nc.vector.tensor_scalar(vin[:, 1, :], vt[:], RMS_EPS, None, ALU.add).then_inc(stats_ready, 1)
                elif what == "rows":
                    if k == 0:
                        dve.wait_ge(roots_ready, f + 1)
                        ln_steps.link(dve, nc.vector.tensor_tensor(sc[:], inv[:, 0, :], inv[:, 1, :], ALU.mult))
                        ln_steps.end()
                    for j in (2 * k, 2 * k + 1):
                        nc.vector.tensor_scalar(xr[:, j, :], x_sb[:, j, :], mv[:, j, 0:1], sc[:, j:j + 1],
                                                ALU.subtract, ALU.mult).then_inc(xr_ready, 1)
                    if first(f) and k:
                        prepare_weights(dve)
                elif what == "front" and k:
                    if n < KT:
                        dve.wait_ge(front_hi, KT * f + n + 1)
                        nc.vector.tensor_tensor(xrT[1][:, n, :], bank, xrT[0][:, n, :].bitcast(F32),
                                                ALU.subtract).then_inc(front_evac, 1)
                    elif n < 8:
                        T, rot = T_ORDER[(n - 2) // 2], n % 2
                        dve.wait_ge(front_psum, NF * f + n + 1)
                        if n == KT and not first(f):
                            dve.wait_ge(parts_ready, 3 * f)
                        nc.vector.tensor_tensor((rs if rot else rc)[:, T, :], bank, (sin if rot else cos)[:],
                                                ALU.mult).then_inc(front_evac, 1)
                    else:
                        dve.wait_ge(front_psum, NF * f + n + 1)
                        nc.vector.tensor_copy(vnew[:], bank[:, 0:NJ * WV].rearrange("p (j g c) -> p j g c", j=NJ, c=HD)
                                              ).then_inc(front_evac, 1)
                elif what == "max":
                    j, heads = MUNITS[k]
                    i = 6 * n + k
                    dve.wait_ge(max_psum, NM_ * m + i + 1)
                    w = (j + 1) * P
                    src = ps[:, MAXB + i % 3, 0:w * len(heads)].rearrange("p (a k) -> p a k", k=w)
                    if len(heads) == 2:
                        dst = negm[:, j, n:n + NU + 1:NU]
                    else:
                        dst = negm[:, j, heads[0] * NU + n:heads[0] * NU + n + 1]
                    nc.vector.tensor_reduce(dst, src, AX, ALU.max, negate=True).then_inc(max_evac, 1)
                elif what == "shift":
                    dve.wait_ge(shift_psum, m + 1)
                    if not first(m):
                        dve.wait_ge(shift_loaded, 32 * m)
                    nc.vector.tensor_copy(negT[:], ps[0:NH, FRONT, :]).then_inc(shift_evac, 1)
                elif what in ("ot", "ot_last"):
                    b, _ = quad_batch(what, e, t, par)
                    dve.wait_ge(ot_psum, NQ * b + n + 1)
                    o = ps[:, TAILB, :].rearrange("p (j s c) -> p j s c", j=NJ, s=4)
                    nc.vector.reciprocal(rsum[:], o[:, :, :, HD]).then_inc(ot_recip, 1)
                    dve.wait_ge(ot_recip, NQ * b + n + 1)
                    nc.vector.tensor_tensor(on2[:, :, n * 64:(n + 1) * 64].rearrange("p j (s c) -> p j s c", s=4),
                                            o[:, :, :, 0:HD], rsum[:].unsqueeze(3).broadcast_to([P, NJ, 4, HD]),
                                            ALU.mult).then_inc(ot_evac, 1)
                elif what == "tail" and k:
                    if n < KT:
                        dve.wait_ge(tail_hi, KT * t + n + 1)
                        nc.vector.tensor_tensor(o2T[1][:, n, :], ps[:, TAILB, :], o2T[0][:, n, :].bitcast(F32),
                                                ALU.subtract).then_inc(tail_evac, 1)
                    else:
                        dve.wait_ge(tail_psum, NT * t + n + 1)
                        if n == KT and not first(t):
                            dve.wait_ge(y2_stored, 16 * t)
                        j = 2 * (n - KT)
                        nc.vector.tensor_copy(y2[:, j:j + 2, :],
                                              ps[:, TAILB, :].rearrange("p (j d) -> p j d", j=2)).then_inc(tail_evac, 1)

        def zero_stacks(i):
            nc.gpsimd.memset(qs[i][:].bitcast(F32), 0.0)
            nc.gpsimd.memset(kp[i][:].bitcast(F32), 0.0).then_inc(zeros_ready, 1)

        def prepare_weights(dve):
            dve.wait_ge(ident_loaded, 16 * 2)
            dve.wait_ge(consts_loaded, 16 * 3)
            nc.vector.tensor_copy(identb[:], ident[:])
            nc.vector.tensor_copy(maskM[:], mask)
            dve.wait_ge(mask_turned, 1)
            nc.vector.tensor_copy(maskE[:], ps[:, TAILB, 0:P]).then_inc(weights_ready, 1)
            dve.wait_ge(weights_loaded, 16 * 4)
            for kt in range(KT):
                ins = nc.vector.tensor_scalar(raw[:, kt, 0:D + 2 * WV], raw[:, kt, 0:D + 2 * WV],
                                              g1c[:, kt:kt + 1], None, ALU.mult)
            dve_prep.link(dve, ins)
            hi, lo = wA
            q = raw[:, :, 0:D]

            def halves(ap):
                return ap.rearrange("p k (h c) -> p k h c", c=HD)

            for kt in range(KT):
                qv = raw[:, kt, 0:D].rearrange("p (h c) -> p h c", c=HD)
                kv = raw[:, kt, D:D + WV].rearrange("p (h c) -> p h c", c=HD)
                nc.vector.tensor_copy(hi[:, kt, 0:D], raw[:, kt, 0:D])
                nc.vector.tensor_copy(hi[:, kt, WQ + WK:], raw[:, kt, D + WV:D + 2 * WV])
                for src, at, n in ((qv, D, D), (kv, WQ + P, WV), (kv, WQ + P + WV, WV)):
                    dst = hi[:, kt, at:at + n].rearrange("p (h c) -> p h c", c=HD)
                    nc.vector.tensor_scalar(dst[:, :, 0:8], src[:, :, 8:16], -1.0, None, ALU.mult)
                    nc.vector.tensor_copy(dst[:, :, 8:16], src[:, :, 0:8])
                for at in (WQ, WQ + WV):
                    nc.vector.tensor_copy(hi[:, kt, at:at + WV], raw[:, kt, D:D + WV])
            dve_prep.link(dve, nc.vector.tensor_copy(wO[0][:], on2[:, 0:KT, :]))
            for kt in range(KT):
                h32 = hi[:, kt, :].bitcast(F32)
                qv = raw[:, kt, 0:D].rearrange("p (h c) -> p h c", c=HD)
                kv = raw[:, kt, D:D + WV].rearrange("p (h c) -> p h c", c=HD)
                for src, at, n in ((raw[:, kt, 0:D], 0, D), (raw[:, kt, D:D + WV], WQ, WV),
                                   (raw[:, kt, D:D + WV], WQ + WV, WV), (raw[:, kt, D + WV:D + 2 * WV], WQ + WK, WV)):
                    nc.vector.tensor_tensor(lo[:, kt, at:at + n], src, h32[:, at:at + n], ALU.subtract)
                for src, at, n in ((qv, D, D), (kv, WQ + P, WV), (kv, WQ + P + WV, WV)):
                    dst = lo[:, kt, at:at + n].rearrange("p (h c) -> p h c", c=HD)
                    h = h32[:, at:at + n].rearrange("p (h c) -> p h c", c=HD)
                    nc.vector.scalar_tensor_tensor(out=dst[:, :, 0:8], in0=src[:, :, 8:16], scalar=-1.0, in1=h[:, :, 0:8],
                                                   op0=ALU.mult, op1=ALU.subtract)
                    nc.vector.tensor_tensor(dst[:, :, 8:16], src[:, :, 0:8], h[:, :, 8:16], ALU.subtract)
            nc.vector.tensor_tensor(wO[1][:], on2[:, 0:KT, :], wO[0][:].bitcast(F32), ALU.subtract).then_inc(weights_ready, 1)

        def pool_part(pool, f, m, e, t, par):
            if f is None:
                return
            if not first(f):
                pool.wait_ge(xr_ready, NJ * f)
                pool.dma_start(x_sb[:], x_v[f]).then_inc(x_loaded, 16)
            pool.wait_ge(stats_ready, f + 1)
            nc.gpsimd.tensor_tensor(inv[:].rearrange("p a j -> p (a j)"), vin[:].rearrange("p a j -> p (a j)"),
                                    mhalf[:], ALU.pow).then_inc(roots_ready, 1)
            if first(f):
                nc.gpsimd.memset(ones, 1.0)
                for i in range(2):
                    nc.gpsimd.memset(v32[i][:], 0.0)
                nc.gpsimd.memset(negm[:], 0.0)
                pool_prep.link(pool, nc.gpsimd.memset(zrow[:], 0.0))
                for i in range(2):
                    nc.gpsimd.memset(v32[i][:, :, :, HD:HD + 1], 1.0)
                zero_stacks(0)
                zero_stacks(1)
            parts_steps.start(f)
            for i, T in enumerate(T_ORDER):
                pool.wait_ge(front_evac, NF * f + 2 * i + 4)
                if i == 0 and not first(f):
                    pool.wait_ge(parts_stored, 16 * 3 * f)
                parts_steps.link(pool, nc.gpsimd.tensor_tensor(qk[:, 0, T, :], rc[:, T, :], rs[:, T, :], ALU.add))
                parts_steps.link(pool, nc.gpsimd.tensor_tensor(rc[:, T, :], rc[:, T, :], rs[:, T, :], ALU.add))
                nc.gpsimd.tensor_tensor(qk[:, 1, T, :], rc[:, T, :], qk[:, 0, T, :].bitcast(F32),
                                        ALU.subtract).then_inc(parts_ready, 1)
            parts_steps.end()

        def program(eng, part):
            part(eng, 0, None, None, None, 1)
            part(eng, 1, 0, None, None, 0)
            part(eng, 2, 1, 0, None, 1)
            part(eng, 3, 2, 1, 0, 0)
            with eng.Fori(1, B // 2 - 1) as i:
                m = 2 * i + 1
                part(eng, m + 1, m, m - 1, m - 2, 1)
                part(eng, m + 2, m + 1, m, m - 1, 0)
            part(eng, None, B - 1, B - 2, B - 3, 1)
            part(eng, None, None, B - 1, B - 2, 0)
            part(eng, None, None, None, B - 1, 1)

        block = ctx.enter_context(nc.Block())

        @block.sync
        def _(sp):
            sp.dma_start(ident[:], ident_d).then_inc(ident_loaded, 16)
            sp.dma_start(mask, mask_d).then_inc(ident_loaded, 16)
            sp.dma_start(g1c[:], g1.rearrange("(k p) -> p k", p=P), allow_slow_non_contiguous=True).then_inc(consts_loaded, 16)
            sp.dma_start(raw[:, :, 0:D], wq.rearrange("(k p) n -> p k n", p=P)).then_inc(weights_loaded, 16)
            sp.dma_start(raw[:, :, D:D + WV], wk.rearrange("(k p) n -> p k n", p=P)).then_inc(weights_loaded, 16)
            sp.dma_start(raw[:, :, D + WV:D + 2 * WV], wv.rearrange("(k p) n -> p k n", p=P)).then_inc(weights_loaded, 16)
            sp.dma_start(on2[:, 0:KT, :], wo.rearrange("(k p) n -> p k n", p=P)).then_inc(weights_loaded, 16)
            sp.dma_start(cos[:], cos_d).then_inc(consts_loaded, 16)
            sp.dma_start(sin[:], sin_d).then_inc(consts_loaded, 16)
            load_ahead(sp)
            program(sp, sync_part)

        @block.tensor
        def _(pe):
            pe.wait_ge(ident_loaded, 16 * 2)
            nc.tensor.transpose(ps[:, TAILB, 0:P], mask, ident[:]).then_inc(mask_turned, 1)
            program(pe, pe_part)

        @block.scalar
        def _(act):
            program(act, act_part)

        @block.gpsimd
        def _(pool):
            pool_prep.link(pool, nc.gpsimd.memset(mhalf[:], -0.5))
            pool.dma_start(x_sb[:], x_v[0]).then_inc(x_loaded, 16)
            program(pool, pool_part)

        @block.vector
        def _(dve):
            zero_ahead()
            program(dve, dve_part)


def linear_attention(nc, x, wk, wv, wo, bo, sel_d, y2_d, z_d, r1_d, ident, pblk, qs, ahead_loaded,
                     y2_stored, z_stored, r1_stored):
    def tiles(ap):
        return ap.rearrange("b (j p) d -> b p j d", p=P)

    x_v, y2_v, z_v, r1_v = map(tiles, (x, y2_d, z_d, r1_d))

    with ExitStack() as ctx:
        def sb(name, shape, dt=F32):
            return ctx.enter_context(nc.sbuf_tensor(name, shape, dt))

        def sem(name):
            return ctx.enter_context(nc.semaphore(name))

        bob = sb("bob", [P, D])
        mhalf = sb("mhalf2", [P, NJ])
        WQ, WK, WV = ([sb(f"{n}{i}", [P, KT, INNER], F32R) for i in range(2)] for n in ("WQ", "WK", "WV"))
        WO = [sb(f"WO{i}", [P, NP_, D], F32R) for i in range(2)]

        xn = sb("xn", [P, NJ, D])
        st = sb("st2", [P, NJ, 6])
        pad = sb("pad2", [P, 1])
        mv = sb("mv2", [P, NJ, 2])
        vin = sb("vin2", [P, NJ])
        inv = sb("inv2", [P, NJ])
        xb = sb("xb", [P, NJ, D])
        r1 = sb("r1", [P, NJ, D])
        xnT = [sb(f"xnT{i}", [P, KT, S], F32R) for i in range(2)]
        kf = sb("kf", [P, NJ, INNER])
        va = sb("va", [P, NJ, NP_, PW])
        epsb = sb("epsb", [P, 1])
        hm = sb("hm", [P, NP_, CT])
        SEL = sb("SEL", [P, NP_, P], F32R)
        lowm = sb("lowm", [P, 1])
        KV = [sb(f"KV{i}", [P, NP_, P], F32R) for i in range(2)]
        KW = [sb(f"KW{i}", [P, NP_, D], F32R) for i in range(2)]
        kss = sb("kss", [P, NP_, CT])
        qf = sb("qf", [P, NP_, S])
        rdT = sb("rdT", [P, S], F32R)
        NQR = 4
        kvf = qs[:, 0:2, :].rearrange("p a (q c) -> p (a q) c", c=P)
        rd, rh = qs[:, 3, :], qs[:, 2, :].bitcast(F32R)
        QS = [sb(f"QS{i}", [P, NP_, S], F32R) for i in range(2)]

        ps = ctx.enter_context(nc.psum_tensor("ps2", [P, 8, 512], F32))
        RING, KVB, DENB, DB, YB = 0, 2, 4, 5, 7
        NUM = [(KVB + i // 3, (i % 3) * PW) for i in range(NP_)]

        wk_loaded = sem("wk_loaded")
        wv_loaded = sem("wv_loaded")
        wo_loaded = sem("wo_loaded")
        turned = sem("w_turned")
        turned_copied = sem("w_turned_copied")
        folded = sem("w_folded")
        hi_made = sem("w_hi_made")
        wv_hi_made = sem("wv_hi_made")
        wo_split = sem("wo_split")
        sel_made = sem("sel_made")
        wo_hi_made = sem("wo_hi_made")
        lo_made = sem("w_lo_made")
        pool_lo_made = sem("w_pool_lo_made")
        zeros_ready = sem("zeros2_ready")
        mhalf_ready = sem("mhalf2_ready")
        sel_loaded = sem("sel_loaded")
        bob_loaded = sem("bob_loaded")
        ones_ready = sem("ones2_ready")
        x_loaded = sem("x2_loaded")
        y2_loaded = sem("y2_loaded")
        xb_loaded = sem("xb_loaded")
        stats_ready = sem("stats2_ready")
        roots_ready = sem("roots2_ready")
        ln_steps = Steps(sem("ln2_step"), 2)
        xn_ready = sem("xn_ready")
        r1_ready = sem("r1_ready")
        xb_ready = sem("xb_ready")
        ring_psum = sem("ring_psum")
        t_hi = sem("t_hi")
        ring_evac_dve = sem("ring_evac_dve")
        ring_evac_act = sem("ring_evac_act")
        kv_psum = sem("kv_psum")
        kv_evac = sem("kv_evac")
        kvt_psum = sem("kvt_psum")
        kv_hi = sem("kv_hi")
        kv_lo = sem("kv_lo")
        kss_ready = sem("kss_ready")
        den_psum = sem("den_psum")
        den_evac = sem("den_evac")
        rd_ready = sem("rd_ready")
        rd_hi = sem("rd_hi")
        rdt_ready = sem("rdt_ready")
        spread_psum = sem("spread_psum")
        qs_ready = sem("qs_ready")
        qs_hi = sem("qs_hi")
        qs_lo = sem("qs_lo")
        kw_psum = sem("kw_psum")
        kw_hi = sem("kw_hi")
        kw_lo = sem("kw_lo")
        y_psum = sem("y_psum")
        y_evac = sem("y_evac")

        NR = 16 + NP_ + KT
        NRD, NRA = 8 + NP_ + KT, 8
        SPREAD_AFTER = range(5, 5 + NP_)
        OUT_AFTER = {15: (0, 1)}
        NKW = NP_ // 2

        def ring_free(eng, base, u):
            u -= 2
            if u < 0:
                eng.wait_ge(ring_evac_dve, NRD * base + KT + u + 1)
            elif u < 16 and u % 4 >= 2:
                eng.wait_ge(ring_evac_act, NRA * base + 2 * (u // 4) + u % 4 - 1)
            elif u < 16:
                eng.wait_ge(ring_evac_dve, NRD * base + KT + 2 * (u // 4) + u % 4 + 1)
            else:
                eng.wait_ge(ring_evac_dve, NRD * base + KT + 8 + (u - 16) + 1)

        def pe_turn(pe, n):
            for kt in range(KT):
                if not first(n):
                    ring_free(pe, n - 1, NR - KT + kt)
                if kt == 0:
                    pe.wait_ge(xn_ready, NJ * n + NJ)
                for j in range(NJ):
                    last = nc.tensor.transpose(ps[:, RING + kt, j * P:(j + 1) * P], xn[:, j, kt * P:(kt + 1) * P], ident[:])
                last.then_inc(ring_psum, 1)

        def pe_out(pe, e, j):
            if j == 0:
                pe.wait_ge(qs_lo, NP_ * (e + 1))
                pe.wait_ge(kw_lo, NKW * (e + 1))
            elif j == 2:
                pe.wait_ge(y_evac, 2 * e + 1)
            for p in range(NP_):
                l = [QS[i][:, p, j * P:(j + 1) * P] for i in range(2)]
                last = mm3(nc, ps[:, YB, (j % 2) * D:(j % 2 + 1) * D], *l, KW[0][:, p, :], KW[1][:, p, :],
                           p == 0, p == NP_ - 1)
            last.then_inc(y_psum, 1)

        def pe_spread(pe, e, p):
            if p == 0:
                pe.wait_ge(rdt_ready, e + 1)
            if p < 2:
                pe.wait_ge(kw_lo, NKW * (e + 1) - 1 + p)
            else:
                pe.wait_ge(qs_ready, NP_ * e + p - 1)
            nc.tensor.matmul(ps[:, DB + p % 2, :], SEL[:, p, :], rdT[:], start=True, stop=True).then_inc(spread_psum, 1)

        def pe_part(pe, b, n):
            pe.wait_ge(ring_evac_dve, NRD * b + KT)
            for u in range(16):
                j, w, half = u // 4, (WK, WK, WV, WV)[u % 4], u % 2
                ring_free(pe, b, u)
                for kt in range(KT):
                    l = [xnT[i][:, kt, j * P:(j + 1) * P] for i in range(2)]
                    r = [w[i][:, kt, half * 512:(half + 1) * 512] for i in range(2)]
                    last = mm3(nc, ps[:, RING + u % 2, :], *l, *r, kt == 0, kt == KT - 1)
                last.then_inc(ring_psum, 1)
                if first(b):
                    continue
                if u in SPREAD_AFTER:
                    pe_spread(pe, b - 1, SPREAD_AFTER.index(u))
                for i in OUT_AFTER.get(u, ()):
                    pe_out(pe, b - 1, i)

            def query(p):
                ring_free(pe, b, 16 + p)
                for kt in range(KT):
                    l = [WQ[i][:, kt, p * P:(p + 1) * P] for i in range(2)]
                    last = mm3(nc, ps[:, RING + p % 2, :], *l, xnT[0][:, kt, :], xnT[1][:, kt, :], kt == 0, kt == KT - 1)
                last.then_inc(ring_psum, 1)

            def kw(i):
                if first(b) and i == 0:
                    pe.wait_ge(wo_split, 1)
                    pe.wait_ge(sel_made, 1)
                if i == 0:
                    pe.wait_ge(kv_lo, 2 * (b + 1))
                if i >= 2:
                    pe.wait_ge(kw_lo, NKW * b + i - 1)
                elif not first(b):
                    pe.wait_ge(qs_ready, NP_ * b - 1 + i)
                for a in range(2):
                    p = 2 * i + a
                    last = mm3(nc, ps[:, DB + i % 2, a * D:(a + 1) * D], KV[0][:, p, :], KV[1][:, p, :],
                               WO[0][:, p, :], WO[1][:, p, :], True, True)
                last.then_inc(kw_psum, 1)

            query(0)
            query(1)
            if not first(b):
                pe_out(pe, b - 1, NJ - 2)
                pe_out(pe, b - 1, NJ - 1)
            pe.wait_ge(ring_evac_dve, NRD * b + KT + 8)
            pe.wait_ge(ring_evac_act, NRA * (b + 1))
            for p in range(NP_):
                bank, at = NUM[p]
                for j in range(NJ):
                    last = nc.tensor.matmul(ps[:, bank, at:at + PW], kf[:, j, p * P:(p + 1) * P], va[:, j, p, :],
                                            start=(j == 0), stop=(j == NJ - 1))
            last.then_inc(kv_psum, 1)
            query(2)
            query(3)
            pe.wait_ge(kv_evac, b + 1)
            pe.wait_ge(kss_ready, b + 1)
            for p in range(NP_):
                last = nc.tensor.transpose(ps[:, KVB + p // 4, (p % 4) * P:(p % 4 + 1) * P], kvf[:, p, :], ident[:])
            last.then_inc(kvt_psum, 1)
            for p in range(4, NP_):
                query(p)
            kw(0)
            if n is not None:
                pe_turn(pe, n)
            kw(1)
            pe.wait_ge(ring_evac_dve, NRD * b + KT + 8 + NP_)
            for g in range(2):
                for c in range(4):
                    p = 4 * g + c
                    last = nc.tensor.matmul(ps[CT * c:CT * c + CT, DENB, :], kss[:, p, :], qf[:, p, :],
                                            start=(g == 0), stop=(g == 1), tile_position=(0, CT * c))
            last.then_inc(den_psum, 1)
            for i in range(2, NKW):
                kw(i)

        def pe_finish(pe, e):
            for p in range(NP_):
                pe_spread(pe, e, p)
            for j in range(NJ):
                pe_out(pe, e, j)

        def act_turn(act, n):
            for kt in range(KT):
                act.wait_ge(ring_psum, NR * n + kt + 1)
                nc.scalar.copy(xnT[0][:, kt, :], ps[:, RING + kt, :]).then_inc(t_hi, 1)

        def act_high(act, e, p):
            act.wait_ge(qs_ready, NP_ * e + p + 1)
            nc.scalar.copy(QS[0][:, p, :], qs[:, p % NQR, :]).then_inc(qs_hi, 1)

        HIGH_BEFORE = ((), (), (0,), (1,), (2, 3, 4), (5,), (6, 7), ())

        def act_part(act, b, n):
            if not first(b):
                act.wait_ge(kv_psum, b)
            for j in range(NJ):
                for h in range(2):
                    if not first(b):
                        for p in HIGH_BEFORE[2 * j + h]:
                            act_high(act, b - 1, p)
                    act.wait_ge(ring_psum, NR * b + KT + 4 * j + 2 + h + 1)
                    nc.scalar.copy(va[:, j, 4 * h:4 * h + 4, 0:P],
                                   ps[:, RING + h, :].rearrange("p (q c) -> p q c", c=P)).then_inc(ring_evac_act, 1)
                if j == 0 and not first(b):
                    act_rd(act, b - 1)
            act.wait_ge(kv_psum, b + 1)
            for bank in range(3):
                m = min(3, NP_ - 3 * bank)
                last = nc.scalar.copy(kvf[:, 3 * bank:3 * bank + m, :],
                                      ps[:, KVB + bank, 0:m * PW].rearrange("p (q c) -> p q c", c=PW)[:, :, 0:P])
            last.then_inc(kv_evac, 1)
            act.wait_ge(kvt_psum, b + 1)
            for a in range(2):
                nc.scalar.copy(diagonal(KV[0], a), diagonal(kvt, a)).then_inc(kv_hi, 1)
            for i in range(NKW):
                if i == 1 and n is not None:
                    act_turn(act, n)
                if i == 2:
                    act.wait_ge(den_psum, b + 1)
                    nc.scalar.activation(rd, ps[:, DENB, :], ACT.Identity, bias=epsb[:]).then_inc(den_evac, 1)
                act.wait_ge(kw_psum, NKW * b + i + 1)
                nc.scalar.copy(KW[0][:, 2 * i:2 * i + 2, :], ps[:, DB + i % 2, :].rearrange("p (a d) -> p a d", a=2)
                               ).then_inc(kw_hi, 1)

        def act_finish(act, e):
            act_rd(act, e)
            for p in range(NP_):
                act_high(act, e, p)

        def act_rd(act, e):
            act.wait_ge(rd_ready, e + 1)
            nc.scalar.copy(rh, rd).then_inc(rd_hi, 1)

        wq_raw = qs[:].rearrange("p a n -> p (a n)").rearrange("p (k n) -> p k n", k=KT)
        wo_raw = kf[:, 2:4, :].rearrange("p a n -> p (a n)").rearrange("p (k n) -> p k n", k=NP_)
        va_k = va[:, 0:2, :, :].rearrange("p j q c -> p (j q c)")[:, 0:KT * INNER].rearrange("p (k n) -> p k n", k=KT)
        kvt = ps[:, KVB:KVB + 2, :].rearrange("p b (q c) -> p (b q) c", c=P)

        def diagonal(t, a):
            return t[64 * a:64 * a + 64, :, LD * a:LD * a + LD]

        def dve_stats(dve, n):
            ln_steps.start(n)
            dve.wait_ge(x_loaded, 16 * (n + 1))
            for j in range(NJ):
                last = nc.vector.bn_stats(st[:, j, :], xn[:, j, :])
            ln_steps.link(dve, last)
            nc.vector.memset(pad[:], 0.0)
            for j in range(NJ):
                last = nc.vector.bn_aggr(mv[:, j, :], st[:, j, :])
            ln_steps.link(dve, last)
            nc.vector.tensor_scalar(vin[:], mv[:, :, 1:2].rearrange("p j o -> p (j o)"), LN_EPS, None,
                                    ALU.add).then_inc(stats_ready, 1)
            ln_steps.end()

        def dve_xn(dve, n):
            dve.wait_ge(roots_ready, n + 1)
            for j in range(NJ):
                nc.vector.tensor_scalar(xn[:, j, :], xn[:, j, :], mv[:, j, 0:1], inv[:, j:j + 1],
                                        ALU.subtract, ALU.mult).then_inc(xn_ready, 1)

        def dve_r1(dve, n):
            dve.wait_ge(xn_ready, NJ * (n + 1))
            dve.wait_ge(y2_loaded, 16 * (n + 1))
            nc.vector.tensor_tensor(r1[:], r1[:], xn[:], ALU.add).then_inc(r1_ready, 1)

        def dve_turn(dve, n):
            for kt in range(KT):
                dve.wait_ge(t_hi, KT * n + kt + 1)
                nc.vector.tensor_tensor(xnT[1][:, kt, :], ps[:, RING + kt, :], xnT[0][:, kt, :].bitcast(F32),
                                        ALU.subtract).then_inc(ring_evac_dve, 1)

        def dve_z(dve, e, i):
            dve.wait_ge(y_psum, NJ * e + 2 * i + 2)
            dve.wait_ge(xb_ready, e + 1)
            nc.vector.tensor_tensor(xb[:, 2 * i:2 * i + 2, :], ps[:, YB, :].rearrange("p (j d) -> p j d", j=2),
                                    xb[:, 2 * i:2 * i + 2, :], ALU.add).then_inc(y_evac, 1)

        def dve_scale(dve, e, p):
            dve.wait_ge(spread_psum, NP_ * e + p + 1)
            if p >= NQR:
                dve.wait_ge(qs_lo, NP_ * e + p - NQR + 1)
            nc.vector.tensor_tensor(qs[:, p % NQR, :], ps[:, DB + p % 2, :], qf[:, p, :], ALU.mult).then_inc(qs_ready, 1)

        SCALE_AFTER = ((), (), (), (0, 1, 2), (3,), (4, 5, 6), (7,), ())

        def dve_part(dve, b, n):
            if not first(b):
                dve.wait_ge(kv_psum, b)
            for j in range(NJ):
                if j == 1 and not first(b):
                    dve_rdt(dve, b - 1)
                if first(b) and j == 2:
                    dve.wait_ge(wo_split, 1)
                for h in range(2):
                    dve.wait_ge(ring_psum, NR * b + KT + 4 * j + h + 1)
                    nc.vector.tensor_scalar(kf[:, j, h * 512:(h + 1) * 512], ps[:, RING + h, :], 0.0, LIN_EPS,
                                            ALU.max, ALU.add).then_inc(ring_evac_dve, 1)
                    if not first(b):
                        for p in SCALE_AFTER[2 * j + h]:
                            dve_scale(dve, b - 1, p)
                    if h and j == 0 and not first(b):
                        dve_rd(dve, b - 1)
                if n is not None and j in (1, 3):
                    (dve_stats, dve_xn)[j // 2](dve, n)
            if not first(b):
                dve_z(dve, b - 1, 0)

            def query(p):
                if p == 0 and not first(b):
                    dve.wait_ge(qs_ready, NP_ * b)
                    dve.wait_ge(den_psum, b)
                dve.wait_ge(ring_psum, NR * b + KT + 16 + p + 1)
                nc.vector.tensor_scalar(qf[:, p, :], ps[:, RING + p % 2, :], 0.0, LIN_EPS,
                                        ALU.max, ALU.add).then_inc(ring_evac_dve, 1)

            def kw(i):
                dve.wait_ge(kw_hi, NKW * b + i + 1)
                nc.vector.tensor_tensor(KW[1][:, 2 * i:2 * i + 2, :], ps[:, DB + i % 2, :].rearrange("p (a d) -> p a d", a=2),
                                        KW[0][:, 2 * i:2 * i + 2, :].bitcast(F32), ALU.subtract).then_inc(kw_lo, 1)

            query(0)
            query(1)
            if not first(b):
                dve_z(dve, b - 1, 1)
            if n is not None:
                dve_r1(dve, n)
            dve.wait_ge(kv_evac, b + 1)
            for bank in range(3):
                m = min(3, NP_ - 3 * bank)
                sums = ps[:, KVB + bank, 0:m * PW].rearrange("p (q c) -> p q c", c=PW)[:, :, P:P + 1]
                last = nc.vector.tensor_tensor(kss[:, 3 * bank:3 * bank + m, :], hm[:, 3 * bank:3 * bank + m, :],
                                               sums.broadcast_to([P, m, CT]), ALU.mult)
            last.then_inc(kss_ready, 1)
            query(2)
            query(3)
            for a in range(2):
                dve.wait_ge(kv_hi, 2 * b + a + 1)
                nc.vector.tensor_tensor(diagonal(KV[1], a), diagonal(kvt, a), diagonal(KV[0], a).bitcast(F32),
                                        ALU.subtract).then_inc(kv_lo, 1)
            for p in range(4, NP_):
                query(p)
            for i in range(NKW):
                if i == 1 and n is not None:
                    dve_turn(dve, n)
                kw(i)

        def dve_rd(dve, e):
            dve.wait_ge(den_evac, e + 1)
            nc.vector.reciprocal(rd, rd).then_inc(rd_ready, 1)

        def dve_rdt(dve, e):
            dve.wait_ge(rd_hi, e + 1)
            nc.vector.scalar_tensor_tensor(out=rdT[:], in0=rh.bitcast(F32), scalar=lowm[:, 0:1], in1=rd,
                                           op0=ALU.mult, op1=ALU.add).then_inc(rdt_ready, 1)
        def dve_finish(dve, e):
            dve_rd(dve, e)
            dve_rdt(dve, e)
            for p in range(NP_):
                dve_scale(dve, e, p)
            for p in range(NP_ // 2, NP_):
                dve.wait_ge(qs_hi, NP_ * e + p + 1)
                nc.vector.tensor_tensor(QS[1][:, p, :], qs[:, p % NQR, :], QS[0][:, p, :].bitcast(F32),
                                        ALU.subtract).then_inc(qs_lo, 1)
            for i in range(2):
                dve_z(dve, e, i)

        def pool_norm(pool, n):
            pool.wait_ge(stats_ready, n + 1)
            nc.gpsimd.tensor_tensor(inv[:], vin[:], mhalf[:], ALU.pow).then_inc(roots_ready, 1)

        def pool_bias(pool, b):
            pool.wait_ge(xb_loaded, 16 * (b + 1))
            nc.gpsimd.tensor_tensor(xb[:], xb[:], bob[:].unsqueeze(1).broadcast_to([P, NJ, D]),
                                    ALU.add).then_inc(xb_ready, 1)

        def pool_load(pool, n):
            if not first(n):
                pool.wait_ge(r1_ready, n)
                pool.wait_ge(ring_psum, NR * (n - 1) + KT)
            pool.dma_start(xn[:], x_v[n]).then_inc(x_loaded, 16)

        def pool_part(pool, b, n):
            if n is not None:
                pool_load(pool, n)
            if not first(b):
                pool_low(pool, b - 1, range(5))
            if n is not None:
                pool_norm(pool, n)
            if not first(b):
                pool_low(pool, b - 1, range(5, NP_))
            pool_bias(pool, b)

        def pool_low(pool, e, pairs):
            for p in pairs:
                pool.wait_ge(qs_hi, NP_ * e + p + 1)
                nc.gpsimd.tensor_tensor(QS[1][:, p, :], qs[:, p % NQR, :], QS[0][:, p, :].bitcast(F32),
                                        ALU.subtract).then_inc(qs_lo, 1)

        def sync_load(sp, n):
            if not first(n):
                sp.wait_ge(r1_stored, 16 * n)
            sp.dma_start(r1[:], y2_v[n]).then_inc(y2_loaded, 16)

        def sync_part(sp, b, n):
            sp.wait_ge(r1_ready, b + 1)
            sp.dma_start(r1_v[b], r1[:]).then_inc(r1_stored, 16)
            if n is not None:
                sync_load(sp, n)
            if not first(b):
                sync_z(sp, b - 1)
                sp.wait_ge(z_stored, 16 * b)
            sp.dma_start(xb[:], x_v[b]).then_inc(xb_loaded, 16)

        def sync_z(sp, e):
            sp.wait_ge(y_evac, 2 * (e + 1))
            sp.dma_start(z_v[e], xb[:]).then_inc(z_stored, 16)

        def program(eng, part):
            part(eng, 0, 1)
            with eng.Fori(1, B - 1) as b:
                part(eng, b, b + 1)
            part(eng, B - 1, None)

        block = ctx.enter_context(nc.Block())

        @block.sync
        def _(sp):
            sp.dma_start(kf[:, 0:2, :], wk.rearrange("(k p) n -> p k n", p=P)).then_inc(wk_loaded, 16)
            sp.dma_start(va_k, wv.rearrange("(k p) n -> p k n", p=P)).then_inc(wv_loaded, 16)
            sp.dma_start(wo_raw, wo.rearrange("(k p) n -> p k n", p=P)).then_inc(wo_loaded, 16)
            sp.dma_start(qf[:, 4:7, :].rearrange("p a n -> p (a n)")[:, 0:NP_ * P + 1], sel_d).then_inc(sel_loaded, 16)
            sp.wait_ge(y2_stored, 16 * B)
            sync_load(sp, 0)
            sp.dma_start(bob[:], bo.rearrange("(a d) -> a d", a=1).broadcast_to([P, D])).then_inc(bob_loaded, 16)
            program(sp, sync_part)
            sync_z(sp, B - 1)

        @block.tensor
        def _(pe):
            for i in range(2):
                if i:
                    pe.wait_ge(wk_loaded, 16)
                else:
                    pe.wait_ge(ahead_loaded, 16 * 3)
                for p in range(NP_):
                    for kt in range(KT):
                        c = p * D + kt * P
                        last = nc.tensor.transpose(ps[:, c // 512, c % 512:c % 512 + P],
                                                   (wq_raw, kf)[i][:, kt, p * P:(p + 1) * P], ident[:])
                last.then_inc(turned, 1)
                pe.wait_ge(turned_copied, 2 * (i + 1))
                if i:
                    pe.wait_ge(lo_made, 1)
                for kt in range(KT):
                    for p in range(NP_):
                        c = p * P
                        last = nc.tensor.matmul(ps[:, 4 + 2 * kt + c // 512, c % 512:c % 512 + P],
                                                qf[:, p // 2, (p % 2) * D + kt * P:(p % 2) * D + (kt + 1) * P], pblk[:],
                                                start=True, stop=True)
                last.then_inc(folded, 1)
            pe_turn(pe, 0)
            pe.wait_ge(lo_made, 2)
            pe.wait_ge(ones_ready, 1)
            pe.wait_ge(zeros_ready, 2)
            program(pe, pe_part)
            pe_finish(pe, B - 1)

        @block.scalar
        def _(act):
            for i, w in enumerate((WQ, WK)):
                act.wait_ge(turned, i + 1)
                if i:
                    act.wait_ge(folded, 1)
                nc.scalar.copy(qf[:, 0:2, :], ps[:, 0:2, :]).then_inc(turned_copied, 1)
                if i:
                    act.wait_ge(wv_loaded, 16)
                    nc.scalar.copy(WV[0][:], va_k).then_inc(wv_hi_made, 1)
                act.wait_ge(folded, i + 1)
                for kt in range(KT):
                    nc.scalar.copy(w[0][:, kt, :].rearrange("p (b n) -> p b n", b=2),
                                   ps[:, 4 + 2 * kt:6 + 2 * kt, :]).then_inc(hi_made, 1)
            act_turn(act, 0)
            act.wait_ge(wo_loaded, 16)
            nc.scalar.copy(WO[0][:], wo_raw).then_inc(wo_hi_made, 1)
            act.wait_ge(lo_made, 2)
            act.wait_ge(pool_lo_made, 1)
            act.wait_ge(zeros_ready, 2)
            program(act, act_part)
            act_finish(act, B - 1)

        @block.gpsimd
        def _(pool):
            nc.gpsimd.memset(mhalf[:], -0.5).then_inc(mhalf_ready, 1)
            pool.wait_ge(mhalf_ready, 1)
            pool_load(pool, 0)
            pool_norm(pool, 0)
            pool.wait_ge(wv_hi_made, 1)
            nc.gpsimd.tensor_tensor(WV[1][:], va_k, WV[0][:].bitcast(F32), ALU.subtract).then_inc(pool_lo_made, 1)
            pool.wait_ge(pool_lo_made, 1)
            nc.gpsimd.memset(va[:, :, :, P:PW].rearrange("p j q c -> p (j q) c"), 1.0).then_inc(ones_ready, 1)
            pool.wait_ge(wo_hi_made, 1)
            nc.gpsimd.tensor_tensor(WO[1][:], wo_raw, WO[0][:].bitcast(F32), ALU.subtract).then_inc(wo_split, 1)
            pool.wait_ge(bob_loaded, 16)
            program(pool, pool_part)
            pool_low(pool, B - 1, range(NP_ // 2))

        @block.vector
        def _(dve):
            def turned_copy(i):
                dve.wait_ge(turned, i + 1)
                if i:
                    dve.wait_ge(folded, 1)
                nc.vector.tensor_copy(qf[:, 2:4, :], ps[:, 2:4, :]).then_inc(turned_copied, 1)

            def split(i):
                w = (WQ, WK)[i]
                for kt in range(KT):
                    dve.wait_ge(hi_made, KT * i + kt + 1)
                    last = nc.vector.tensor_tensor(w[1][:, kt, :].rearrange("p (b n) -> p b n", b=2),
                                                   ps[:, 4 + 2 * kt:6 + 2 * kt, :],
                                                   w[0][:, kt, :].rearrange("p (b n) -> p b n", b=2).bitcast(F32),
                                                   ALU.subtract)
                last.then_inc(lo_made, 1)

            turned_copy(0)
            nc.vector.memset(epsb[:], LIN_EPS)
            nc.vector.memset(hm[:], 0.0).then_inc(zeros_ready, 1)
            dve.wait_ge(zeros_ready, 1)
            for i in range(2):
                for c in range(0, P, CT):
                    last = nc.vector.tensor_copy(KV[i][:, :, c:c + CT], hm[:])
            last.then_inc(zeros_ready, 1)
            dve.wait_ge(zeros_ready, 2)
            for g in range(2):
                for a in range(2):
                    r = 2 * g + a
                    nc.vector.memset(hm[64 * a:64 * a + 64, 4 * g:4 * g + 4, r:r + CT // 2 + 1:CT // 2], 1.0)
            turned_copy(1)
            split(0)
            dve_stats(dve, 0)
            dve_xn(dve, 0)
            split(1)
            dve_turn(dve, 0)
            dve_r1(dve, 0)
            dve.wait_ge(sel_loaded, 16)
            nc.vector.tensor_copy(lowm[:], qf[:, 6, 0:1])
            nc.vector.tensor_copy(SEL[:].rearrange("p q c -> p (q c)"), qf[:, 4:6, :].rearrange("p a n -> p (a n)")
                                  ).then_inc(sel_made, 1)
            dve.wait_ge(sel_made, 1)
            program(dve, dve_part)
            dve_finish(dve, B - 1)


def experts(nc, g2, gate, w1, w2, w3, ident, z_d, r1_d, out, room, z_stored, r1_stored):
    def tiles(ap):
        return ap.rearrange("b (j p) d -> b p j d", p=P)

    z_v, r1_v, out_v = map(tiles, (z_d, r1_d, out))

    with ExitStack() as ctx:
        def sb(name, shape, dt=F32):
            return ctx.enter_context(nc.sbuf_tensor(name, shape, dt))

        def sem(name):
            return ctx.enter_context(nc.semaphore(name))

        g2c = sb("g2c", [P, KT])
        mhalf = sb("mhalf3", [P, NJ])
        graw = sb("graw", [P, KT, NE])
        W1, W3 = ([sb(f"{n}{i}", [P, NE, KT, HID], F32R) for i in range(2)] for n in ("W1_", "W3_"))
        W2 = [sb(f"W2_{i}", [P, NE, NM, D], F32R) for i in range(2)]
        G = [sb(f"G{i}", [P, KT, NE], F32R) for i in range(2)]

        WC, NST = KT * HID, 3
        staged = sb("staged", [P, NST, WC])
        r1, xf, acc = (sb(name, [P, NJ, D])[:] for name in ("r1_3", "xf", "acc"))
        sl, h32 = room[:, 0:2, :], room[:, 2:4, :]
        st = sb("st3", [P, NJ, 6])
        pad = sb("pad3", [P, 1])
        mv = sb("mv3", [P, NJ, 2])
        ms = sb("ms", [P, NJ])
        inv = sb("inv3", [P, NJ])
        xfT = [sb(f"xfT{i}", [P, KT, S], F32R) for i in range(2)]
        NHR = 3
        hT = [sb(f"hT{i}", [P, NHR, S], F32R) for i in range(2)]
        lg = sb("lg", [P, NJ, NE])
        lmax = sb("lmax", [P, NJ])
        le = sb("le", [P, NJ, NE])
        lsum = sb("lsum", [P, NJ])
        pr = sb("pr", [P, NJ, NE])
        over = sb("over", [P, NJ, NE, NE])
        rank = sb("rank", [P, NJ, NE])
        comb = sb("comb", [P, NJ, NE])

        ps = ctx.enter_context(nc.psum_tensor("ps3", [P, 8, 512], F32))
        YB = 4

        consts_loaded = sem("consts3_loaded")
        w_loaded = [sem(f"w3_loaded{i}") for i in range(NST)]
        hi_steps = Steps(sem("w3_hi"), 3 * NE)
        w_split = sem("w3_split")
        gate_steps0 = Steps(sem("gate_prep"), 2)
        zeros_ready = sem("zeros3_ready")
        r1_loaded = sem("r1_loaded")
        z_loaded = sem("z_loaded")
        n_steps = Steps(sem("norm3_step"), 3)
        ms_ready = sem("ms_ready")
        roots_ready = sem("roots3_ready")
        xf_ready = sem("xf_ready")
        acc_ready = sem("acc_ready")
        xt_psum = sem("xt_psum")
        xt_hi = sem("xt_hi")
        xt_lo = sem("xt_lo")
        gate_psum = sem("gate_psum")
        gate_steps = Steps(sem("gate_step"), 9)
        lg_ready = sem("lg_ready")
        lmax_ready = sem("lmax_ready")
        le_ready = sem("le_ready")
        ab_psum = sem("ab_psum")
        silu_done = sem("silu_done")
        h_ready = sem("h_ready")
        h_hi = sem("h_hi")
        h_lo = sem("h_lo")
        y_used = sem("y3_used")
        y_evac = sem("y3_evac")
        out_stored = sem("out_stored")

        NH_ = NE * NM


        def pe_turn(pe, n):
            if not first(n):
                pe.wait_ge(h_ready, NH_ * n)
            pe.wait_ge(xf_ready, NJ * (n + 1))
            for kt in range(KT):
                for j in range(NJ):
                    last = nc.tensor.transpose(ps[:, kt, j * P:(j + 1) * P], xf[:, j, kt * P:(kt + 1) * P], ident[:])
                last.then_inc(xt_psum, 1)

        def pe_gate(pe, n):
            pe.wait_ge(xt_lo, KT * (n + 1))
            for j in range(NJ):
                for kt in range(KT):
                    l = [xfT[i][:, kt, j * P:(j + 1) * P] for i in range(2)]
                    last = mm3(nc, ps[:, 2, j * NE:(j + 1) * NE], *l, G[0][:, kt, :], G[1][:, kt, :],
                               kt == 0, kt == KT - 1)
            last.then_inc(gate_psum, 1)

        def pe_part(pe, b, n):
            def hidden(i):
                e, m = divmod(i, NM)
                if first(b) and m == 0:
                    pe.wait_ge(w_split, 3 * e + 2)
                if i == 0:
                    pass
                elif i == 1:
                    pe.wait_ge(lg_ready, b + 1)
                else:
                    pe.wait_ge(h_ready, NH_ * b + i - 1)
                for w, bank in ((W1, 2 * (i % 2)), (W3, 2 * (i % 2) + 1)):
                    for kt in range(KT):
                        l = [w[h][:, e, kt, m * P:(m + 1) * P] for h in range(2)]
                        last = mm3(nc, ps[:, bank, :], *l, xfT[0][:, kt, :], xfT[1][:, kt, :], kt == 0, kt == KT - 1)
                last.then_inc(ab_psum, 1)

            def down(i):
                e, m = divmod(i, NM)
                pe.wait_ge(h_lo, NH_ * b + i + 1)
                if first(b) and m == 0:
                    pe.wait_ge(w_split, 3 * (e + 1))
                if m == 0 and not (first(b) and e == 0):
                    pe.wait_ge(y_evac, NE * b + e)
                for j in range(NJ):
                    l = [hT[h][:, i % NHR, j * P:(j + 1) * P] for h in range(2)]
                    last = mm3(nc, ps[:, YB + j, 0:D], *l, W2[0][:, e, m, :], W2[1][:, e, m, :], m == 0, m == NM - 1)
                last.then_inc(y_used, 1)

            for i in range(NH_):
                hidden(i)
                if i >= 2:
                    down(i - 2)
            if n is not None:
                pe_turn(pe, n)
            down(NH_ - 2)
            down(NH_ - 1)
            if n is not None:
                pe_gate(pe, n)

        def act_turn(act, n):
            for kt in range(KT):
                act.wait_ge(xt_psum, KT * n + kt + 1)
                nc.scalar.copy(xfT[0][:, kt, :], ps[:, kt, :]).then_inc(xt_hi, 1)

        def act_gate(act, n):
            act.wait_ge(lmax_ready, n + 1)
            nc.scalar.activation(le[:], lg[:], ACT.Exp).then_inc(le_ready, 1)

        def act_part(act, b, n):
            for i in range(NH_ + 1):
                if i < NH_:
                    act.wait_ge(ab_psum, NH_ * b + i + 1)
                    if i >= 2:
                        act.wait_ge(h_ready, NH_ * b + i - 1)
                    elif not first(b):
                        act.wait_ge(h_ready, NH_ * b)
                    nc.scalar.activation(sl[:, i % 2, :], ps[:, 2 * (i % 2), :], ACT.Silu).then_inc(silu_done, 1)
                if i:
                    k = i - 1
                    act.wait_ge(h_ready, NH_ * b + k + 1)
                    if k >= NHR:
                        act.wait_ge(y_used, NH_ * b + k - NHR + 1)
                    elif not first(b):
                        act.wait_ge(y_used, NH_ * b - NHR + k + 1)
                    nc.scalar.copy(hT[0][:, k % NHR, :], h32[:, k % 2, :]).then_inc(h_hi, 1)
                if i == GATE_AT[1]:
                    act_gate(act, b)
            if n is not None:
                act_turn(act, n)

        def dve_norm(dve, n):
            n_steps.start(n)
            dve.wait_ge(r1_loaded, 16 * (n + 1))
            for j in range(NJ):
                last = nc.vector.bn_stats(st[:, j, :], r1[:, j, :])
            n_steps.link(dve, last)
            nc.vector.memset(pad[:], 0.0)
            for j in range(NJ):
                last = nc.vector.bn_aggr(mv[:, j, :], st[:, j, :])
            n_steps.link(dve, last)
            mean, var = (mv[:, :, i:i + 1].rearrange("p j o -> p (j o)") for i in range(2))
            n_steps.link(dve, nc.vector.tensor_tensor(ms[:], mean, mean, ALU.mult))
            nc.vector.scalar_tensor_tensor(out=ms[:], in0=ms[:], scalar=RMS_EPS, in1=var,
                                           op0=ALU.add, op1=ALU.add).then_inc(ms_ready, 1)
            n_steps.end()
            dve.wait_ge(roots_ready, n + 1)
            if not first(n):
                dve.wait_ge(xt_psum, KT * n)
            for j in range(NJ):
                nc.vector.tensor_scalar(xf[:, j, :], r1[:, j, :], inv[:, j:j + 1], None, ALU.mult).then_inc(xf_ready, 1)

        def dve_turn(dve, n):
            for kt in range(KT):
                dve.wait_ge(xt_hi, KT * n + kt + 1)
                nc.vector.tensor_tensor(xfT[1][:, kt, :], ps[:, kt, :], xfT[0][:, kt, :].bitcast(F32),
                                        ALU.subtract).then_inc(xt_lo, 1)

        GATE_AT = (0, 2, 3)

        def dve_logits(dve, n):
            dve.wait_ge(gate_psum, n + 1)
            nc.vector.tensor_copy(lg[:], ps[:, 2, 0:NJ * NE].rearrange("p (j e) -> p j e", e=NE)).then_inc(lg_ready, 1)

        def wide(ap):
            return ap.unsqueeze(2).broadcast_to([P, NJ, NE])

        def dve_shift(dve, n):
            s = gate_steps
            s.start(n)
            dve.wait_ge(lg_ready, n + 1)
            s.link(dve, nc.vector.tensor_reduce(lmax[:], lg[:], AX, ALU.max))
            nc.vector.tensor_tensor(lg[:], lg[:], wide(lmax[:]), ALU.subtract).then_inc(lmax_ready, 1)

        def dve_gate(dve, n):
            s = gate_steps
            dve.wait_ge(le_ready, n + 1)
            s.link(dve, nc.vector.reduce_sum(lsum[:], le[:], AX))
            s.link(dve, nc.vector.reciprocal(lsum[:], lsum[:]))
            s.link(dve, nc.vector.tensor_tensor(pr[:], le[:], wide(lsum[:]), ALU.mult))
            for r in range(NE):
                if r:
                    last = nc.vector.tensor_tensor(over[:, :, 0:r, r], pr[:, :, r:r + 1].broadcast_to([P, NJ, r]),
                                                   pr[:, :, 0:r], ALU.is_gt)
                if r < NE - 1:
                    k = NE - 1 - r
                    last = nc.vector.tensor_tensor(over[:, :, r + 1:NE, r], pr[:, :, r:r + 1].broadcast_to([P, NJ, k]),
                                                   pr[:, :, r + 1:NE], ALU.is_ge)
            s.link(dve, last)
            s.link(dve, nc.vector.reduce_sum(rank[:], over[:], AX))
            s.link(dve, nc.vector.scalar_tensor_tensor(out=comb[:], in0=rank[:], scalar=1.5, in1=pr[:],
                                                       op0=ALU.is_lt, op1=ALU.mult))
            s.link(dve, nc.vector.reduce_sum(lsum[:], comb[:], AX))
            s.link(dve, nc.vector.reciprocal(lsum[:], lsum[:]))
            nc.vector.tensor_tensor(comb[:], comb[:], wide(lsum[:]), ALU.mult).then_inc(comb_ready, 1)
            s.end()

        comb_ready = sem("comb_ready")

        def dve_part(dve, b, n):
            def weigh(e):
                if e == 0:
                    dve.wait_ge(comb_ready, b + 1)
                    dve.wait_ge(acc_ready, b + 1)
                else:
                    dve.wait_ge(y_evac, NE * b + e)
                dve.wait_ge(y_used, NH_ * b + NM * (e + 1))
                for j in range(NJ):
                    last = nc.vector.scalar_tensor_tensor(out=acc[:, j, :], in0=ps[:, YB + j, 0:D], scalar=comb[:, j, e:e + 1],
                                                          in1=acc[:, j, :], op0=ALU.mult, op1=ALU.add)
                last.then_inc(y_evac, 1)

            for i in range(NH_):
                dve.wait_ge(silu_done, NH_ * b + i + 1)
                if i >= 2:
                    dve.wait_ge(h_lo, NH_ * b + i - 1)
                elif not first(b):
                    dve.wait_ge(h_lo, NH_ * b - 1 + i)
                nc.vector.tensor_tensor(h32[:, i % 2, :], sl[:, i % 2, :], ps[:, 2 * (i % 2) + 1, :],
                                        ALU.mult).then_inc(h_ready, 1)
                if i == GATE_AT[0]:
                    dve_shift(dve, b)
                if i == GATE_AT[2]:
                    dve_gate(dve, b)
                if i % NM == 1 and i > NM:
                    weigh(i // NM - 1)
                if first(b) and i % 2 == 0 and i < NH_ - NM:
                    dve_split(dve, 3 + i // 2)
                if i == 12 and n is not None:
                    dve_norm(dve, n)
            if n is not None:
                dve_turn(dve, n)
            weigh(NE - 1)
            if n is not None:
                dve_logits(dve, n)

        def pool_norm(pool, n):
            pool.wait_ge(ms_ready, n + 1)
            nc.gpsimd.tensor_tensor(inv[:], ms[:], mhalf[:], ALU.pow).then_inc(roots_ready, 1)

        def pool_part(pool, b, n):
            for i in range(NH_):
                pool.wait_ge(h_hi, NH_ * b + i + 1)
                nc.gpsimd.tensor_tensor(hT[1][:, i % NHR, :], h32[:, i % 2, :], hT[0][:, i % NHR, :].bitcast(F32),
                                        ALU.subtract).then_inc(h_lo, 1)
                if i == 3:
                    pool_acc(pool, b)
                    if n is not None:
                        pool_load(pool, n)
                if i == 11 and n is not None:
                    pool_norm(pool, n)

        def pool_acc(pool, n):
            pool.wait_ge(z_loaded, 16 * (n + 1))
            pool.wait_ge(r1_loaded, 16 * (n + 1))
            nc.gpsimd.tensor_tensor(acc, acc, r1, ALU.add).then_inc(acc_ready, 1)

        def pool_load(pool, n):
            if first(n):
                pool.wait_ge(r1_stored, 16 * B)
            else:
                pool.wait_ge(acc_ready, n)
                pool.wait_ge(xf_ready, NJ * n)
            pool.dma_start(r1, r1_v[n]).then_inc(r1_loaded, 16)

        def sync_part(sp, b, n):
            sp.wait_ge(y_evac, NE * (b + 1))
            sp.dma_start(out_v[b], acc).then_inc(out_stored, 16)
            sp.wait_ge(out_stored, 16 * (b + 1))
            if n is not None:
                sp.dma_start(acc, z_v[n]).then_inc(z_loaded, 16)

        def program(eng, part):
            part(eng, 0, 1)
            with eng.Fori(1, B - 1) as b:
                part(eng, b, b + 1)
            part(eng, B - 1, None)

        CH = [(e, k) for e in range(NE) for k in range(3)]

        def sync_weights(sp, chunks):
            for i in chunks:
                e, k = CH[i]
                if i >= NST:
                    sp.wait_ge(w_split, i - NST + 1)
                w = (w1, w3, w2)[k]
                sp.dma_start(staged[:, i % NST, :].rearrange("p (k n) -> p k n", n=D if k == 2 else HID),
                             w[e].rearrange("(k p) n -> p k n", p=P)).then_inc(w_loaded[i % NST], 16)

        def dve_split(dve, i):
            e, k = CH[i]
            dve.wait_ge(w_loaded[i % NST], 16 * (i // NST + 1))
            if k < 2:
                w = (W1, W3)[k]
                src = staged[:, i % NST, :].rearrange("p (k n) -> p k n", n=HID)
                for kt in range(KT):
                    last = nc.vector.tensor_scalar(w[0][:, e, kt, :], src[:, kt, :], g2c[:, kt:kt + 1], None, ALU.mult)
                hi_steps.link(dve, last)
                for kt in range(KT):
                    last = nc.vector.scalar_tensor_tensor(out=w[1][:, e, kt, :], in0=src[:, kt, :],
                                                          scalar=g2c[:, kt:kt + 1], in1=w[0][:, e, kt, :].bitcast(F32),
                                                          op0=ALU.mult, op1=ALU.subtract)
            else:
                src = staged[:, i % NST, :].rearrange("p (k n) -> p k n", n=D)
                hi_steps.link(dve, nc.vector.tensor_copy(W2[0][:, e, :, :], src))
                last = nc.vector.tensor_tensor(W2[1][:, e, :, :], src, W2[0][:, e, :, :].bitcast(F32), ALU.subtract)
            last.then_inc(w_split, 1)

        block = ctx.enter_context(nc.Block())

        @block.sync
        def _(sp):
            sp.dma_start(g2c[:], g2.rearrange("(k p) -> p k", p=P), allow_slow_non_contiguous=True).then_inc(consts_loaded, 16)
            sp.dma_start(graw[:], gate.rearrange("(k p) e -> p k e", p=P)).then_inc(consts_loaded, 16)
            sync_weights(sp, range(3))
            sp.wait_ge(z_stored, 16 * B)
            sp.dma_start(acc, z_v[0]).then_inc(z_loaded, 16)
            sync_weights(sp, range(3, len(CH)))
            program(sp, sync_part)

        @block.tensor
        def _(pe):
            pe.wait_ge(consts_loaded, 16 * 2)
            pe_turn(pe, 0)
            pe_gate(pe, 0)
            program(pe, pe_part)

        @block.scalar
        def _(act):
            act_turn(act, 0)
            program(act, act_part)

        @block.gpsimd
        def _(pool):
            nc.gpsimd.memset(mhalf[:], -0.5).then_inc(zeros_ready, 1)
            pool.wait_ge(zeros_ready, 1)
            pool_load(pool, 0)
            pool_norm(pool, 0)
            program(pool, pool_part)

        @block.vector
        def _(dve):
            nc.vector.memset(over[:], 0.0)
            dve.wait_ge(consts_loaded, 16 * 2)
            for kt in range(KT):
                last = nc.vector.tensor_scalar(G[0][:, kt, :], graw[:, kt, :], g2c[:, kt:kt + 1], None, ALU.mult)
            gate_steps0.link(dve, last)
            for kt in range(KT):
                last = nc.vector.scalar_tensor_tensor(out=G[1][:, kt, :], in0=graw[:, kt, :], scalar=g2c[:, kt:kt + 1],
                                                      in1=G[0][:, kt, :].bitcast(F32), op0=ALU.mult, op1=ALU.subtract)
            gate_steps0.link(dve, last)
            dve_norm(dve, 0)
            dve_turn(dve, 0)
            dve_split(dve, 0)
            dve_split(dve, 1)
            dve_logits(dve, 0)
            dve_split(dve, 2)
            program(dve, dve_part)


_INS = ['L0_attn_x', 'L0_attn_Wq', 'L0_attn_Wk', 'L0_attn_Wv', 'L0_attn_proj', 'L0_attn_Wo', 'L0_attn_bo',
        'L0_ffn_g1', 'L0_ffn_g2', 'L0_ffn_wq', 'L0_ffn_wk', 'L0_ffn_wv', 'L0_ffn_wo', 'L0_ffn_gate',
        'L0_ffn_w1', 'L0_ffn_w2', 'L0_ffn_w3']


def build(nc, t, out):
    qk_d = [nc.dram_tensor(f"qk_scratch{i}", (2, 3 * P, S), F32).ap() for i in range(2)]
    y2_d = nc.dram_tensor("y2_scratch", (B, S, D), F32).ap()
    z_d = nc.dram_tensor("z_scratch", (B, S, D), F32).ap()
    r1_d = nc.dram_tensor("r1_scratch", (B, S, D), F32).ap()
    with ExitStack() as ctx:
        ident, pblk, qs = (ctx.enter_context(nc.sbuf_tensor(name, shape, F32))
                           for name, shape in (("ident", [P, P]), ("pblk", [P, P]), ("qs", [P, 4, S])))
        pblk_zero, ahead_loaded, y2_stored, z_stored, r1_stored = (
            ctx.enter_context(nc.semaphore(name)) for name in ("pblk_zero", "ahead_loaded", "y2_stored", "z_stored", "r1_stored"))

        def load_ahead(sp):
            sp.dma_start(qs[:].rearrange("p a n -> p (a n)").rearrange("p (k n) -> p k n", k=KT),
                         t['L0_attn_Wq'].rearrange("(k p) n -> p k n", p=P)).then_inc(ahead_loaded, 16)
            sp.wait_ge(pblk_zero, 1)
            for a in range(2):
                sp.dma_start(pblk[64 * a:64 * a + 64, 64 * a:64 * a + 64], t['L0_attn_proj']).then_inc(ahead_loaded, 16)

        def zero_ahead():
            nc.vector.memset(pblk[:], 0.0).then_inc(pblk_zero, 1)

        softmax_attention(nc, t['L0_attn_x'], t['L0_ffn_g1'], t['L0_ffn_wq'], t['L0_ffn_wk'], t['L0_ffn_wv'],
                          t['L0_ffn_wo'], t['ident'], t['mask'], t['cos'], t['sin'], qk_d, y2_d,
                          y2_stored, ident, load_ahead, zero_ahead)
        linear_attention(nc, t['L0_attn_x'], t['L0_attn_Wk'], t['L0_attn_Wv'], t['L0_attn_Wo'], t['L0_attn_bo'],
                         t['sel'], y2_d, z_d, r1_d, ident, pblk, qs, ahead_loaded,
                         y2_stored, z_stored, r1_stored)
        experts(nc, t['L0_ffn_g2'], t['L0_ffn_gate'], t['L0_ffn_w1'], t['L0_ffn_w2'], t['L0_ffn_w3'], ident, z_d,
                r1_d, out, qs, z_stored, r1_stored)


def constants():
    import numpy as np
    q, k = np.arange(P)[:, None], np.arange(P)[None, :]
    sel = np.zeros((P, NP_ * P + 1), dtype=np.float32)
    for p in range(NP_):
        for a in range(2):
            r, c = CT * (p % 4) + 2 * (p // 4) + a, p * P + a * LD
            sel[[r, r + CT // 2], c:c + LD] = 1.0
    sel[np.arange(P) % CT >= CT // 2, NP_ * P] = -1.0
    inv_freq = (np.float32(1.0) / np.float32(10000.0) ** (np.arange(0, HD, 2, dtype=np.float32) / np.float32(HD)))
    angle = (np.arange(S, dtype=np.float32)[:, None] * inv_freq.astype(np.float32)[None, :]).astype(np.float32)
    angle = np.tile(np.concatenate([angle, angle], axis=-1).T, (P // HD, 1))
    return {
        'ident': np.eye(P, dtype=np.float32),
        'sel': sel,
        'mask': np.where(k > q, np.float32(-1e30), np.float32(0.0)).astype(np.float32),
        'cos': np.ascontiguousarray(np.cos(angle), dtype=np.float32),
        'sin': np.ascontiguousarray(np.sin(angle), dtype=np.float32),
    }


def kernel(**inputs):
    import numpy as np
    import concourse.bacc as bacc
    from concourse.bass_utils import run_bass_kernel_spmd

    nc = bacc.Bacc("TRN2", target_bir_lowering=False, num_devices=1)
    arrays = {f"in_{n}": np.ascontiguousarray(inputs[n]) for n in _INS}
    arrays |= {f"in_{n}": a for n, a in constants().items()}
    t = {n[3:]: nc.dram_tensor(n, a.shape, mybir.dt.from_np(a.dtype), kind="ExternalInput").ap()
         for n, a in arrays.items()}
    out = nc.dram_tensor("out", (B, S, D), F32, kind="ExternalOutput").ap()
    build(nc, t, out)
    r = run_bass_kernel_spmd(nc, [arrays], core_ids=[0])
    return r.results[0]["out"]
```
